# Optimizing a Trainium2 kernel written in Bass

```python
import numpy as np
import jax
import jax.numpy as jnp

def _softmax(x, axis=-1):
    return jax.nn.softmax(x, axis=axis)

def _gelu(x):
    return jax.nn.gelu(x, approximate=True)

def _silu(x):
    return jax.nn.silu(x)

def _sigmoid(x):
    return jax.nn.sigmoid(x)

def _layernorm(x, axis=-1, eps=1e-05):
    m = jnp.mean(x, axis=axis, keepdims=True)
    v = jnp.var(x, axis=axis, keepdims=True)
    return (x - m) / jnp.sqrt(v + eps)

def _scatter_add(tgt, idx, src, axis=0):
    return tgt.at[idx].add(src)

def _segment_sum(src, seg, n):
    return jax.ops.segment_sum(src, seg, n)
kernel_name = 'mk_macaron_d2_jaxref_r8_18b18e'

def setup_inputs(seed: int=0):
    np.random.seed(seed)
    _w = jnp.asarray

    def _L0_attn_setup():
        import jax, jax.numpy as jnp
        import numpy as np
        EMBED = 128
        WIN = 128
        NUM_HEADS = 16
        HQ = 16
        HKV = 4
        HEAD_DIM = EMBED // NUM_HEADS
        G = HQ // HKV
        key = jax.random.key(seed)
        k = jax.random.split(key, 5)
        B, S = (1, 256)
        x = jax.random.normal(k[0], (B, S, EMBED), dtype=jnp.float32)
        Wq = jax.random.normal(k[1], (HQ * HEAD_DIM, EMBED), dtype=jnp.float32) * 0.02
        Wk = jax.random.normal(k[2], (HKV * HEAD_DIM, EMBED), dtype=jnp.float32) * 0.02
        Wv = jax.random.normal(k[3], (HKV * HEAD_DIM, EMBED), dtype=jnp.float32) * 0.02
        Wo = jax.random.normal(k[4], (EMBED, HQ * HEAD_DIM), dtype=jnp.float32) * 0.02
        return {'x': x, 'Wq': Wq, 'Wk': Wk, 'Wv': Wv, 'Wo': Wo}
    _L0_attn_in = _L0_attn_setup()

    def _L0_ffn_setup():
        import jax, jax.numpy as jnp
        import numpy as np
        N_EMBD = 128
        N_EXPERTS = 8
        TOP_K = 2
        CAPACITY_FACTOR = 1.25
        key = jax.random.key(seed)
        ks = jax.random.split(key, 8)
        B, T, C, E, H = (8, 256, N_EMBD, N_EXPERTS, 4 * N_EMBD)
        w = lambda k, shape: jax.random.normal(k, shape, jnp.float32) * 0.02
        return {'x': jax.random.normal(ks[0], (B, T, C), jnp.float32), 'rW1': w(ks[1], (C, H)), 'rb1': jnp.zeros((H,), jnp.float32), 'rW2': w(ks[2], (H, H)), 'rb2': jnp.zeros((H,), jnp.float32), 'rW3': w(ks[3], (H, E)), 'rb3': jnp.zeros((E,), jnp.float32), 'eW1': w(ks[4], (E, C, H)), 'eb1': jnp.zeros((E, H), jnp.float32), 'eW2': w(ks[5], (E, H, C)), 'eb2': jnp.zeros((E, C), jnp.float32)}
    _L0_ffn_in = _L0_ffn_setup()

    def _L1_attn_setup():
        import jax, jax.numpy as jnp
        import numpy as np
        DIM = 128
        HEADS = 16
        HEAD_DIM = DIM // HEADS
        COLLAPSE_THRESHOLD = 0.27
        SHARPNESS = 15.0
        LN_EPS = 1e-05
        NORM_EPS = 1e-12

        def _layernorm(x, gamma, beta):
            mu = jnp.mean(x, axis=-1, keepdims=True)
            var = jnp.mean(jnp.square(x - mu), axis=-1, keepdims=True)
            return (x - mu) * jax.lax.rsqrt(var + LN_EPS) * gamma + beta

        def _l2_normalize(x):
            n = jnp.sqrt(jnp.sum(jnp.square(x), axis=-1, keepdims=True))
            return x / jnp.maximum(n, NORM_EPS)
        key = jax.random.key(seed)
        ks = jax.random.split(key, 9)
        B, T = (2, 256)
        s = 1.0 / np.sqrt(DIM)
        sh = 1.0 / np.sqrt(HEAD_DIM)
        return {'x': jax.random.normal(ks[0], (B, T, DIM), dtype=jnp.float32), 'w_q': jax.random.normal(ks[1], (DIM, DIM), dtype=jnp.float32) * s, 'w_k': jax.random.normal(ks[2], (DIM, DIM), dtype=jnp.float32) * s, 'w_v': jax.random.normal(ks[3], (DIM, DIM), dtype=jnp.float32) * s, 'g_q': jax.random.normal(ks[4], (HEAD_DIM,), dtype=jnp.float32) * sh, 'g_k': jax.random.normal(ks[5], (HEAD_DIM,), dtype=jnp.float32) * sh, 'w_o': jax.random.normal(ks[6], (DIM, DIM), dtype=jnp.float32) * s, 'b_o': jnp.zeros((DIM,), dtype=jnp.float32), 'gamma': jnp.ones((DIM,), dtype=jnp.float32), 'beta': jnp.zeros((DIM,), dtype=jnp.float32)}
    _L1_attn_in = _L1_attn_setup()

    def _L1_ffn_setup():
        import jax, jax.numpy as jnp
        import numpy as np
        DIM = 128
        HIDDEN = 384
        SCALE = 1.0 / 127.0

        def _dequant(w_int, dtype):
            return w_int.astype(dtype) * jnp.asarray(SCALE, dtype)
        key = jax.random.key(seed)
        k_x, k_g, k_u, k_d = jax.random.split(key, 4)
        x = jax.random.normal(k_x, (4, 256, DIM), dtype=jnp.float32)
        w_gate = jax.random.randint(k_g, (HIDDEN, DIM), -127, 128, dtype=jnp.int32)
        w_up = jax.random.randint(k_u, (HIDDEN, DIM), -127, 128, dtype=jnp.int32)
        w_down = jax.random.randint(k_d, (DIM, HIDDEN), -127, 128, dtype=jnp.int32)
        return {'x': x, 'w_gate': w_gate, 'w_up': w_up, 'w_down': w_down}
    _L1_ffn_in = _L1_ffn_setup()
    _d = {'L0_attn_x': _L0_attn_in['x'], 'L0_attn_Wq': _L0_attn_in['Wq'], 'L0_attn_Wk': _L0_attn_in['Wk'], 'L0_attn_Wv': _L0_attn_in['Wv'], 'L0_attn_Wo': _L0_attn_in['Wo'], 'L0_ffn_rW1': _L0_ffn_in['rW1'], 'L0_ffn_rb1': _L0_ffn_in['rb1'], 'L0_ffn_rW2': _L0_ffn_in['rW2'], 'L0_ffn_rb2': _L0_ffn_in['rb2'], 'L0_ffn_rW3': _L0_ffn_in['rW3'], 'L0_ffn_rb3': _L0_ffn_in['rb3'], 'L0_ffn_eW1': _L0_ffn_in['eW1'], 'L0_ffn_eb1': _L0_ffn_in['eb1'], 'L0_ffn_eW2': _L0_ffn_in['eW2'], 'L0_ffn_eb2': _L0_ffn_in['eb2'], 'L1_attn_w_q': _L1_attn_in['w_q'], 'L1_attn_w_k': _L1_attn_in['w_k'], 'L1_attn_w_v': _L1_attn_in['w_v'], 'L1_attn_g_q': _L1_attn_in['g_q'], 'L1_attn_g_k': _L1_attn_in['g_k'], 'L1_attn_w_o': _L1_attn_in['w_o'], 'L1_attn_b_o': _L1_attn_in['b_o'], 'L1_attn_gamma': _L1_attn_in['gamma'], 'L1_attn_beta': _L1_attn_in['beta'], 'L1_ffn_w_gate': _L1_ffn_in['w_gate'], 'L1_ffn_w_up': _L1_ffn_in['w_up'], 'L1_ffn_w_down': _L1_ffn_in['w_down']}
    _x0 = _d['L0_attn_x']
    _d['L0_attn_x'] = jax.random.normal(jax.random.fold_in(jax.random.key(seed), 1), (32, 256, 128), dtype=_x0.dtype)
    del _x0
    return _d

def reference(L0_attn_x, L0_attn_Wq, L0_attn_Wk, L0_attn_Wv, L0_attn_Wo, L0_ffn_rW1, L0_ffn_rb1, L0_ffn_rW2, L0_ffn_rb2, L0_ffn_rW3, L0_ffn_rb3, L0_ffn_eW1, L0_ffn_eb1, L0_ffn_eW2, L0_ffn_eb2, L1_attn_w_q, L1_attn_w_k, L1_attn_w_v, L1_attn_g_q, L1_attn_g_k, L1_attn_w_o, L1_attn_b_o, L1_attn_gamma, L1_attn_beta, L1_ffn_w_gate, L1_ffn_w_up, L1_ffn_w_down):

    def _L0_attn_ref(x, Wq, Wk, Wv, Wo):
        import jax, jax.numpy as jnp
        import numpy as np
        EMBED = 128
        WIN = 128
        NUM_HEADS = 16
        HQ = 16
        HKV = 4
        HEAD_DIM = EMBED // NUM_HEADS
        G = HQ // HKV
        B, S, _ = x.shape
        W = 2 * WIN + 1
        scale = 1.0 / np.sqrt(HEAD_DIM).astype(np.float32)
        Q = (x @ Wq.T).reshape(B, S, HKV, G, HEAD_DIM)
        K = (x @ Wk.T).reshape(B, S, HKV, HEAD_DIM)
        V = (x @ Wv.T).reshape(B, S, HKV, HEAD_DIM)
        offs = jnp.arange(W) - WIN
        idx = jnp.arange(S)[:, None] + offs[None, :]
        valid = (idx >= 0) & (idx < S)
        idxc = jnp.clip(idx, 0, S - 1)
        K_win = K[:, idxc]
        V_win = V[:, idxc]
        scores = jnp.einsum('bskgd,bswkd->bskgw', Q, K_win) * scale
        scores = jnp.where(valid[None, :, None, None, :], scores, jnp.float32(-jnp.inf))
        attn = jax.nn.softmax(scores, axis=-1)
        out = jnp.einsum('bskgw,bswkd->bskgd', attn, V_win)
        out = out.reshape(B, S, HQ * HEAD_DIM)
        return out @ Wo.T

    def _L0_ffn_ref(x, rW1, rb1, rW2, rb2, rW3, rb3, eW1, eb1, eW2, eb2):
        import jax, jax.numpy as jnp
        import numpy as np
        N_EMBD = 128
        N_EXPERTS = 8
        TOP_K = 2
        CAPACITY_FACTOR = 1.25
        B, T, C = x.shape
        E = rb3.shape[0]
        k = TOP_K
        capacity = int(T / E * CAPACITY_FACTOR)
        h = jax.nn.relu(x @ rW1 + rb1)
        h = jax.nn.relu(h @ rW2 + rb2)
        scales = jax.nn.softmax(h @ rW3 + rb3, axis=-1)
        topk_scales, topk_experts = jax.lax.top_k(scales, k)
        e_flat = topk_experts.reshape(B, T * k)
        onehot = jax.nn.one_hot(e_flat, E, dtype=jnp.int32)
        pos_excl = jnp.cumsum(onehot, axis=1) - onehot
        pos = jnp.take_along_axis(pos_excl, e_flat[..., None], axis=-1)[..., 0]
        keep = pos < capacity
        pos_c = jnp.where(keep, pos, capacity)
        b_idx = jnp.broadcast_to(jnp.arange(B)[:, None], (B, T * k))
        x_rep = jnp.repeat(x, k, axis=1)
        dispatched = jnp.zeros((E, B, capacity, C), x.dtype)
        dispatched = dispatched.at[e_flat, b_idx, pos_c].set(jnp.where(keep[..., None], x_rep, 0.0), mode='drop')
        hh = jax.nn.relu(jnp.einsum('ebnc,ech->ebnh', dispatched, eW1) + eb1[:, None, None, :])
        eout = jnp.einsum('ebnh,ehc->ebnc', hh, eW2) + eb2[:, None, None, :]
        gathered = eout[e_flat, b_idx, pos_c]
        gathered = jnp.where(keep[..., None], gathered, 0.0).reshape(B, T, k, C)
        out = jnp.sum(topk_scales[..., None] * gathered, axis=2)
        return out

    def _L1_attn_ref(x, w_q, w_k, w_v, g_q, g_k, w_o, b_o, gamma, beta):
        import jax, jax.numpy as jnp
        import numpy as np
        DIM = 128
        HEADS = 16
        HEAD_DIM = DIM // HEADS
        COLLAPSE_THRESHOLD = 0.27
        SHARPNESS = 15.0
        LN_EPS = 1e-05
        NORM_EPS = 1e-12

        def _layernorm(x, gamma, beta):
            mu = jnp.mean(x, axis=-1, keepdims=True)
            var = jnp.mean(jnp.square(x - mu), axis=-1, keepdims=True)
            return (x - mu) * jax.lax.rsqrt(var + LN_EPS) * gamma + beta

        def _l2_normalize(x):
            n = jnp.sqrt(jnp.sum(jnp.square(x), axis=-1, keepdims=True))
            return x / jnp.maximum(n, NORM_EPS)
        B, T, D = x.shape
        x_norm = _layernorm(x, gamma, beta)
        q = (x_norm @ w_q).reshape(B, T, HEADS, HEAD_DIM).transpose(0, 2, 1, 3)
        k = (x_norm @ w_k).reshape(B, T, HEADS, HEAD_DIM).transpose(0, 2, 1, 3)
        v = (x @ w_v).reshape(B, T, HEADS, HEAD_DIM).transpose(0, 2, 1, 3)
        q = _l2_normalize(q)
        k = _l2_normalize(k)
        align = jnp.einsum('bhqd,bhkd->bhqk', q, k)
        resonance = 0.5 + 0.5 * jnp.tanh((align - COLLAPSE_THRESHOLD) * SHARPNESS)
        gate_q = 0.25 + 0.75 * jax.nn.sigmoid(jnp.einsum('bhtd,d->bht', q, g_q))
        gate_k = 0.25 + 0.75 * jax.nn.sigmoid(jnp.einsum('bhtd,d->bht', k, g_k))
        modulation = resonance * gate_q[..., :, None] * gate_k[..., None, :]
        fused = jnp.einsum('bhqk,bhkd->bhqd', modulation, v)
        fused = fused.transpose(0, 2, 1, 3).reshape(B, T, HEADS * HEAD_DIM)
        return fused @ w_o + b_o

    def _L1_ffn_ref(x, w_gate, w_up, w_down):
        import jax, jax.numpy as jnp
        import numpy as np
        DIM = 128
        HIDDEN = 384
        SCALE = 1.0 / 127.0

        def _dequant(w_int, dtype):
            return w_int.astype(dtype) * jnp.asarray(SCALE, dtype)
        wg = _dequant(w_gate, x.dtype)
        wu = _dequant(w_up, x.dtype)
        wd = _dequant(w_down, x.dtype)
        gate = jnp.einsum('bsd,hd->bsh', x, wg)
        up = jnp.einsum('bsd,hd->bsh', x, wu)
        h = jax.nn.silu(gate) * up
        return jnp.einsum('bsh,dh->bsd', h, wd)
    x = L0_attn_x
    x = x + 0.5 * _L0_ffn_ref(_layernorm(x, axis=-1), L0_ffn_rW1, L0_ffn_rb1, L0_ffn_rW2, L0_ffn_rb2, L0_ffn_rW3, L0_ffn_rb3, L0_ffn_eW1, L0_ffn_eb1, L0_ffn_eW2, L0_ffn_eb2)
    x = x + _L0_attn_ref(_layernorm(x, axis=-1), L0_attn_Wq, L0_attn_Wk, L0_attn_Wv, L0_attn_Wo)
    x = x + 0.5 * _L0_ffn_ref(_layernorm(x, axis=-1), L0_ffn_rW1, L0_ffn_rb1, L0_ffn_rW2, L0_ffn_rb2, L0_ffn_rW3, L0_ffn_rb3, L0_ffn_eW1, L0_ffn_eb1, L0_ffn_eW2, L0_ffn_eb2)
    x = x + 0.5 * _L1_ffn_ref(_layernorm(x, axis=-1), L1_ffn_w_gate, L1_ffn_w_up, L1_ffn_w_down)
    x = x + _L1_attn_ref(_layernorm(x, axis=-1), L1_attn_w_q, L1_attn_w_k, L1_attn_w_v, L1_attn_g_q, L1_attn_g_k, L1_attn_w_o, L1_attn_b_o, L1_attn_gamma, L1_attn_beta)
    x = x + 0.5 * _L1_ffn_ref(_layernorm(x, axis=-1), L1_ffn_w_gate, L1_ffn_w_up, L1_ffn_w_down)
    return x

_drawn_inputs = setup_inputs


def setup_inputs(seed=0):
    import zlib

    import numpy as np

    out = dict(_drawn_inputs(seed))
    spreads = {'L0_ffn_rb1': (0.0, 0.689),
     'L0_ffn_rb2': (0.0, 0.417),
     'L0_ffn_rb3': (0.0, 0.284),
     'L0_ffn_eb1': (0.0, 0.8),
     'L0_ffn_eb2': (0.0, 0.472),
     'L1_attn_b_o': (0.0, 2.0),
     'L1_attn_gamma': (1.0, 0.6),
     'L1_attn_beta': (0.0, 2.0)}
    factors = {'L0_attn_Wq': 8.0,
     'L0_attn_Wk': 8.0,
     'L0_attn_Wv': 8.0,
     'L0_attn_Wo': 8.0,
     'L0_ffn_rW1': 4.301,
     'L0_ffn_rW2': 4.613,
     'L0_ffn_rW3': 3.526,
     'L0_ffn_eW1': 5.54,
     'L0_ffn_eW2': 4.275,
     'L1_attn_g_q': 8.0,
     'L1_attn_g_k': 25.678}
    for name, (base, spread) in spreads.items():
        noise = np.random.default_rng([zlib.crc32(name.encode()), seed]).standard_normal(out[name].shape)
        drawn = base * np.exp(spread * noise) if base else spread * noise
        out[name] = jnp.asarray(drawn.astype(out[name].dtype))
    for name, factor in factors.items():
        out[name] = (out[name] * factor).astype(out[name].dtype)
    return out
```

```python
from contextlib import ExitStack

import concourse.bass as bass
from concourse import mybir

ALU = mybir.AluOpType
ACT = mybir.ActivationFunctionType
AX = mybir.AxisListType
F32 = mybir.dt.float32
F32R = mybir.dt.float32r
BF16 = mybir.dt.bfloat16
I32 = mybir.dt.int32
U32 = mybir.dt.uint32

P = 128
C = 128
SEQ = 256
TS = SEQ // P
NB = 2
NT = NB * TS
TOK = NT * P
STREAMS = 2
PSF = 512

RH = 512
HC = RH // P
E = 8
CAP = SEQ * 5 // 4 // E
SLOTS = E * CAP
CHUNKS = [(c, min(P, SLOTS - c)) for c in range(0, SLOTS, P)]
EG = 4

HEADS = 16
HD = 8
KV = 4
GQ = HEADS // KV
PART = 32
USED = 3 * HD
FH = 384
FC = FH // P

LN_EPS = 1e-5
NORM_FLOOR = 1e-24
MASKED = -1e30
SHARP = 15.0
THRESHOLD = 0.27
DEQUANT = 1.0 / 127.0

RING = 6
P_RING = 3
UNITS = NB * 8
SKEW = 2
CONSTS = 16 + STREAMS

MOE = ["stats", "norm", "norm_t", "router1", "router2", "logits", "choose", "prefix", "dispatch", "experts", "slots",
       "combine"]
WINDOW = ["stats", "norm", "norm_t", "qkv", "stack_t", "row_max", "stack_t", "window", "heads_t", "project"]
GATED = ["stats", "norm", "norm_t", "gate_up", "down"]
RESONANCE = ["stats", "norm", "restats", "renorm", "norm_t2", "qkv1", "unit", "split1", "stack1_t", "resonance",
             "heads_t", "project1"]
ROUND_STEPS = MOE + WINDOW + MOE + GATED + RESONANCE + GATED


def psum_uses(step, n):
    return {
        "norm_t": [1], "router1": [1] * HC, "router2": [1] * HC, "logits": [1], "prefix": [1],
        "dispatch": [1] * (NB + len(CHUNKS)), "experts": ["a"] * (E // EG) + [1] * E, "slots": [1] * NB,
        "combine": [1], "qkv": [1] * (NT // 2), "stack_t": [1] * (5 - n), "row_max": [2] * (NT * 4),
        "window": ["a"] * NB + [2] * UNITS, "heads_t": [1], "project": [1], "gate_up": [1] * (2 * FC), "down": [1],
        "norm_t2": [1, 1], "qkv1": [1] * (NT // 2 + 1), "stack1_t": [1] * 8,
        "resonance": ["a"] * NB + [2] * UNITS, "project1": [1],
    }.get(step, [])


def schedule():
    seen, out = {}, []
    for step in ROUND_STEPS:
        for s in range(STREAMS):
            n = seen.get((step, s), 0)
            seen[(step, s)] = n + 1
            out.append((step, s, n))
    return out


def bank_plan(steps):
    plan, count, last = {}, [0] * 8, [None] * 8
    at = held = 0
    for step, s, n in steps:
        for i, size in enumerate(psum_uses(step, n)):
            if size == "a":
                b, width = RING + held, 1
                held = (held + 1) % 2
            else:
                width = size
                at += at % width
                b = at % RING
                at += width
            before = {last[k] for k in range(b, b + width)} - {None}
            count[b] += 1
            for k in range(b, b + width):
                last[k] = (b, count[b])
            plan[(step, s, n, i)] = (b, count[b], sorted(before))
    return plan


def macaron_kernel(nc, x_in, w, out):
    B = x_in.shape[0]
    ROUNDS = B // (NB * STREAMS)
    STEPS = schedule()
    PLAN = bank_plan(STEPS)
    unit_base = {}
    for step, s, n in STEPS:
        if step in ("window", "resonance"):
            unit_base[(step, s, n)] = UNITS * len(unit_base)

    ctx = ExitStack()
    with ctx:
        def sb(name, shape, dt=F32):
            return ctx.enter_context(nc.sbuf_tensor(name, shape, dt))

        round_sems = []

        def sem(name):
            one = ctx.enter_context(nc.semaphore(name))
            round_sems.append(one)
            return one

        def per_stream(name):
            return [sem(f"{name}{s}") for s in range(STREAMS)]

        W = {name: sb(f"w_{name}", list(ap.shape), ap.dtype) for name, ap in w.items() if ap.dtype != I32}
        gate_f = sb("gate_f", [P, FH])
        up_f = sb("up_f", [P, FH])
        down_f = sb("down_f", [P, FC, C])
        ident = sb("ident", [P, P])
        ident_b = sb("ident_b", [P, P], BF16)
        ones = sb("ones", [P, P])
        ones_b = sb("ones_b", [P, P], BF16)
        earlier = sb("earlier", [P, P], BF16)
        slot_no = sb("slot_no", [P, CAP])
        expert_no = sb("expert_no", [P, E])
        far_low = sb("far_low", [P, P], BF16)
        far_high = sb("far_high", [P, P], BF16)
        minus_half = sb("minus_half", [P, NT * 2 * HEADS])
        tanh_bias = sb("tanh_bias", [P, 1])

        def both(name, shape, dt=F32):
            return [sb(f"{name}{s}", shape, dt) for s in range(STREAMS)]

        x = both("x", [P, NT, C])
        stats = both("stats", [P, NT, 6])
        mean_var = both("mean_var", [P, NT, 2])
        var_eps = both("var_eps", [P, NT])
        rstd = both("rstd", [P, NT])
        xn = both("xn", [P, NT, C])
        xh = both("xh", [P, NT, C])
        xnT = both("xnT", [P, TOK])
        big = both("big", [P, 2 * HC * TOK])
        hid = both("hid", [P, HC * E * NB * CAP])
        small = both("small", [P, 8, NT, E])
        top = both("top", [P, NT, 8])
        top_at = both("top_at", [P, NT, 8], U32)
        chosen = both("chosen", [P, NT, E], BF16)
        shareT = both("shareT", [P, len(CHUNKS), TOK])
        slotT = both("slotT", [P, E, NB, CAP])
        hraw = both("hraw", [P, 2, HC, NB * CAP])
        eoT = both("eoT", [P, NB, E, CAP])
        eo = both("eo", [P, NB, len(CHUNKS), C])
        v0 = both("v0", [P, NT, KV, HD + 1])
        ss = both("ss", [P, NT, 2 * HEADS])
        inv = both("inv", [P, NT, 2 * HEADS])
        gates = both("gates", [P, NT, 2 * HEADS])
        rden = both("rden", [P, NT, HEADS])
        probs = sb("probs", [P, P_RING, 2 * PSF])

        h1 = [big[s][:, 0:HC * TOK].rearrange("p (c t) -> p c t", c=HC) for s in range(STREAMS)]
        h2 = [big[s][:, HC * TOK:2 * HC * TOK].rearrange("p (c t) -> p c t", c=HC) for s in range(STREAMS)]
        qT = [sb(f"qT{s}", [P, 4, TOK], F32R) for s in range(STREAMS)]
        kT = [sb(f"kT{s}", [P, 4, TOK], F32R) for s in range(STREAMS)]
        place = [hid[s][:, 0:NT * SLOTS].rearrange("p (t c) -> p t c", t=NT) for s in range(STREAMS)]
        share = [hid[s][:, NT * SLOTS:2 * NT * SLOTS].rearrange("p (t c) -> p t c", t=NT) for s in range(STREAMS)]
        xhT = [shareT[s][:, 0, :] for s in range(STREAMS)]
        v1 = [eo[s][:, :, :, :].rearrange("p b i c -> p (b i c)")[:, 0:NT * C].rearrange("p (t c) -> p t c", t=NT)
              for s in range(STREAMS)]
        hh = [hid[s][:, :].rearrange("p (e c n) -> p e c n", e=E, c=HC) for s in range(STREAMS)]
        qs = [big[s][:, 0:NT * HEADS * PART].rearrange("p (t h r) -> p t h r", t=NT, h=HEADS) for s in range(STREAMS)]
        ks = [big[s][:, NT * HEADS * PART:2 * NT * HEADS * PART].rearrange("p (t h r) -> p t h r", t=NT, h=HEADS)
              for s in range(STREAMS)]
        qk = [hid[s][:, 0:NT * 2 * C].rearrange("p (t n) -> p t n", t=NT) for s in range(STREAMS)]
        qk2 = [hid[s][:, NT * 2 * C:2 * NT * 2 * C].rearrange("p (t n) -> p t n", t=NT) for s in range(STREAMS)]
        gt = [hid[s][:, 0:TOK] for s in range(STREAMS)]
        gg = [hid[s][:, TOK:(1 + FC) * TOK].rearrange("p (c t) -> p c t", c=FC) for s in range(STREAMS)]
        gh = [big[s][:, 0:FC * TOK].rearrange("p (c t) -> p c t", c=FC) for s in range(STREAMS)]

        at = 0
        for name, ap in w.items():
            if ap.dtype == I32:
                n = ap.shape[1] if len(ap.shape) == 2 else ap.shape[1] * ap.shape[2]
                W[name] = big[0][:, at:at + n].bitcast(I32)
                if len(ap.shape) == 3:
                    W[name] = W[name].rearrange("p (c n) -> p c n", c=ap.shape[1])
                at += n

        psum = ctx.enter_context(nc.psum_tensor("psum", [P, 8, PSF], F32))

        weights_in = ctx.enter_context(nc.semaphore("weights_in"))
        consts_done = ctx.enter_context(nc.semaphore("consts_done"))
        dequant_done = ctx.enter_context(nc.semaphore("dequant_done"))
        first = len(round_sems)
        bank_full = [sem(f"bank_full{b}") for b in range(8)]
        bank_read = [sem(f"bank_read{b}") for b in range(8)]
        probs_used = sem("probs_used")
        x_in_done = per_stream("x_in_done")
        x_out_done = per_stream("x_out_done")
        dve_link = sem("dve_link")
        var_ready = per_stream("var_ready")
        rstd_ready = per_stream("rstd_ready")
        xn_ready = per_stream("xn_ready")
        logit_shifted = per_stream("logit_shifted")
        logit_exp = per_stream("logit_exp")
        chosen_ready = per_stream("chosen_ready")
        place_ready = per_stream("place_ready")
        share_ready = per_stream("share_ready")
        hh_ready = per_stream("hh_ready")
        k_ones = per_stream("k_ones")
        q_high = per_stream("q_high")
        q_stacked = per_stream("q_stacked")
        tanh_gate = per_stream("tanh_gate")
        squares_ready = per_stream("squares_ready")
        inv_ready = per_stream("inv_ready")
        unit_qk = per_stream("unit_qk")
        gate_arg = per_stream("gate_arg")
        gate_tanh = per_stream("gate_tanh")

        def bank(step, s, n, i):
            return PLAN[(step, s, n, i)][0]

        def cols(step, s, n, i, lo, hi):
            b = bank(step, s, n, i)
            if hi <= PSF:
                return psum[:, b, lo:hi]
            return psum[:, b:b + 2, :].rearrange("p a n -> p (a n)")[:, lo:hi]

        def wait_full(eng, step, s, n, i):
            b, k, _ = PLAN[(step, s, n, i)]
            eng.wait_ge(bank_full[b], k)

        def wait_free(eng, step, s, n, i):
            for b, k in PLAN[(step, s, n, i)][2]:
                eng.wait_ge(bank_read[b], k)

        def full(step, s, n, i):
            return bank_full[bank(step, s, n, i)]

        def read(step, s, n, i):
            return bank_read[bank(step, s, n, i)]

        def wait_read(eng, step, s, n, i):
            b, k, _ = PLAN[(step, s, n, i)]
            eng.wait_ge(bank_read[b], k)

        def wait_probs_used(eng, unit):
            step, s, n = next(key for key, base in unit_base.items() if base <= unit < base + UNITS)
            u = unit - unit_base[(step, s, n)]
            if u % 8 == 7:
                wait_full(eng, step, s, n, u // 8)
            else:
                eng.wait_ge(probs_used, unit + 1 - (unit + 1) // 8)

        with nc.Block() as block:
            @block.sync
            def _(sp):
                for name, ap in w.items():
                    sp.dma_start(W[name][...], ap).then_inc(weights_in, 16)

            @block.gpsimd
            def _(pool):
                done = [0]

                def const(ins):
                    done[0] += 1
                    ins.then_inc(consts_done, 1)

                def chained(ins):
                    const(ins)
                    pool.wait_ge(consts_done, done[0])

                const(pool.memset(ones[:, :], 1.0))
                const(pool.memset(ones_b[:, :], 1.0))
                const(pool.memset(minus_half[:, :], -0.5))
                const(pool.memset(tanh_bias[:, :], -SHARP * THRESHOLD))
                for m in (ident, ident_b, far_low, far_high):
                    const(pool.memset(m[:, :], 0.0))
                chained(pool.memset(earlier[:, :], 1.0))
                for m in (ident, ident_b):
                    const(pool.affine_select(out=m[:, :], in_=m[:, :], compare_op=ALU.not_equal, fill=1.0,
                                             base=0, pattern=[[-1, P]], channel_multiplier=1))
                const(pool.affine_select(out=earlier[:, :], in_=earlier[:, :], compare_op=ALU.is_gt, fill=0.0,
                                         base=0, pattern=[[1, P]], channel_multiplier=-1))
                const(pool.affine_select(out=far_low[:, :], in_=far_low[:, :], compare_op=ALU.is_ge, fill=MASKED,
                                         base=0, pattern=[[-1, P]], channel_multiplier=1))
                const(pool.affine_select(out=far_high[:, :], in_=far_high[:, :], compare_op=ALU.is_ge, fill=MASKED,
                                         base=0, pattern=[[1, P]], channel_multiplier=-1))
                const(pool.iota(slot_no[:, :], pattern=[[1, CAP]], base=1, channel_multiplier=0,
                                allow_small_or_imprecise_dtypes=True))
                const(pool.iota(expert_no[:, :], pattern=[[1, E]], base=0, channel_multiplier=0,
                                allow_small_or_imprecise_dtypes=True))
                for s in range(STREAMS):
                    const(pool.memset(v0[s][:, :, :, HD:HD + 1], 1.0))

            @block.vector
            def _(dve):
                dve.wait_ge(weights_in, 16 * len(w))
                for a, b in ((gate_f, "w_gate"), (up_f, "w_up"), (down_f, "w_down")):
                    dve.tensor_scalar(a[...], W[b][...], DEQUANT, None, ALU.mult).then_inc(dequant_done, 1)

        with nc.Fori(0, ROUNDS) as rnd:
            with nc.Block() as block:
                @block.sync
                def _(sp):
                    for s in range(STREAMS):
                        src = x_in[bass.ds(rnd * (NB * STREAMS) + s * NB, NB)].rearrange("b (k p) c -> p (b k) c", p=P)
                        sp.dma_start(x[s][:, :, :], src).then_inc(x_in_done[s], 16)
                    for s in range(STREAMS):
                        wait_read(sp, "down", s, 1, 0)
                        dst = out[bass.ds(rnd * (NB * STREAMS) + s * NB, NB)].rearrange("b (k p) c -> p (b k) c", p=P)
                        sp.dma_start(dst, x[s][:, :, :]).then_inc(x_out_done[s], 16)
                    for s in range(STREAMS):
                        sp.wait_ge(x_out_done[s], 16)

                @block.tensor
                def _(pe):
                    def transposes(step, s, n, i, src, tiles):
                        wait_free(pe, step, s, n, i)
                        for t in range(tiles):
                            last = pe.transpose(cols(step, s, n, i, t * P, (t + 1) * P), src(t), ident[:, :])
                        last.then_inc(full(step, s, n, i), 1)

                    def norm_t(s, n):
                        pe.wait_ge(xn_ready[s], [1, 2, 3, 4, 7][n])
                        transposes("norm_t", s, n, 0, lambda t: xn[s][:, t, :], NT)

                    def router1(s, n):
                        wait_read(pe, "norm_t", s, 2 * n, 0)
                        for c in range(HC):
                            wait_free(pe, "router1", s, n, c)
                            pe.matmul(cols("router1", s, n, c, 0, TOK), W["rW1"][:, c * P:(c + 1) * P], xnT[s][:, :],
                                      start=True, stop=True).then_inc(full("router1", s, n, c), 1)

                    def router2(s, n):
                        for c in range(HC):
                            wait_read(pe, "router1", s, n, c)
                        for c in range(HC):
                            wait_free(pe, "router2", s, n, c)
                            for k in range(HC):
                                last = pe.matmul(cols("router2", s, n, c, 0, TOK), W["rW2"][:, k, c * P:(c + 1) * P],
                                                 h1[s][:, k, :], start=(k == 0), stop=(k == HC - 1))
                            last.then_inc(full("router2", s, n, c), 1)

                    def logits(s, n):
                        for c in range(HC):
                            wait_read(pe, "router2", s, n, c)
                        wait_free(pe, "logits", s, n, 0)
                        for t in range(NT):
                            for k in range(HC):
                                last = pe.matmul(cols("logits", s, n, 0, t * E, (t + 1) * E),
                                                 h2[s][:, k, t * P:(t + 1) * P], W["rW3"][:, k, :],
                                                 start=(k == 0), stop=(k == HC - 1))
                        last.then_inc(full("logits", s, n, 0), 1)

                    def prefix(s, n):
                        pe.wait_ge(chosen_ready[s], n + 1)
                        wait_free(pe, "prefix", s, n, 0)
                        for t in range(NT):
                            o = cols("prefix", s, n, 0, t * E, (t + 1) * E)
                            first_tile = t % TS == 0
                            last = pe.matmul(o, earlier[:, :], chosen[s][:, t, :], start=True, stop=first_tile)
                            if not first_tile:
                                last = pe.matmul(o, ones_b[:, :], chosen[s][:, t - 1, :], start=False, stop=True)
                        last.then_inc(full("prefix", s, n, 0), 1)

                    def dispatch(s, n):
                        pe.wait_ge(place_ready[s], n + 1)
                        for b in range(NB):
                            wait_free(pe, "dispatch", s, n, b)
                            for k in range(TS):
                                t = b * TS + k
                                last = pe.matmul(cols("dispatch", s, n, b, 0, SLOTS), xn[s][:, t, :],
                                                 place[s][:, t, :], start=(k == 0), stop=(k == TS - 1))
                            last.then_inc(full("dispatch", s, n, b), 1)
                        pe.wait_ge(share_ready[s], n + 1)
                        for i, (c, m) in enumerate(CHUNKS):
                            u = NB + i
                            wait_free(pe, "dispatch", s, n, u)
                            for t in range(NT):
                                last = pe.transpose(cols("dispatch", s, n, u, t * P, (t + 1) * P)[0:m, :],
                                                    share[s][:, t, c:c + m], ident[:, :])
                            last.then_inc(full("dispatch", s, n, u), 1)

                    def experts(s, n):
                        for b in range(NB):
                            wait_read(pe, "dispatch", s, n, b)
                        ns = NB * CAP
                        for i in range(E + SKEW):
                            if i < E:
                                wait_free(pe, "experts", s, n, 2 + i)
                                for c in range(HC):
                                    last = pe.matmul(cols("experts", s, n, 2 + i, c * ns, (c + 1) * ns),
                                                     W["eW1"][:, i, c * P:(c + 1) * P],
                                                     slotT[s][:, i, :, :].rearrange("p b c -> p (b c)"),
                                                     start=True, stop=True)
                                last.then_inc(full("experts", s, n, 2 + i), 1)
                            e = i - SKEW
                            if e < 0:
                                continue
                            if e % EG == 0:
                                wait_free(pe, "experts", s, n, e // EG)
                            pe.wait_ge(hh_ready[s], E * n + e + 1)
                            for c in range(HC):
                                last = pe.matmul(cols("experts", s, n, e // EG, e % EG * ns, (e % EG + 1) * ns),
                                                 W["eW2"][:, e, c, :], hh[s][:, e, c, :],
                                                 start=(c == 0), stop=(c == HC - 1))
                            if e % EG == EG - 1:
                                last.then_inc(full("experts", s, n, e // EG), 1)

                    def slots(s, n):
                        for i in range(E // EG):
                            wait_read(pe, "experts", s, n, i)
                        for b in range(NB):
                            wait_free(pe, "slots", s, n, b)
                            flat = eoT[s][:, b, :, :].rearrange("p e c -> p (e c)")
                            for i, (c, m) in enumerate(CHUNKS):
                                last = pe.transpose(cols("slots", s, n, b, i * P, (i + 1) * P)[0:m, :],
                                                    flat[:, c:c + m], ident[:, :])
                            last.then_inc(full("slots", s, n, b), 1)

                    def combine(s, n):
                        for b in range(NB):
                            wait_read(pe, "slots", s, n, b)
                        for i in range(len(CHUNKS)):
                            wait_read(pe, "dispatch", s, n, NB + i)
                        wait_free(pe, "combine", s, n, 0)
                        for t in range(NT):
                            for i, (c, m) in enumerate(CHUNKS):
                                last = pe.matmul(cols("combine", s, n, 0, t * C, (t + 1) * C),
                                                 shareT[s][0:m, i, t * P:(t + 1) * P], eo[s][0:m, t // TS, i, :],
                                                 start=(i == 0), stop=(i == len(CHUNKS) - 1))
                        last.then_inc(full("combine", s, n, 0), 1)

                    def qkv(s, n):
                        wait_read(pe, "norm_t", s, 1, 0)
                        for i in range(NT // 2):
                            wait_free(pe, "qkv", s, n, i)
                            for j in range(2):
                                t = 2 * i + j
                                last = pe.matmul(cols("qkv", s, n, i, j * 192, (j + 1) * 192),
                                                 xnT[s][:, t * P:(t + 1) * P], W["qkv0"][:, :], start=True, stop=True)
                            last.then_inc(full("qkv", s, n, i), 1)

                    def stack_t(s, n):
                        if n == 0:
                            for i in range(NT // 2):
                                wait_read(pe, "qkv", s, 0, i)
                            pe.wait_ge(k_ones[s], 1)
                        else:
                            for u in range(NT * 4):
                                wait_read(pe, "row_max", s, 0, u)
                        for j in range(4):
                            transposes("stack_t", s, n, j, lambda t: qs[s][:, t, 4 * j:4 * j + 4, :]
                                       .rearrange("p h r -> p (h r)"), NT)
                        if n == 0:
                            transposes("stack_t", s, n, 4, lambda t: ks[s][:, t, 0:4, :]
                                       .rearrange("p h r -> p (h r)"), NT)

                    def row_max(s, n):
                        for j in range(5):
                            wait_read(pe, "stack_t", s, 0, j)
                        for t in range(NT):
                            b, k = t // TS, t % TS
                            for m in range(4):
                                u = 4 * t + m
                                wait_free(pe, "row_max", s, n, u)
                                for gg_ in range(2):
                                    g = 2 * (m // 2) + gg_
                                    for jj in range(2):
                                        j = 2 * (m % 2) + jj
                                        o = cols("row_max", s, n, u, gg_ * PSF + jj * SEQ, gg_ * PSF + (jj + 1) * SEQ)
                                        pe.matmul(o, qT[s][g * PART:g * PART + USED, j, t * P:(t + 1) * P],
                                                  kT[s][g * PART:g * PART + USED, 0, b * SEQ:(b + 1) * SEQ],
                                                  start=(jj == 0), stop=False, skip_group_check=True)
                                for gg_ in range(2):
                                    o = cols("row_max", s, n, u, gg_ * PSF, (gg_ + 1) * PSF) \
                                        .rearrange("p (j k) -> p j k", j=2)[:, :, (1 - k) * P:(2 - k) * P]
                                    far = (far_low if k == 0 else far_high)[:, None, :].to_broadcast([P, 2, P])
                                    last = pe.matmul(o, ident_b[:, :], far, start=False, stop=True,
                                                     skip_group_check=True)
                                last.then_inc(full("row_max", s, n, u), 1)

                    def window(s, n):
                        for j in range(4):
                            wait_read(pe, "stack_t", s, 1, j)
                        base = unit_base[("window", s, n)]
                        for i in range(UNITS + SKEW):
                            if i < UNITS:
                                b, g, jp = i // 8, i // 2 % 4, i % 2
                                wait_free(pe, "window", s, n, 2 + i)
                                for k in range(TS):
                                    o = cols("window", s, n, 2 + i, k * PSF, (k + 1) * PSF)
                                    rows = slice(g * PART, g * PART + USED + 1)
                                    pe.matmul(o, kT[s][rows, 0, b * SEQ + k * P:b * SEQ + (k + 1) * P],
                                              qT[s][rows, 2 * jp:2 * jp + 2, b * SEQ:(b + 1) * SEQ],
                                              start=True, stop=False, skip_group_check=True)
                                for k in range(TS):
                                    o = cols("window", s, n, 2 + i, k * PSF, (k + 1) * PSF) \
                                        .rearrange("p (j q) -> p j q", j=2)[:, :, (1 - k) * P:(2 - k) * P]
                                    far = (far_low if k == 0 else far_high)[:, None, :].to_broadcast([P, 2, P])
                                    last = pe.matmul(o, ident_b[:, :], far, start=False, stop=True,
                                                     skip_group_check=True)
                                last.then_inc(full("window", s, n, 2 + i), 1)
                            u = i - SKEW
                            if u < 0:
                                continue
                            b, g, jp = u // 8, u // 2 % 4, u % 2
                            if u % 8 == 0:
                                wait_free(pe, "window", s, n, b)
                            wait_read(pe, "window", s, n, 2 + u)
                            pr = probs[:, (base + u) % P_RING, :].rearrange("p (k j q) -> p k j q", k=TS, j=2)
                            for jj in range(2):
                                h = 4 * g + 2 * jp + jj
                                for q in range(TS):
                                    at = (q * HEADS + h) * (HD + 1)
                                    for k in range(TS):
                                        last = pe.matmul(cols("window", s, n, b, at, at + HD + 1),
                                                         pr[:, k, jj, q * P:(q + 1) * P],
                                                         v0[s][:, b * TS + k, g, :], start=(k == 0), stop=(k == TS - 1))
                            last.then_inc(full("window", s, n, b) if u % 8 == 7 else probs_used, 1)

                    def heads_t(s, n):
                        for b in range(NB):
                            wait_read(pe, ("window", "resonance")[n], s, 0, b)
                        transposes("heads_t", s, n, 0, lambda t: xh[s][:, t, :], NT)

                    def project(s, n, step="project", wname="wo0", k=0):
                        wait_read(pe, "heads_t", s, k, 0)
                        wait_free(pe, step, s, n, 0)
                        for t in range(NT):
                            last = pe.matmul(cols(step, s, n, 0, t * C, (t + 1) * C), xhT[s][:, t * P:(t + 1) * P],
                                             W[wname][:, :], start=True, stop=True)
                        last.then_inc(full(step, s, n, 0), 1)

                    def gate_up(s, n):
                        wait_read(pe, "norm_t", s, 3 + n, 0)
                        for c in range(FC):
                            for i, wt in enumerate((gate_f, up_f)):
                                wait_free(pe, "gate_up", s, n, 2 * c + i)
                                pe.matmul(cols("gate_up", s, n, 2 * c + i, 0, TOK), wt[:, c * P:(c + 1) * P],
                                          xnT[s][:, :], start=True, stop=True) \
                                    .then_inc(full("gate_up", s, n, 2 * c + i), 1)

                    def down(s, n):
                        for c in range(FC):
                            wait_read(pe, "gate_up", s, n, 2 * c + 1)
                        wait_free(pe, "down", s, n, 0)
                        for t in range(NT):
                            for c in range(FC):
                                last = pe.matmul(cols("down", s, n, 0, t * C, (t + 1) * C),
                                                 gh[s][:, c, t * P:(t + 1) * P], down_f[:, c, :],
                                                 start=(c == 0), stop=(c == FC - 1))
                        last.then_inc(full("down", s, n, 0), 1)

                    def norm_t2(s, n):
                        pe.wait_ge(xn_ready[s], 5)
                        transposes("norm_t2", s, n, 0, lambda t: xn[s][:, t, :], NT)
                        pe.wait_ge(xn_ready[s], 6)
                        transposes("norm_t2", s, n, 1, lambda t: xh[s][:, t, :], NT)

                    def qkv1(s, n):
                        wait_read(pe, "norm_t2", s, 0, 0)
                        wait_read(pe, "norm_t2", s, 0, 1)
                        for i in range(NT // 2):
                            wait_free(pe, "qkv1", s, n, i)
                            for j in range(2):
                                t = 2 * i + j
                                last = pe.matmul(cols("qkv1", s, n, i, j * 2 * C, (j + 1) * 2 * C),
                                                 xhT[s][:, t * P:(t + 1) * P], W["qk1"][:, :], start=True, stop=True)
                            last.then_inc(full("qkv1", s, n, i), 1)
                        i = NT // 2
                        wait_free(pe, "qkv1", s, n, i)
                        for t in range(NT):
                            last = pe.matmul(cols("qkv1", s, n, i, t * C, (t + 1) * C), xnT[s][:, t * P:(t + 1) * P],
                                             W["v1"][:, :], start=True, stop=True)
                        last.then_inc(full("qkv1", s, n, i), 1)

                    def stack1_t(s, n):
                        pe.wait_ge(q_stacked[s], NT)
                        for m, src in enumerate((qs, ks)):
                            for j in range(4):
                                transposes("stack1_t", s, n, 4 * m + j, lambda t: src[s][:, t, 4 * j:4 * j + 4, :]
                                           .rearrange("p h r -> p (h r)"), NT)

                    def resonance(s, n):
                        for i in range(8):
                            wait_read(pe, "stack1_t", s, n, i)
                        wait_read(pe, "qkv1", s, n, 2)
                        base = unit_base[("resonance", s, n)]
                        for i in range(UNITS + SKEW):
                            if i < UNITS:
                                b, r, m = i // 8, i // 2 % 4, i % 2
                                wait_free(pe, "resonance", s, n, 2 + i)
                                rows = slice(r * PART, r * PART + USED)
                                for k in range(TS):
                                    for jj in range(2):
                                        o = cols("resonance", s, n, 2 + i, k * PSF + jj * SEQ, k * PSF + (jj + 1) * SEQ)
                                        blk = 2 * m + jj
                                        last = pe.matmul(o, kT[s][rows, blk, b * SEQ + k * P:b * SEQ + (k + 1) * P],
                                                         qT[s][rows, blk, b * SEQ:(b + 1) * SEQ],
                                                         start=True, stop=True)
                                last.then_inc(full("resonance", s, n, 2 + i), 1)
                            u = i - SKEW
                            if u < 0:
                                continue
                            b, r, m = u // 8, u // 2 % 4, u % 2
                            if u % 8 == 0:
                                wait_free(pe, "resonance", s, n, b)
                                for k in range(TS):
                                    vv = v1[s][:, b * TS + k, None, :].to_broadcast([P, TS, C])
                                    pe.matmul(cols("resonance", s, n, b, 0, TS * C), ones[:, :], vv,
                                              start=(k == 0), stop=False, skip_group_check=True)
                            wait_read(pe, "resonance", s, n, 2 + u)
                            pr = probs[:, (base + u) % P_RING, :].rearrange("p (k j q) -> p k j q", k=TS, j=2)
                            for jj in range(2):
                                h = 4 * (2 * m + jj) + r
                                for q in range(TS):
                                    at = q * C + h * HD
                                    for k in range(TS):
                                        last = pe.matmul(cols("resonance", s, n, b, at, at + HD),
                                                         pr[:, k, jj, q * P:(q + 1) * P],
                                                         v1[s][:, b * TS + k, h * HD:(h + 1) * HD],
                                                         start=False, stop=(k == TS - 1), skip_group_check=True)
                            last.then_inc(full("resonance", s, n, b) if u % 8 == 7 else probs_used, 1)

                    pe.wait_ge(weights_in, 16 * len(w))
                    pe.wait_ge(consts_done, CONSTS)
                    pe.wait_ge(dequant_done, 3)
                    todo = {"norm_t": norm_t, "router1": router1, "router2": router2, "logits": logits,
                            "prefix": prefix, "dispatch": dispatch, "experts": experts, "slots": slots,
                            "combine": combine, "qkv": qkv, "stack_t": stack_t, "row_max": row_max,
                            "window": window, "heads_t": heads_t, "project": project, "gate_up": gate_up,
                            "down": down, "norm_t2": norm_t2, "qkv1": qkv1, "stack1_t": stack1_t,
                            "resonance": resonance,
                            "project1": lambda s, n: project(s, n, "project1", "wo1", 1)}
                    for step, s, n in STEPS:
                        if step in todo:
                            todo[step](s, n)

                @block.scalar
                def _(act):
                    def copy_out(step, s, n, i, dst, lo, hi):
                        wait_full(act, step, s, n, i)
                        act.activation(dst, cols(step, s, n, i, lo, hi), ACT.Copy).then_inc(read(step, s, n, i), 1)

                    def router(step, s, n, dst, bias):
                        for c in range(0, HC, 2):
                            wait_full(act, step, s, n, c)
                            act.activation(dst[:, c, :], cols(step, s, n, c, 0, TOK), ACT.Relu,
                                           bias=W[bias][:, c:c + 1]).then_inc(read(step, s, n, c), 1)

                    def choose(s, n):
                        act.wait_ge(logit_shifted[s], n + 1)
                        act.activation(small[s][:, 1, :, :], small[s][:, 0, :, :], ACT.Exp).then_inc(logit_exp[s], 1)

                    def dispatch(s, n):
                        for b in range(NB):
                            wait_full(act, "dispatch", s, n, b)
                            act.activation(slotT[s][:, :, b, :],
                                           cols("dispatch", s, n, b, 0, SLOTS).rearrange("p (e c) -> p e c", e=E),
                                           ACT.Copy).then_inc(read("dispatch", s, n, b), 1)

                    def slots(s, n):
                        whole = SLOTS // P
                        m = CHUNKS[-1][1]
                        for b in range(NB):
                            wait_full(act, "slots", s, n, b)
                            act.activation(eo[s][:, b, 0:whole, :], cols("slots", s, n, b, 0, whole * P)
                                           .rearrange("p (i c) -> p i c", c=C), ACT.Copy)
                            act.activation(eo[s][0:m, b, whole, :],
                                           cols("slots", s, n, b, whole * P, (whole + 1) * P)[0:m, :],
                                           ACT.Copy).then_inc(read("slots", s, n, b), 1)

                    def high_parts(s, t, heads_q, heads_k):
                        nk = heads_k.shape[1]
                        act.activation(qs[s][:, t, :, 0:2 * HD].bitcast(F32R).rearrange("p h (c d) -> p h c d", c=2),
                                       heads_q[:, :, None, :].to_broadcast([P, HEADS, 2, HD]), ACT.Copy)
                        for c in (0, 2):
                            last = act.activation(ks[s][:, t, 0:nk, c * HD:(c + 1) * HD].bitcast(F32R), heads_k, ACT.Copy)
                        last.then_inc(q_high[s], 1)

                    def qkv(s, n):
                        for i in range(NT // 2):
                            wait_full(act, "qkv", s, n, i)
                            for j in range(2):
                                ps = cols("qkv", s, n, i, j * 192, (j + 1) * 192)
                                heads = ps.rearrange("p (h d) -> p h d", d=HD)
                                act.activation(v0[s][:, 2 * i + j, :, 0:HD], heads[:, HEADS + KV:, :], ACT.Copy)
                                high_parts(s, 2 * i + j, heads[:, 0:HEADS, :], heads[:, HEADS:HEADS + KV, :])

                    def attend(step, s, n, func, scale, bias):
                        base = unit_base[(step, s, n)]
                        for u in range(UNITS):
                            wait_full(act, step, s, n, 2 + u)
                            if base + u >= P_RING:
                                wait_probs_used(act, base + u - P_RING)
                            act.activation(probs[:, (base + u) % P_RING, :], cols(step, s, n, 2 + u, 0, 2 * PSF), func,
                                           scale=scale, bias=bias).then_inc(read(step, s, n, 2 + u), 1)

                    def gate_up(s, n):
                        for c in range(FC):
                            wait_full(act, "gate_up", s, n, 2 * c)
                            if c:
                                wait_read(act, "gate_up", s, n, 2 * c - 2)
                            act.activation(gt[s], cols("gate_up", s, n, 2 * c, 0, TOK), ACT.Tanh, scale=0.5) \
                                .then_inc(tanh_gate[s], 1)

                    def qkv1(s, n):
                        for i in range(NT // 2):
                            wait_full(act, "qkv1", s, n, i)
                            src = cols("qkv1", s, n, i, 0, PSF).rearrange("p (t n) -> p t n", t=2)
                            act.activation(qk2[s][:, 2 * i:2 * i + 2, :], src, ACT.Square)
                            act.activation(qk[s][:, 2 * i:2 * i + 2, :], src, ACT.Copy) \
                                .then_inc(read("qkv1", s, n, i), 1)

                    def unit(s, n):
                        for t in range(NT):
                            act.wait_ge(unit_qk[s], t + 1)
                            u = qk[s][:, t, :].rearrange("p (m h d) -> p m h d", m=2, d=HD)
                            high_parts(s, t, u[:, 0, :, :], u[:, 1, :, :])

                    def split1(s, n):
                        act.wait_ge(gate_arg[s], 1)
                        act.activation(gates[s][:, :, :], ss[s][:, :, :], ACT.Tanh, scale=0.5).then_inc(gate_tanh[s], 1)

                    def stack_t(s, n):
                        for j in range(0, 4, 2):
                            copy_out("stack_t", s, n, j, qT[s][:, j, :], 0, TOK)

                    def stack1_t(s, n):
                        for i in range(0, 8, 2):
                            copy_out("stack1_t", s, n, i, (qT if i < 4 else kT)[s][:, i % 4, :], 0, TOK)

                    todo = {
                        "norm_t": lambda s, n: copy_out("norm_t", s, n, 0, xnT[s][:, :], 0, TOK),
                        "norm_t2": lambda s, n: copy_out("norm_t2", s, n, 0, xnT[s][:, :], 0, TOK),
                        "heads_t": lambda s, n: copy_out("heads_t", s, n, 0, xhT[s], 0, TOK),
                        "choose": choose, "dispatch": dispatch, "slots": slots, "qkv": qkv, "stack_t": stack_t,
                        "gate_up": gate_up, "qkv1": qkv1, "unit": unit, "split1": split1, "stack1_t": stack1_t,
                        "router1": lambda s, n: router("router1", s, n, h1[s], "rb1"),
                        "router2": lambda s, n: router("router2", s, n, h2[s], "rb2"),
                        "window": lambda s, n: attend("window", s, n, ACT.Exp, HD ** -0.5, 0.0),
                        "resonance": lambda s, n: attend("resonance", s, n, ACT.Tanh, SHARP, tanh_bias[:, 0:1]),
                    }
                    act.wait_ge(weights_in, 16 * len(w))
                    act.wait_ge(consts_done, CONSTS)
                    for step, s, n in STEPS:
                        if step in todo:
                            todo[step](s, n)

                @block.gpsimd
                def _(pool):
                    def power(s, k):
                        pool.wait_ge(var_ready[s], k)
                        pool.tensor_tensor(rstd[s][:, :], var_eps[s][:, :], minus_half[:, 0:NT], ALU.pow) \
                            .then_inc(rstd_ready[s], 1)

                    def dispatch(s, n):
                        pool.wait_ge(place_ready[s], n + 1)
                        pool.tensor_tensor(share[s].rearrange("p t (e c) -> p (t e) c", e=E),
                                           place[s].rearrange("p t (e c) -> p (t e) c", e=E),
                                           small[s][:, 6, :, :].rearrange("p t e -> p (t e)")[:, :, None]
                                           .to_broadcast([P, NT * E, CAP]), ALU.mult).then_inc(share_ready[s], 1)

                    def experts(s, n):
                        for e in range(E):
                            wait_read(pool, "experts", s, n, 2 + e)
                            pool.tensor_scalar(hh[s][:, e, :, :], hraw[s][:, e % 2, :, :], 0.0, None, ALU.max) \
                                .then_inc(hh_ready[s], 1)

                    def qkv(s, n):
                        pool.wait_ge(xn_ready[s], 2)
                        pool.memset(ks[s][:, :, 0:KV, USED:USED + 1], 1.0).then_inc(k_ones[s], 1)

                    def unit(s, n):
                        pool.wait_ge(squares_ready[s], 1)
                        pool.tensor_tensor(inv[s][:, :, :].rearrange("p t h -> p (t h)"),
                                           ss[s][:, :, :].rearrange("p t h -> p (t h)"), minus_half[:, :], ALU.pow) \
                            .then_inc(inv_ready[s], 1)

                    todo = {
                        "norm": lambda s, n: power(s, [1, 2, 3, 4, 5, 7][n]), "renorm": lambda s, n: power(s, 6),
                        "dispatch": dispatch, "experts": experts, "qkv": qkv, "unit": unit,
                    }
                    for step, s, n in STEPS:
                        if step in todo:
                            todo[step](s, n)

                @block.vector
                def _(dve):
                    linked = [0]

                    def link(ins):
                        linked[0] += 1
                        ins.then_inc(dve_link, 1)

                    def settle():
                        dve.wait_ge(dve_link, linked[0])

                    def variances(s, src):
                        for t in range(NT):
                            link(dve.bn_stats(stats[s][:, t, :], src[s][:, t, :]))
                        settle()
                        for t in range(NT):
                            link(dve.bn_aggr(mean_var[s][:, t, :], stats[s][:, t, :]))
                        settle()
                        dve.tensor_scalar(var_eps[s][:, :], mean_var[s][:, :, 1], LN_EPS, None, ALU.add) \
                            .then_inc(var_ready[s], 1)

                    def stats_of_x(s, n):
                        if n == 0:
                            dve.wait_ge(x_in_done[s], 16)
                        else:
                            step, k = [None, ("combine", 0), ("project", 0), ("combine", 1), ("down", 0),
                                       ("project1", 0)][n]
                            wait_read(dve, step, s, k, 0)
                        variances(s, x)

                    def normalise(s, src, dst, k):
                        dve.wait_ge(rstd_ready[s], k)
                        for t in range(NT):
                            last = dve.tensor_scalar(dst[s][:, t, :], src[s][:, t, :], mean_var[s][:, t, 0:1],
                                                     rstd[s][:, t:t + 1], ALU.subtract, ALU.mult)
                        last.then_inc(xn_ready[s], 1)

                    def norm(s, n):
                        normalise(s, x, xn, [1, 2, 3, 4, 5, 7][n])

                    def restats(s, n):
                        dve.wait_ge(xn_ready[s], 5)
                        variances(s, xn)

                    def renorm(s, n):
                        normalise(s, xn, xh, 6)
                        dve.tensor_tensor(x[s][:, :, :], x[s][:, :, :],
                                          W["bo1"][:, None, :].to_broadcast([P, NT, C]), ALU.add)

                    def router(step, s, n, dst, bias):
                        for c in range(1, HC, 2):
                            wait_full(dve, step, s, n, c)
                            dve.tensor_scalar(dst[:, c, :], cols(step, s, n, c, 0, TOK), W[bias][:, c:c + 1], 0.0,
                                              ALU.add, ALU.max).then_inc(read(step, s, n, c), 1)

                    def row(s, i):
                        return small[s][:, i, :, :]

                    def over_experts(ap):
                        return ap.to_broadcast([P, NT, E])

                    def logits(s, n):
                        wait_full(dve, "logits", s, n, 0)
                        ps = cols("logits", s, n, 0, 0, NT * E).rearrange("p (t e) -> p t e", e=E)
                        dve.tensor_tensor(row(s, 7), ps, W["rb3"][:, None, :].to_broadcast([P, NT, E]), ALU.add) \
                            .then_inc(read("logits", s, n, 0), 1)
                        wait_read(dve, "logits", s, n, 0)
                        link(dve.tensor_reduce(row(s, 3)[:, :, 0:1], row(s, 7), AX.X, ALU.max))
                        settle()
                        dve.tensor_tensor(row(s, 0), row(s, 7), over_experts(row(s, 3)[:, :, 0:1]), ALU.subtract) \
                            .then_inc(logit_shifted[s], 1)

                    def choose(s, n):
                        dve.wait_ge(logit_exp[s], n + 1)
                        link(dve.tensor_reduce(row(s, 3)[:, :, 1:2], row(s, 1), AX.X, ALU.add))
                        settle()
                        link(dve.reciprocal(row(s, 3)[:, :, 2:3], row(s, 3)[:, :, 1:2]))
                        settle()
                        link(dve.tensor_tensor(row(s, 2), row(s, 1), over_experts(row(s, 3)[:, :, 2:3]), ALU.mult))
                        settle()
                        for t in range(NT):
                            link(dve.max(top[s][:, t, :], small[s][:, 2, t, :]))
                        settle()
                        for t in range(NT):
                            link(dve.max_index(top_at[s][:, t, :], top[s][:, t, :], small[s][:, 2, t, :]))
                        settle()
                        numbers = expert_no[:, None, :].to_broadcast([P, NT, E])
                        for k in range(2):
                            link(dve.tensor_tensor(row(s, 4 + k), numbers, over_experts(top_at[s][:, :, k:k + 1]),
                                                   ALU.is_equal))
                        settle()
                        dve.tensor_tensor(chosen[s][:, :, :], row(s, 4), row(s, 5), ALU.add) \
                            .then_inc(chosen_ready[s], 1)
                        dve.wait_ge(chosen_ready[s], n + 1)
                        link(dve.tensor_tensor(row(s, 6), row(s, 2), chosen[s][:, :, :], ALU.mult))

                    def prefix(s, n):
                        wait_full(dve, "prefix", s, n, 0)
                        ps = cols("prefix", s, n, 0, 0, NT * E).rearrange("p (t e) -> p t e", e=E)
                        dve.scalar_tensor_tensor(out=row(s, 5), in0=ps, scalar=1.0, in1=chosen[s][:, :, :],
                                                 op0=ALU.add, op1=ALU.mult).then_inc(read("prefix", s, n, 0), 1)
                        wait_read(dve, "prefix", s, n, 0)
                        dve.tensor_tensor(place[s].rearrange("p t (e c) -> p (t e) c", e=E),
                                          slot_no[:, None, :].to_broadcast([P, NT * E, CAP]),
                                          row(s, 5).rearrange("p t e -> p (t e)")[:, :, None]
                                          .to_broadcast([P, NT * E, CAP]), ALU.is_equal).then_inc(place_ready[s], 1)

                    def dispatch(s, n):
                        for i, (c, m) in enumerate(CHUNKS):
                            wait_full(dve, "dispatch", s, n, NB + i)
                            dve.tensor_copy(shareT[s][0:m, i, :], cols("dispatch", s, n, NB + i, 0, TOK)[0:m, :]) \
                                .then_inc(read("dispatch", s, n, NB + i), 1)

                    def experts(s, n):
                        ns = NB * CAP
                        for i in range(E + SKEW):
                            if i < E:
                                wait_full(dve, "experts", s, n, 2 + i)
                                if E * n + i >= 2:
                                    dve.wait_ge(hh_ready[s], E * n + i - 1)
                                dve.tensor_tensor(hraw[s][:, i % 2, :, :],
                                                  cols("experts", s, n, 2 + i, 0, HC * ns)
                                                  .rearrange("p (c n) -> p c n", c=HC),
                                                  W["eb1"][:, i, :, None].to_broadcast([P, HC, ns]), ALU.add) \
                                    .then_inc(read("experts", s, n, 2 + i), 1)
                            e = i - SKEW
                            if e < 0 or e % EG != EG - 1:
                                continue
                            g = e // EG
                            wait_full(dve, "experts", s, n, g)
                            ps = cols("experts", s, n, g, 0, EG * ns).rearrange("p (e b c) -> p e b c", e=EG, b=NB)
                            for b in range(NB):
                                last = dve.tensor_tensor(eoT[s][:, b, g * EG:(g + 1) * EG, :], ps[:, :, b, :],
                                                         W["eb2"][:, g * EG:(g + 1) * EG, None]
                                                         .to_broadcast([P, EG, CAP]), ALU.add)
                            last.then_inc(read("experts", s, n, g), 1)

                    def add_to_x(step, s, n, factor):
                        wait_full(dve, step, s, n, 0)
                        dve.scalar_tensor_tensor(out=x[s][:, :, :].rearrange("p t c -> p (t c)"),
                                                 in0=cols(step, s, n, 0, 0, NT * C), scalar=factor,
                                                 in1=x[s][:, :, :].rearrange("p t c -> p (t c)"),
                                                 op0=ALU.mult, op1=ALU.add).then_inc(read(step, s, n, 0), 1)

                    def qkv(s, n):
                        for i in range(NT // 2):
                            wait_full(dve, "qkv", s, n, i)
                            dve.wait_ge(q_high[s], 2 * i + 2)
                            for j in range(2):
                                t = 2 * i + j
                                heads = cols("qkv", s, n, i, j * 192, (j + 1) * 192) \
                                    .rearrange("p (h d) -> p h d", d=HD)
                                dve.tensor_tensor(qs[s][:, t, :, 2 * HD:3 * HD], heads[:, 0:HEADS, :],
                                                  qs[s][:, t, :, 0:HD], ALU.subtract)
                                last = dve.tensor_tensor(ks[s][:, t, 0:KV, HD:2 * HD], heads[:, HEADS:HEADS + KV, :],
                                                         ks[s][:, t, 0:KV, 0:HD], ALU.subtract)
                            last.then_inc(read("qkv", s, n, i), 1)

                    def copy_out(step, s, n, i, dst):
                        wait_full(dve, step, s, n, i)
                        dve.tensor_copy(dst, cols(step, s, n, i, 0, TOK)).then_inc(read(step, s, n, i), 1)

                    def stack_t(s, n):
                        for j in range(1, 4, 2):
                            copy_out("stack_t", s, n, j, qT[s][:, j, :])
                        if n == 0:
                            copy_out("stack_t", s, n, 4, kT[s][:, 0, :])

                    def stack1_t(s, n):
                        for i in range(1, 8, 2):
                            copy_out("stack1_t", s, n, i, (qT if i < 4 else kT)[s][:, i % 4, :])

                    def row_max(s, n):
                        for t in range(NT):
                            for m in range(4):
                                u = 4 * t + m
                                g, j = 2 * (m // 2), 2 * (m % 2)
                                wait_full(dve, "row_max", s, n, u)
                                into = qs[s][:, t, :, USED:USED + 1].rearrange("p (j g) o -> p g j o", g=KV)
                                dve.tensor_reduce(into[:, g:g + 2, j:j + 2, :],
                                                  cols("row_max", s, n, u, 0, 2 * PSF)
                                                  .rearrange("p (g j k) -> p g j k", g=2, j=2),
                                                  AX.X, ALU.max, negate=True).then_inc(read("row_max", s, n, u), 1)

                    def window(s, n):
                        for b in range(NB):
                            wait_full(dve, "window", s, n, b)
                            ps = cols("window", s, n, b, 0, TS * HEADS * (HD + 1)) \
                                .rearrange("p (q e) -> p q e", e=HD + 1)
                            den = rden[s][:, b * TS:(b + 1) * TS, :].rearrange("p q h -> p (q h)")[:, :, None]
                            link(dve.reciprocal(den, ps[:, :, HD:HD + 1]))
                            settle()
                            dve.tensor_tensor(xh[s][:, b * TS:(b + 1) * TS, :].rearrange("p q (h d) -> p (q h) d", d=HD),
                                              ps[:, :, 0:HD], den.to_broadcast([P, TS * HEADS, HD]), ALU.mult) \
                                .then_inc(read("window", s, n, b), 1)

                    def resonance(s, n):
                        for b in range(NB):
                            wait_full(dve, "resonance", s, n, b)
                            for q in range(TS):
                                t = b * TS + q
                                last = dve.tensor_tensor(
                                    xh[s][:, t, :].rearrange("p (h d) -> p h d", d=HD),
                                    cols("resonance", s, n, b, q * C, (q + 1) * C).rearrange("p (h d) -> p h d", d=HD),
                                    gates[s][:, t, 0:HEADS, None].to_broadcast([P, HEADS, HD]), ALU.mult)
                            last.then_inc(read("resonance", s, n, b), 1)

                    def gate_up(s, n):
                        for c in range(FC):
                            wait_full(dve, "gate_up", s, n, 2 * c)
                            dve.wait_ge(tanh_gate[s], FC * n + c + 1)
                            dve.scalar_tensor_tensor(out=gg[s][:, c, :], in0=gt[s], scalar=1.0,
                                                     in1=cols("gate_up", s, n, 2 * c, 0, TOK),
                                                     op0=ALU.add, op1=ALU.mult) \
                                .then_inc(read("gate_up", s, n, 2 * c), 1)
                            wait_read(dve, "gate_up", s, n, 2 * c)
                            wait_full(dve, "gate_up", s, n, 2 * c + 1)
                            dve.tensor_tensor(gh[s][:, c, :], gg[s][:, c, :], cols("gate_up", s, n, 2 * c + 1, 0, TOK),
                                              ALU.mult).then_inc(read("gate_up", s, n, 2 * c + 1), 1)

                    def norm_t2(s, n):
                        wait_full(dve, "norm_t2", s, n, 1)
                        dve.tensor_scalar(xhT[s], cols("norm_t2", s, n, 1, 0, TOK), W["gamma"][:, 0:1],
                                          W["beta"][:, 0:1], ALU.mult, ALU.add).then_inc(read("norm_t2", s, n, 1), 1)

                    def heads_of(ap):
                        return ap.rearrange("p t (h d) -> p (t h) d", d=HD)

                    def per_head(ap):
                        return ap.rearrange("p t h -> p (t h)")[:, :, None]

                    def qkv1(s, n):
                        for i in range(NT // 2):
                            wait_read(dve, "qkv1", s, n, i)
                            link(dve.tensor_reduce(per_head(ss[s][:, 2 * i:2 * i + 2, :]),
                                                   heads_of(qk2[s][:, 2 * i:2 * i + 2, :]), AX.X, ALU.add))
                        settle()
                        dve.tensor_scalar(ss[s][:, :, :], ss[s][:, :, :], NORM_FLOOR, None, ALU.max) \
                            .then_inc(squares_ready[s], 1)

                    def unit(s, n):
                        dve.wait_ge(inv_ready[s], 1)
                        for t in range(NT):
                            a = qk[s][:, t, :].rearrange("p (h d) -> p h d", d=HD)
                            dve.tensor_tensor(a, a, inv[s][:, t, :, None].to_broadcast([P, 2 * HEADS, HD]), ALU.mult) \
                                .then_inc(unit_qk[s], 1)
                        dve.wait_ge(unit_qk[s], NT)
                        link(dve.tensor_tensor(qk2[s], qk[s], W["g_qk"][:, None, :].to_broadcast([P, NT, 2 * C]),
                                               ALU.mult))
                        settle()
                        dve.tensor_reduce(per_head(ss[s][:, :, :]), heads_of(qk2[s]), AX.X, ALU.add) \
                            .then_inc(gate_arg[s], 1)

                    def split1(s, n):
                        for t in range(NT):
                            dve.wait_ge(q_high[s], NT + t + 1)
                            u = qk[s][:, t, :].rearrange("p (m h d) -> p m h d", m=2, d=HD)
                            dve.tensor_tensor(qs[s][:, t, :, 2 * HD:3 * HD], u[:, 0, :, :], qs[s][:, t, :, 0:HD],
                                              ALU.subtract)
                            dve.tensor_tensor(ks[s][:, t, :, HD:2 * HD], u[:, 1, :, :], ks[s][:, t, :, 0:HD],
                                              ALU.subtract).then_inc(q_stacked[s], 1)
                        dve.wait_ge(gate_tanh[s], 1)
                        link(dve.tensor_scalar(gates[s][:, :, 0:HEADS], gates[s][:, :, 0:HEADS], 0.1875, 0.3125,
                                               ALU.mult, ALU.add))
                        link(dve.tensor_scalar(gates[s][:, :, HEADS:], gates[s][:, :, HEADS:], 0.375, 0.625,
                                               ALU.mult, ALU.add))
                        settle()
                        wait_full(dve, "qkv1", s, n, 2)
                        for t in range(NT):
                            last = dve.tensor_tensor(
                                v1[s][:, t, :].rearrange("p (h d) -> p h d", d=HD),
                                cols("qkv1", s, n, 2, t * C, (t + 1) * C).rearrange("p (h d) -> p h d", d=HD),
                                gates[s][:, t, HEADS:, None].to_broadcast([P, HEADS, HD]), ALU.mult)
                        last.then_inc(read("qkv1", s, n, 2), 1)

                    todo = {
                        "stats": stats_of_x, "norm": norm, "restats": restats, "renorm": renorm,
                        "router1": lambda s, n: router("router1", s, n, h1[s], "rb1"),
                        "router2": lambda s, n: router("router2", s, n, h2[s], "rb2"),
                        "logits": logits, "choose": choose, "prefix": prefix, "dispatch": dispatch,
                        "experts": experts, "combine": lambda s, n: add_to_x("combine", s, n, 0.5),
                        "qkv": qkv, "stack_t": stack_t, "row_max": row_max, "window": window,
                        "project": lambda s, n: add_to_x("project", s, n, 1.0), "gate_up": gate_up,
                        "down": lambda s, n: add_to_x("down", s, n, 0.25),
                        "norm_t2": norm_t2, "qkv1": qkv1, "unit": unit, "split1": split1, "stack1_t": stack1_t,
                        "resonance": resonance, "project1": lambda s, n: add_to_x("project1", s, n, 1.0),
                    }
                    dve.wait_ge(weights_in, 16 * len(w))
                    dve.wait_ge(consts_done, CONSTS)
                    for step, s, n in STEPS:
                        if step in todo:
                            todo[step](s, n)

            numbers = sorted(one.num for one in round_sems)
            assert numbers == list(range(numbers[0], numbers[-1] + 1))
            nc.gpsimd.sem_clear(range(numbers[0], numbers[-1] + 1))
            nc.all_engine_barrier()


def lay_out(inputs):
    import numpy as np

    g = {k: np.asarray(v) for k, v in inputs.items()}

    def rows(a, shape):
        return np.broadcast_to(a, shape)

    def chunks(a):
        return a.reshape(-1, P, a.shape[-1]).transpose(1, 0, 2)

    wq = g["L0_attn_Wq"].reshape(KV, GQ, HD, C).transpose(1, 0, 2, 3).reshape(HEADS * HD, C)
    out = {
        "rW1": g["L0_ffn_rW1"],
        "rb1": g["L0_ffn_rb1"].reshape(HC, P).T,
        "rb2": g["L0_ffn_rb2"].reshape(HC, P).T,
        "rW2": chunks(g["L0_ffn_rW2"]),
        "rW3": chunks(g["L0_ffn_rW3"]),
        "rb3": rows(g["L0_ffn_rb3"], (P, E)),
        "eb1": g["L0_ffn_eb1"].reshape(E, HC, P).transpose(2, 0, 1),
        "eb2": g["L0_ffn_eb2"].T,
        "w_gate": g["L1_ffn_w_gate"].T,
        "w_up": g["L1_ffn_w_up"].T,
        "w_down": chunks(g["L1_ffn_w_down"].T),
        "eW1": g["L0_ffn_eW1"].transpose(1, 0, 2),
        "eW2": g["L0_ffn_eW2"].reshape(E, HC, P, C).transpose(2, 0, 1, 3),
        "qkv0": np.concatenate([wq, g["L0_attn_Wk"], g["L0_attn_Wv"]]).T,
        "wo0": g["L0_attn_Wo"].T,
        "qk1": np.concatenate([g["L1_attn_w_q"], g["L1_attn_w_k"]], 1),
        "v1": g["L1_attn_w_v"],
        "wo1": g["L1_attn_w_o"],
        "bo1": rows(g["L1_attn_b_o"], (P, C)),
        "gamma": g["L1_attn_gamma"].reshape(C, 1),
        "beta": g["L1_attn_beta"].reshape(C, 1),
        "g_qk": rows(np.concatenate([np.tile(g["L1_attn_g_q"], HEADS), np.tile(g["L1_attn_g_k"], HEADS)]),
                     (P, 2 * C)),
    }
    return {k: np.ascontiguousarray(v) for k, v in out.items()}


def kernel(**inputs):
    import numpy as np
    from concourse import bacc
    from concourse.bass_utils import run_bass_kernel_spmd

    x = np.ascontiguousarray(np.asarray(inputs["L0_attn_x"]))
    arrays = {"x": x, **{f"w_{k}": v for k, v in lay_out(inputs).items()}}
    nc = bacc.Bacc("TRN2", target_bir_lowering=False, num_devices=1)
    dram = {k: nc.dram_tensor(f"{k}_dram", v.shape, mybir.dt.from_np(v.dtype), kind="ExternalInput").ap()
            for k, v in arrays.items()}
    out = nc.dram_tensor("out_dram", x.shape, F32, kind="ExternalOutput").ap()
    macaron_kernel(nc, dram["x"], {k[2:]: ap for k, ap in dram.items() if k != "x"}, out)
    r = run_bass_kernel_spmd(nc, [{f"{k}_dram": v for k, v in arrays.items()}], core_ids=[0])
    return r.results[0]["out_dram"]
```

```python
from contextlib import ExitStack

import concourse.bass as bass
from concourse import mybir

ALU = mybir.AluOpType
ACT = mybir.ActivationFunctionType
AX = mybir.AxisListType
F32 = mybir.dt.float32
F32R = mybir.dt.float32r
BF16 = mybir.dt.bfloat16
I32 = mybir.dt.int32
U32 = mybir.dt.uint32

P = 128
C = 128
SEQ = 256
TS = SEQ // P
NB = 2
NT = NB * TS
TOK = NT * P
STREAMS = 2
PSF = 512

RH = 512
HC = RH // P
E = 8
CAP = SEQ * 5 // 4 // E
SLOTS = E * CAP
CHUNKS = [(c, min(P, SLOTS - c)) for c in range(0, SLOTS, P)]
NSB = STREAMS * NB
SLOT4 = NSB * CAP
EG = 2

HEADS = 16
HD = 8
KV = 4
GQ = HEADS // KV
PART = 32
USED = 3 * HD
FH = 384
FC = FH // P

LN_EPS = 1e-5
NORM_FLOOR = 1e-24
GUESS = float(0x5F3759DF)
MASKED = -1e30
SHARP = 15.0
THRESHOLD = 0.27
DEQUANT = 1.0 / 127.0

RING = 6
P_RING = 3
UNITS = NB * 8
CTX = NB * 2
SKEW = 2
CONSTS = 16 + 2 * STREAMS

MOE = ["stats", "norm", "norm_t", "router1", "router2", "logits", "choose", "prefix", "dispatch", "experts", "slots",
       "combine"]
WINDOW = ["stats", "norm", "norm_t", "qkv", "stack_t", "row_max", "stack_t", "window", "context_t",
          "heads_t", "project"]
GATED = ["stats", "norm", "norm_t", "gate_up", "down"]
RESONANCE = ["stats", "norm", "restats", "renorm", "norm_t2", "qkv1", "unit", "split1", "stack1_t", "resonance",
             "context1_t", "heads_t", "project1"]
ROUND_STEPS = MOE + WINDOW + MOE + GATED + RESONANCE + GATED


def psum_uses(step, n):
    return {
        "norm_t": [1], "router1": [1] * HC, "router2": [1] * HC, "logits": [1], "prefix": [1],
        "dispatch": [1] * (NB + len(CHUNKS)), "experts": ["a"] * (E // EG) + [2] * E, "slots": [1] * NB,
        "combine": [1], "qkv": [1] * (NT // 2), "stack_t": [1] * (5 - n), "row_max": [2] * (NT * 4),
        "window": ["a"] * CTX + [2] * UNITS, "context_t": [1] * CTX, "heads_t": [1], "project": [1], "gate_up": [1] * (2 * FC), "down": [1],
        "norm_t2": [1, 1], "qkv1": [1] * (NT // 2 + 1), "stack1_t": [1] * 8,
        "resonance": ["a"] * CTX + [2] * UNITS, "context1_t": [1] * (CTX + 1), "project1": [1],
    }.get(step, [])


def schedule():
    seen, out = {}, []
    for step in ROUND_STEPS:
        for s in range(1 if step == "experts" else STREAMS):
            n = seen.get((step, s), 0)
            seen[(step, s)] = n + 1
            out.append((step, s, n))
    return out


def bank_plan(steps):
    plan, count, last = {}, [0] * 8, [None] * 8
    at = held = 0
    for step, s, n in steps:
        for i, size in enumerate(psum_uses(step, n)):
            if size == "a":
                b, width = RING + held, 1
                held = (held + 1) % 2
            else:
                width = size
                at += at % width
                b = at % RING
                at += width
            before = {last[k] for k in range(b, b + width)} - {None}
            count[b] += 1
            for k in range(b, b + width):
                last[k] = (b, count[b])
            plan[(step, s, n, i)] = (b, count[b], sorted(before))
    return plan


def macaron_kernel(nc, x_in, w, out):
    B = x_in.shape[0]
    ROUNDS = B // (NB * STREAMS)
    STEPS = schedule()
    PLAN = bank_plan(STEPS)
    unit_base = {}
    for step, s, n in STEPS:
        if step in ("window", "resonance"):
            unit_base[(step, s, n)] = UNITS * len(unit_base)

    ctx = ExitStack()
    with ctx:
        def sb(name, shape, dt=F32):
            return ctx.enter_context(nc.sbuf_tensor(name, shape, dt))

        round_sems = []

        def sem(name):
            one = ctx.enter_context(nc.semaphore(name))
            round_sems.append(one)
            return one

        def per_stream(name):
            return [sem(f"{name}{s}") for s in range(STREAMS)]

        W = {name: sb(f"w_{name}", list(ap.shape), ap.dtype) for name, ap in w.items() if ap.dtype != I32}
        gate_f = sb("gate_f", [P, FH])
        up_f = sb("up_f", [P, FH])
        down_f = sb("down_f", [P, FC, C])
        ident = sb("ident", [P, P])
        ident_b = sb("ident_b", [P, P], BF16)
        ones = sb("ones", [P, P])
        ones_b = sb("ones_b", [P, P], BF16)
        earlier = sb("earlier", [P, P], BF16)
        slot_no = sb("slot_no", [P, CAP])
        expert_no = sb("expert_no", [P, E])
        far_low = sb("far_low", [P, P], BF16)
        far_high = sb("far_high", [P, P], BF16)
        minus_half = sb("minus_half", [P, NT])
        tanh_bias = sb("tanh_bias", [P, 1])

        def both(name, shape, dt=F32):
            return [sb(f"{name}{s}", shape, dt) for s in range(STREAMS)]

        x = both("x", [P, NT, C])
        stats = both("stats", [P, NT, 6])
        mean_var = both("mean_var", [P, NT, 2])
        var_eps = both("var_eps", [P, NT])
        rstd = both("rstd", [P, NT])
        xn = both("xn", [P, NT, C])
        xnT = both("xnT", [P, TOK])
        big = both("big", [P, 2 * HC * TOK])
        hid_all = sb("hid", [P, STREAMS, HC * E * NB * CAP])
        hid = [hid_all[:, s, :] for s in range(STREAMS)]
        small = both("small", [P, 8, NT, E])
        top = both("top", [P, NT, 8])
        top_at = both("top_at", [P, NT, 8], U32)
        chosen = both("chosen", [P, NT, E], BF16)
        shareT = both("shareT", [P, len(CHUNKS), TOK])
        slotT = sb("slotT", [P, E, NSB, CAP])
        hraw = sb("hraw", [P, 2, HC, SLOT4])
        eoT = sb("eoT", [P, NSB, E, CAP])
        eo_flat = eoT[:, :, :, :].rearrange("p b e c -> p (b e c)")
        xh = [eo_flat[:, s * TOK:(s + 1) * TOK].rearrange("p (t c) -> p t c", t=NT) for s in range(STREAMS)]
        eo = both("eo", [P, NB, len(CHUNKS), C])
        v0 = both("v0", [P, NT, KV + 1, 2 * HD])
        ss = both("ss", [P, NT, 2 * HEADS])
        inv = both("inv", [P, NT, 2 * HEADS])
        gates = both("gates", [P, NT, 2 * HEADS])
        rden = both("rden", [P, CTX, 4, KV])
        vsum = both("vsum", [P, NB, C])
        newton = both("newton", [P, NT * 2 * HEADS])
        probs = sb("probs", [P, P_RING, 2 * PSF])

        h1 = [big[s][:, 0:HC * TOK].rearrange("p (c t) -> p c t", c=HC) for s in range(STREAMS)]
        h2 = [big[s][:, HC * TOK:2 * HC * TOK].rearrange("p (c t) -> p c t", c=HC) for s in range(STREAMS)]
        qT = [sb(f"qT{s}", [P, 4, TOK], F32R) for s in range(STREAMS)]
        kT = [sb(f"kT{s}", [P, 4, TOK], F32R) for s in range(STREAMS)]
        place = [hid[s][:, 0:NT * SLOTS].rearrange("p (t c) -> p t c", t=NT) for s in range(STREAMS)]
        share = [hid[s][:, NT * SLOTS:2 * NT * SLOTS].rearrange("p (t c) -> p t c", t=NT) for s in range(STREAMS)]
        xhT = [shareT[s][:, 0, :] for s in range(STREAMS)]
        v1 = [eo[s][:, :, :, :].rearrange("p b i c -> p (b i c)")[:, 0:NT * C].rearrange("p (t c) -> p t c", t=NT)
              for s in range(STREAMS)]
        hh = hid_all[:, :, :].rearrange("p s n -> p (s n)").rearrange("p (e c n) -> p e c n", e=E, c=HC)
        ctxT = [big[s][:, 0:CTX * PSF].rearrange("p (u n) -> p u n", u=CTX) for s in range(STREAMS)]
        qs = [big[s][:, 0:NT * HEADS * PART].rearrange("p (t h r) -> p t h r", t=NT, h=HEADS) for s in range(STREAMS)]
        ks = [big[s][:, NT * HEADS * PART:2 * NT * HEADS * PART].rearrange("p (t h r) -> p t h r", t=NT, h=HEADS)
              for s in range(STREAMS)]
        qk = [hid[s][:, 0:NT * 2 * C].rearrange("p (t n) -> p t n", t=NT) for s in range(STREAMS)]
        qk2 = [hid[s][:, NT * 2 * C:2 * NT * 2 * C].rearrange("p (t n) -> p t n", t=NT) for s in range(STREAMS)]
        gt = [hid[s][:, 0:TOK] for s in range(STREAMS)]
        gg = [hid[s][:, TOK:(1 + FC) * TOK].rearrange("p (c t) -> p c t", c=FC) for s in range(STREAMS)]
        gh = [big[s][:, 0:FC * TOK].rearrange("p (c t) -> p c t", c=FC) for s in range(STREAMS)]

        at = 0
        for name, ap in w.items():
            if ap.dtype == I32:
                n = ap.shape[1] if len(ap.shape) == 2 else ap.shape[1] * ap.shape[2]
                W[name] = big[0][:, at:at + n].bitcast(I32)
                if len(ap.shape) == 3:
                    W[name] = W[name].rearrange("p (c n) -> p c n", c=ap.shape[1])
                at += n

        psum = ctx.enter_context(nc.psum_tensor("psum", [P, 8, PSF], F32))

        weights_in = ctx.enter_context(nc.semaphore("weights_in"))
        consts_done = ctx.enter_context(nc.semaphore("consts_done"))
        dequant_done = ctx.enter_context(nc.semaphore("dequant_done"))
        first = len(round_sems)
        bank_full = [sem(f"bank_full{b}") for b in range(8)]
        bank_read = [sem(f"bank_read{b}") for b in range(8)]
        probs_used = sem("probs_used")
        x_in_done = per_stream("x_in_done")
        x_out_done = per_stream("x_out_done")
        dve_link = sem("dve_link")
        var_ready = per_stream("var_ready")
        rstd_ready = per_stream("rstd_ready")
        xn_ready = per_stream("xn_ready")
        logit_shifted = per_stream("logit_shifted")
        logit_exp = per_stream("logit_exp")
        chosen_ready = per_stream("chosen_ready")
        place_ready = per_stream("place_ready")
        share_ready = per_stream("share_ready")
        hh_ready = sem("hh_ready")
        k_ones = per_stream("k_ones")
        q_high = per_stream("q_high")
        q_stacked = per_stream("q_stacked")
        tanh_gate = per_stream("tanh_gate")
        unit_qk = per_stream("unit_qk")
        gate_arg = per_stream("gate_arg")
        gated_heads = per_stream("gated_heads")
        gate_tanh = per_stream("gate_tanh")

        def bank(step, s, n, i):
            return PLAN[(step, s, n, i)][0]

        def cols(step, s, n, i, lo, hi):
            b = bank(step, s, n, i)
            if hi <= PSF:
                return psum[:, b, lo:hi]
            return psum[:, b:b + 2, :].rearrange("p a n -> p (a n)")[:, lo:hi]

        def wait_full(eng, step, s, n, i):
            b, k, _ = PLAN[(step, s, n, i)]
            eng.wait_ge(bank_full[b], k)

        def wait_free(eng, step, s, n, i):
            for b, k in PLAN[(step, s, n, i)][2]:
                eng.wait_ge(bank_read[b], k)

        def full(step, s, n, i):
            return bank_full[bank(step, s, n, i)]

        def read(step, s, n, i):
            return bank_read[bank(step, s, n, i)]

        def wait_read(eng, step, s, n, i):
            b, k, _ = PLAN[(step, s, n, i)]
            eng.wait_ge(bank_read[b], k)

        def wait_probs_used(eng, unit):
            step, s, n = next(key for key, base in unit_base.items() if base <= unit < base + UNITS)
            u = unit - unit_base[(step, s, n)]
            if u % 4 == 3:
                wait_full(eng, step, s, n, u // 4)
            else:
                eng.wait_ge(probs_used, unit + 1 - (unit + 1) // 4)

        with nc.Block() as block:
            @block.sync
            def _(sp):
                for name, ap in w.items():
                    sp.dma_start(W[name][...], ap).then_inc(weights_in, 16)

            @block.gpsimd
            def _(pool):
                done = [0]

                def const(ins):
                    done[0] += 1
                    ins.then_inc(consts_done, 1)

                def chained(ins):
                    const(ins)
                    pool.wait_ge(consts_done, done[0])

                const(pool.memset(ones[:, :], 1.0))
                const(pool.memset(ones_b[:, :], 1.0))
                const(pool.memset(minus_half[:, :], -0.5))
                const(pool.memset(tanh_bias[:, :], -SHARP * THRESHOLD))
                for m in (ident, ident_b, far_low, far_high):
                    const(pool.memset(m[:, :], 0.0))
                chained(pool.memset(earlier[:, :], 1.0))
                for m in (ident, ident_b):
                    const(pool.affine_select(out=m[:, :], in_=m[:, :], compare_op=ALU.not_equal, fill=1.0,
                                             base=0, pattern=[[-1, P]], channel_multiplier=1))
                const(pool.affine_select(out=earlier[:, :], in_=earlier[:, :], compare_op=ALU.is_gt, fill=0.0,
                                         base=0, pattern=[[1, P]], channel_multiplier=-1))
                const(pool.affine_select(out=far_low[:, :], in_=far_low[:, :], compare_op=ALU.is_ge, fill=MASKED,
                                         base=0, pattern=[[-1, P]], channel_multiplier=1))
                const(pool.affine_select(out=far_high[:, :], in_=far_high[:, :], compare_op=ALU.is_ge, fill=MASKED,
                                         base=0, pattern=[[1, P]], channel_multiplier=-1))
                const(pool.iota(slot_no[:, :], pattern=[[1, CAP]], base=1, channel_multiplier=0,
                                allow_small_or_imprecise_dtypes=True))
                const(pool.iota(expert_no[:, :], pattern=[[1, E]], base=0, channel_multiplier=0,
                                allow_small_or_imprecise_dtypes=True))
                for s in range(STREAMS):
                    chained(pool.memset(v0[s][:, :, :, :], 0.0))
                    const(pool.memset(v0[s][:, :, :, HD:HD + 1], 1.0))

            @block.vector
            def _(dve):
                dve.wait_ge(weights_in, 16 * len(w))
                for a, b in ((gate_f, "w_gate"), (up_f, "w_up"), (down_f, "w_down")):
                    dve.tensor_scalar(a[...], W[b][...], DEQUANT, None, ALU.mult).then_inc(dequant_done, 1)

        with nc.Fori(0, ROUNDS) as rnd:
            with nc.Block() as block:
                @block.sync
                def _(sp):
                    for s in range(STREAMS):
                        src = x_in[bass.ds(rnd * (NB * STREAMS) + s * NB, NB)].rearrange("b (k p) c -> p (b k) c", p=P)
                        sp.dma_start(x[s][:, :, :], src).then_inc(x_in_done[s], 16)
                    for s in range(STREAMS):
                        wait_read(sp, "down", s, 1, 0)
                        dst = out[bass.ds(rnd * (NB * STREAMS) + s * NB, NB)].rearrange("b (k p) c -> p (b k) c", p=P)
                        sp.dma_start(dst, x[s][:, :, :]).then_inc(x_out_done[s], 16)
                    for s in range(STREAMS):
                        sp.wait_ge(x_out_done[s], 16)

                @block.tensor
                def _(pe):
                    def transposes(step, s, n, i, src, tiles):
                        wait_free(pe, step, s, n, i)
                        for t in range(tiles):
                            last = pe.transpose(cols(step, s, n, i, t * P, (t + 1) * P), src(t), ident[:, :])
                        last.then_inc(full(step, s, n, i), 1)

                    def norm_t(s, n):
                        pe.wait_ge(xn_ready[s], [1, 2, 3, 4, 7][n])
                        transposes("norm_t", s, n, 0, lambda t: xn[s][:, t, :], NT)

                    def router1(s, n):
                        wait_read(pe, "norm_t", s, 2 * n, 0)
                        for c in range(HC):
                            wait_free(pe, "router1", s, n, c)
                            pe.matmul(cols("router1", s, n, c, 0, TOK), W["rW1"][:, c * P:(c + 1) * P], xnT[s][:, :],
                                      start=True, stop=True).then_inc(full("router1", s, n, c), 1)

                    def router2(s, n):
                        for c in range(HC):
                            wait_read(pe, "router1", s, n, c)
                        for c in range(HC):
                            wait_free(pe, "router2", s, n, c)
                            for k in range(HC):
                                last = pe.matmul(cols("router2", s, n, c, 0, TOK), W["rW2"][:, k, c * P:(c + 1) * P],
                                                 h1[s][:, k, :], start=(k == 0), stop=(k == HC - 1))
                            last.then_inc(full("router2", s, n, c), 1)

                    def logits(s, n):
                        for c in range(HC):
                            wait_read(pe, "router2", s, n, c)
                        wait_free(pe, "logits", s, n, 0)
                        for t in range(NT):
                            for k in range(HC):
                                last = pe.matmul(cols("logits", s, n, 0, t * E, (t + 1) * E),
                                                 h2[s][:, k, t * P:(t + 1) * P], W["rW3"][:, k, :],
                                                 start=(k == 0), stop=(k == HC - 1))
                        last.then_inc(full("logits", s, n, 0), 1)

                    def prefix(s, n):
                        pe.wait_ge(chosen_ready[s], n + 1)
                        wait_free(pe, "prefix", s, n, 0)
                        for t in range(NT):
                            o = cols("prefix", s, n, 0, t * E, (t + 1) * E)
                            first_tile = t % TS == 0
                            last = pe.matmul(o, earlier[:, :], chosen[s][:, t, :], start=True, stop=first_tile)
                            if not first_tile:
                                last = pe.matmul(o, ones_b[:, :], chosen[s][:, t - 1, :], start=False, stop=True)
                        last.then_inc(full("prefix", s, n, 0), 1)

                    def dispatch(s, n):
                        pe.wait_ge(place_ready[s], n + 1)
                        for b in range(NB):
                            wait_free(pe, "dispatch", s, n, b)
                            for k in range(TS):
                                t = b * TS + k
                                last = pe.matmul(cols("dispatch", s, n, b, 0, SLOTS), xn[s][:, t, :],
                                                 place[s][:, t, :], start=(k == 0), stop=(k == TS - 1))
                            last.then_inc(full("dispatch", s, n, b), 1)
                        pe.wait_ge(share_ready[s], n + 1)
                        for i, (c, m) in enumerate(CHUNKS):
                            u = NB + i
                            wait_free(pe, "dispatch", s, n, u)
                            for t in range(NT):
                                last = pe.transpose(cols("dispatch", s, n, u, t * P, (t + 1) * P)[0:m, :],
                                                    share[s][:, t, c:c + m], ident[:, :])
                            last.then_inc(full("dispatch", s, n, u), 1)

                    def experts(s, n):
                        for one in range(STREAMS):
                            for b in range(NB):
                                wait_read(pe, "dispatch", one, n, b)
                        for i in range(E + SKEW):
                            if i < E:
                                if i == 0:
                                    for one in range(STREAMS):
                                        for c in range(len(CHUNKS)):
                                            wait_read(pe, "dispatch", one, n, NB + c)
                                wait_free(pe, "experts", s, n, E // EG + i)
                                for c in range(HC):
                                    at = c // 2 * PSF + c % 2 * SLOT4
                                    last = pe.matmul(cols("experts", s, n, E // EG + i, at, at + SLOT4),
                                                     W["eW1"][:, i, c * P:(c + 1) * P],
                                                     slotT[:, i, :, :].rearrange("p b c -> p (b c)"),
                                                     start=True, stop=True)
                                last.then_inc(full("experts", s, n, E // EG + i), 1)
                            e = i - SKEW
                            if e < 0:
                                continue
                            if e % EG == 0:
                                wait_free(pe, "experts", s, n, e // EG)
                            pe.wait_ge(hh_ready, E * n + e + 1)
                            for c in range(HC):
                                last = pe.matmul(cols("experts", s, n, e // EG, e % EG * SLOT4, (e % EG + 1) * SLOT4),
                                                 W["eW2"][:, e, c, :], hh[:, e, c, :],
                                                 start=(c == 0), stop=(c == HC - 1))
                            if e % EG == EG - 1:
                                last.then_inc(full("experts", s, n, e // EG), 1)

                    def slots(s, n):
                        for i in range(E // EG):
                            wait_read(pe, "experts", 0, n, i)
                        for b in range(NB):
                            wait_free(pe, "slots", s, n, b)
                            flat = eoT[:, s * NB + b, :, :].rearrange("p e c -> p (e c)")
                            for i, (c, m) in enumerate(CHUNKS):
                                last = pe.transpose(cols("slots", s, n, b, i * P, (i + 1) * P)[0:m, :],
                                                    flat[:, c:c + m], ident[:, :])
                            last.then_inc(full("slots", s, n, b), 1)

                    def combine(s, n):
                        for b in range(NB):
                            wait_read(pe, "slots", s, n, b)
                        for i in range(len(CHUNKS)):
                            wait_read(pe, "dispatch", s, n, NB + i)
                        wait_free(pe, "combine", s, n, 0)
                        for t in range(NT):
                            for i, (c, m) in enumerate(CHUNKS):
                                last = pe.matmul(cols("combine", s, n, 0, t * C, (t + 1) * C),
                                                 shareT[s][0:m, i, t * P:(t + 1) * P], eo[s][0:m, t // TS, i, :],
                                                 start=(i == 0), stop=(i == len(CHUNKS) - 1))
                        last.then_inc(full("combine", s, n, 0), 1)

                    def qkv(s, n):
                        wait_read(pe, "norm_t", s, 1, 0)
                        for i in range(NT // 2):
                            wait_free(pe, "qkv", s, n, i)
                            for j in range(2):
                                t = 2 * i + j
                                last = pe.matmul(cols("qkv", s, n, i, j * 192, (j + 1) * 192),
                                                 xnT[s][:, t * P:(t + 1) * P], W["qkv0"][:, :], start=True, stop=True)
                            last.then_inc(full("qkv", s, n, i), 1)

                    def stack_t(s, n):
                        if n == 0:
                            for i in range(NT // 2):
                                wait_read(pe, "qkv", s, 0, i)
                            pe.wait_ge(k_ones[s], 1)
                        else:
                            for u in range(NT * 4):
                                wait_read(pe, "row_max", s, 0, u)
                        for j in range(4):
                            transposes("stack_t", s, n, j, lambda t: qs[s][:, t, 4 * j:4 * j + 4, :]
                                       .rearrange("p h r -> p (h r)"), NT)
                        if n == 0:
                            transposes("stack_t", s, n, 4, lambda t: ks[s][:, t, 0:4, :]
                                       .rearrange("p h r -> p (h r)"), NT)

                    def row_max(s, n):
                        for j in range(5):
                            wait_read(pe, "stack_t", s, 0, j)
                        for t in range(NT):
                            b, k = t // TS, t % TS
                            for m in range(4):
                                u = 4 * t + m
                                wait_free(pe, "row_max", s, n, u)
                                for gg_ in range(2):
                                    g = 2 * (m // 2) + gg_
                                    for jj in range(2):
                                        j = 2 * (m % 2) + jj
                                        o = cols("row_max", s, n, u, gg_ * PSF + jj * SEQ, gg_ * PSF + (jj + 1) * SEQ)
                                        pe.matmul(o, qT[s][g * PART:g * PART + USED, j, t * P:(t + 1) * P],
                                                  kT[s][g * PART:g * PART + USED, 0, b * SEQ:(b + 1) * SEQ],
                                                  start=(jj == 0), stop=False, skip_group_check=True)
                                for gg_ in range(2):
                                    o = cols("row_max", s, n, u, gg_ * PSF, (gg_ + 1) * PSF) \
                                        .rearrange("p (j k) -> p j k", j=2)[:, :, (1 - k) * P:(2 - k) * P]
                                    far = (far_low if k == 0 else far_high)[:, None, :].to_broadcast([P, 2, P])
                                    last = pe.matmul(o, ident_b[:, :], far, start=False, stop=True,
                                                     skip_group_check=True)
                                last.then_inc(full("row_max", s, n, u), 1)

                    def window(s, n):
                        for j in range(4):
                            wait_read(pe, "stack_t", s, 1, j)
                        base = unit_base[("window", s, n)]
                        for i in range(UNITS + SKEW):
                            if i < UNITS:
                                b, jp, g = i // 8, i // 4 % 2, i % 4
                                wait_free(pe, "window", s, n, CTX + i)
                                for k in range(TS):
                                    o = cols("window", s, n, CTX + i, k * PSF, (k + 1) * PSF)
                                    rows = slice(g * PART, g * PART + USED + 1)
                                    pe.matmul(o, kT[s][rows, 0, b * SEQ + k * P:b * SEQ + (k + 1) * P],
                                              qT[s][rows, 2 * jp:2 * jp + 2, b * SEQ:(b + 1) * SEQ],
                                              start=True, stop=False, skip_group_check=True)
                                for k in range(TS):
                                    o = cols("window", s, n, CTX + i, k * PSF, (k + 1) * PSF) \
                                        .rearrange("p (j q) -> p j q", j=2)[:, :, (1 - k) * P:(2 - k) * P]
                                    far = (far_low if k == 0 else far_high)[:, None, :].to_broadcast([P, 2, P])
                                    last = pe.matmul(o, ident_b[:, :], far, start=False, stop=True,
                                                     skip_group_check=True)
                                last.then_inc(full("window", s, n, CTX + i), 1)
                            u = i - SKEW
                            if u < 0:
                                continue
                            b, jp, g = u // 8, u // 4 % 2, u % 4
                            if g == 0:
                                wait_free(pe, "window", s, n, u // 4)
                            wait_read(pe, "window", s, n, CTX + u)
                            pr = probs[:, (base + u) % P_RING, :].rearrange("p (k n) -> p k n", k=TS)
                            for k in range(TS):
                                vv = v0[s][:, b * TS + k, g:g + 2, :].rearrange("p g d -> p (g d)")
                                last = pe.matmul(cols("window", s, n, u // 4, 0, PSF)[g * PART:(g + 1) * PART, :],
                                                 vv, pr[:, k, :], start=(k == 0), stop=(k == TS - 1))
                            last.then_inc(full("window", s, n, u // 4) if g == 3 else probs_used, 1)

                    def context_t(s, n, step="context_t", source="window"):
                        for i in range(CTX):
                            wait_read(pe, source, s, n, i)
                            transposes(step, s, n, i, lambda t: ctxT[s][:, i, t * P:(t + 1) * P], 4)

                    def context1_t(s, n):
                        wait_free(pe, "context1_t", s, n, CTX)
                        for b in range(NB):
                            for k in range(TS):
                                last = pe.matmul(cols("context1_t", s, n, CTX, b * C, (b + 1) * C), ones[:, :],
                                                 v1[s][:, b * TS + k, :], start=(k == 0), stop=(k == TS - 1))
                        last.then_inc(full("context1_t", s, n, CTX), 1)
                        context_t(s, n, "context1_t", "resonance")

                    def heads_t(s, n):
                        if n == 0:
                            for i in range(CTX):
                                wait_read(pe, "context_t", s, 0, i)
                        else:
                            pe.wait_ge(gated_heads[s], 1)
                        transposes("heads_t", s, n, 0, lambda t: xh[s][:, t, :], NT)

                    def project(s, n, step="project", wname="wo0", k=0):
                        wait_read(pe, "heads_t", s, k, 0)
                        wait_free(pe, step, s, n, 0)
                        for t in range(NT):
                            last = pe.matmul(cols(step, s, n, 0, t * C, (t + 1) * C), xhT[s][:, t * P:(t + 1) * P],
                                             W[wname][:, :], start=True, stop=True)
                        last.then_inc(full(step, s, n, 0), 1)

                    def gate_up(s, n):
                        wait_read(pe, "norm_t", s, 3 + n, 0)
                        for c in range(FC):
                            for i, wt in enumerate((gate_f, up_f)):
                                wait_free(pe, "gate_up", s, n, 2 * c + i)
                                pe.matmul(cols("gate_up", s, n, 2 * c + i, 0, TOK), wt[:, c * P:(c + 1) * P],
                                          xnT[s][:, :], start=True, stop=True) \
                                    .then_inc(full("gate_up", s, n, 2 * c + i), 1)

                    def down(s, n):
                        for c in range(FC):
                            wait_read(pe, "gate_up", s, n, 2 * c + 1)
                        wait_free(pe, "down", s, n, 0)
                        for t in range(NT):
                            for c in range(FC):
                                last = pe.matmul(cols("down", s, n, 0, t * C, (t + 1) * C),
                                                 gh[s][:, c, t * P:(t + 1) * P], down_f[:, c, :],
                                                 start=(c == 0), stop=(c == FC - 1))
                        last.then_inc(full("down", s, n, 0), 1)

                    def norm_t2(s, n):
                        pe.wait_ge(xn_ready[s], 5)
                        transposes("norm_t2", s, n, 0, lambda t: xn[s][:, t, :], NT)
                        pe.wait_ge(xn_ready[s], 6)
                        transposes("norm_t2", s, n, 1, lambda t: xh[s][:, t, :], NT)

                    def qkv1(s, n):
                        wait_read(pe, "norm_t2", s, 0, 0)
                        wait_read(pe, "norm_t2", s, 0, 1)
                        for i in range(NT // 2):
                            wait_free(pe, "qkv1", s, n, i)
                            for j in range(2):
                                t = 2 * i + j
                                last = pe.matmul(cols("qkv1", s, n, i, j * 2 * C, (j + 1) * 2 * C),
                                                 xhT[s][:, t * P:(t + 1) * P], W["qk1"][:, :], start=True, stop=True)
                            last.then_inc(full("qkv1", s, n, i), 1)
                        i = NT // 2
                        wait_free(pe, "qkv1", s, n, i)
                        for t in range(NT):
                            last = pe.matmul(cols("qkv1", s, n, i, t * C, (t + 1) * C), xnT[s][:, t * P:(t + 1) * P],
                                             W["v1"][:, :], start=True, stop=True)
                        last.then_inc(full("qkv1", s, n, i), 1)

                    def stack1_t(s, n):
                        pe.wait_ge(q_stacked[s], NT)
                        for m, src in enumerate((qs, ks)):
                            for j in range(4):
                                transposes("stack1_t", s, n, 4 * m + j, lambda t: src[s][:, t, 4 * j:4 * j + 4, :]
                                           .rearrange("p h r -> p (h r)"), NT)

                    def resonance(s, n):
                        for i in range(8):
                            wait_read(pe, "stack1_t", s, n, i)
                        wait_read(pe, "qkv1", s, n, 2)
                        base = unit_base[("resonance", s, n)]
                        for i in range(UNITS + SKEW):
                            if i < UNITS:
                                b, m, r = i // 8, i // 4 % 2, i % 4
                                wait_free(pe, "resonance", s, n, CTX + i)
                                rows = slice(r * PART, r * PART + USED)
                                for k in range(TS):
                                    for jj in range(2):
                                        o = cols("resonance", s, n, CTX + i, k * PSF + jj * SEQ, k * PSF + (jj + 1) * SEQ)
                                        blk = 2 * m + jj
                                        last = pe.matmul(o, kT[s][rows, blk, b * SEQ + k * P:b * SEQ + (k + 1) * P],
                                                         qT[s][rows, blk, b * SEQ:(b + 1) * SEQ],
                                                         start=True, stop=True)
                                last.then_inc(full("resonance", s, n, CTX + i), 1)
                            u = i - SKEW
                            if u < 0:
                                continue
                            b, m, r = u // 8, u // 4 % 2, u % 4
                            if r == 0:
                                wait_free(pe, "resonance", s, n, u // 4)
                            wait_read(pe, "resonance", s, n, CTX + u)
                            pr = probs[:, (base + u) % P_RING, :].rearrange("p (k j q) -> p k j q", k=TS, j=2)
                            for jj in range(2):
                                o = cols("resonance", s, n, u // 4, jj * SEQ, (jj + 1) * SEQ)
                                for k in range(TS):
                                    vv = v1[s][:, b * TS + k, (2 * m + jj) * PART:(2 * m + jj + 1) * PART]
                                    last = pe.matmul(o[r * PART:(r + 1) * PART, :], vv, pr[:, k, jj, :],
                                                     start=(k == 0), stop=(k == TS - 1))
                            last.then_inc(full("resonance", s, n, u // 4) if r == 3 else probs_used, 1)

                    pe.wait_ge(weights_in, 16 * len(w))
                    pe.wait_ge(consts_done, CONSTS)
                    pe.wait_ge(dequant_done, 3)
                    todo = {"norm_t": norm_t, "router1": router1, "router2": router2, "logits": logits,
                            "prefix": prefix, "dispatch": dispatch, "experts": experts, "slots": slots,
                            "combine": combine, "qkv": qkv, "stack_t": stack_t, "row_max": row_max,
                            "window": window, "heads_t": heads_t, "project": project, "gate_up": gate_up,
                            "down": down, "norm_t2": norm_t2, "qkv1": qkv1, "stack1_t": stack1_t,
                            "resonance": resonance, "context_t": context_t, "context1_t": context1_t,
                            "project1": lambda s, n: project(s, n, "project1", "wo1", 1)}
                    for step, s, n in STEPS:
                        if step in todo:
                            todo[step](s, n)

                @block.scalar
                def _(act):
                    def copy_out(step, s, n, i, dst, lo, hi):
                        wait_full(act, step, s, n, i)
                        act.activation(dst, cols(step, s, n, i, lo, hi), ACT.Copy).then_inc(read(step, s, n, i), 1)

                    def router(step, s, n, dst, bias):
                        for c in range(0, HC, 2):
                            wait_full(act, step, s, n, c)
                            act.activation(dst[:, c, :], cols(step, s, n, c, 0, TOK), ACT.Relu,
                                           bias=W[bias][:, c:c + 1]).then_inc(read(step, s, n, c), 1)

                    def choose(s, n):
                        act.wait_ge(logit_shifted[s], n + 1)
                        act.activation(small[s][:, 1, :, :], small[s][:, 0, :, :], ACT.Exp).then_inc(logit_exp[s], 1)

                    def dispatch(s, n):
                        for b in range(NB):
                            wait_full(act, "dispatch", s, n, b)
                            act.activation(slotT[:, :, s * NB + b, :],
                                           cols("dispatch", s, n, b, 0, SLOTS).rearrange("p (e c) -> p e c", e=E),
                                           ACT.Copy).then_inc(read("dispatch", s, n, b), 1)

                    def slots(s, n):
                        whole = SLOTS // P
                        m = CHUNKS[-1][1]
                        for b in range(NB):
                            wait_full(act, "slots", s, n, b)
                            act.activation(eo[s][:, b, 0:whole, :], cols("slots", s, n, b, 0, whole * P)
                                           .rearrange("p (i c) -> p i c", c=C), ACT.Copy)
                            act.activation(eo[s][0:m, b, whole, :],
                                           cols("slots", s, n, b, whole * P, (whole + 1) * P)[0:m, :],
                                           ACT.Copy).then_inc(read("slots", s, n, b), 1)

                    def high_parts(s, t, heads_q, heads_k):
                        nk = heads_k.shape[1]
                        act.activation(qs[s][:, t, :, 0:2 * HD].bitcast(F32R).rearrange("p h (c d) -> p h c d", c=2),
                                       heads_q[:, :, None, :].to_broadcast([P, HEADS, 2, HD]), ACT.Copy)
                        for c in (0, 2):
                            last = act.activation(ks[s][:, t, 0:nk, c * HD:(c + 1) * HD].bitcast(F32R), heads_k, ACT.Copy)
                        last.then_inc(q_high[s], 1)

                    def qkv(s, n):
                        for i in range(NT // 2):
                            wait_full(act, "qkv", s, n, i)
                            for j in range(2):
                                ps = cols("qkv", s, n, i, j * 192, (j + 1) * 192)
                                heads = ps.rearrange("p (h d) -> p h d", d=HD)
                                act.activation(v0[s][:, 2 * i + j, 0:KV, 0:HD], heads[:, HEADS + KV:, :], ACT.Copy)
                                high_parts(s, 2 * i + j, heads[:, 0:HEADS, :], heads[:, HEADS:HEADS + KV, :])

                    def attend(step, s, n, func, scale, bias):
                        base = unit_base[(step, s, n)]
                        for i in range(UNITS + SKEW + 1):
                            if i < UNITS:
                                wait_full(act, step, s, n, CTX + i)
                                if base + i >= P_RING:
                                    wait_probs_used(act, base + i - P_RING)
                                act.activation(probs[:, (base + i) % P_RING, :],
                                               cols(step, s, n, CTX + i, 0, 2 * PSF), func,
                                               scale=scale, bias=bias).then_inc(read(step, s, n, CTX + i), 1)
                            u = i - SKEW - 1
                            if u % 4 == 3 and u > 0:
                                copy_out(step, s, n, u // 4, ctxT[s][:, u // 4, :], 0, PSF)

                    def context1_t(s, n):
                        copy_out("context1_t", s, n, CTX, vsum[s][:, :, :].rearrange("p b c -> p (b c)"), 0, NB * C)

                    def gate_up(s, n):
                        for c in range(FC):
                            wait_full(act, "gate_up", s, n, 2 * c)
                            if c:
                                wait_read(act, "gate_up", s, n, 2 * c - 2)
                            act.activation(gt[s], cols("gate_up", s, n, 2 * c, 0, TOK), ACT.Tanh, scale=0.5) \
                                .then_inc(tanh_gate[s], 1)

                    def qkv1(s, n):
                        for i in range(NT // 2):
                            wait_full(act, "qkv1", s, n, i)
                            src = cols("qkv1", s, n, i, 0, PSF).rearrange("p (t n) -> p t n", t=2)
                            act.activation(qk2[s][:, 2 * i:2 * i + 2, :], src, ACT.Square)
                            act.activation(qk[s][:, 2 * i:2 * i + 2, :], src, ACT.Copy) \
                                .then_inc(read("qkv1", s, n, i), 1)

                    def unit(s, n):
                        for t in range(NT):
                            act.wait_ge(unit_qk[s], t + 1)
                            u = qk[s][:, t, :].rearrange("p (m h d) -> p m h d", m=2, d=HD)
                            high_parts(s, t, u[:, 0, :, :], u[:, 1, :, :])

                    def split1(s, n):
                        act.wait_ge(gate_arg[s], 1)
                        act.activation(gates[s][:, :, :], ss[s][:, :, :], ACT.Tanh, scale=0.5).then_inc(gate_tanh[s], 1)

                    def stack_t(s, n):
                        for j in range(0, 4, 2):
                            copy_out("stack_t", s, n, j, qT[s][:, j, :], 0, TOK)

                    def stack1_t(s, n):
                        for i in range(0, 8, 2):
                            copy_out("stack1_t", s, n, i, (qT if i < 4 else kT)[s][:, i % 4, :], 0, TOK)

                    todo = {
                        "norm_t": lambda s, n: copy_out("norm_t", s, n, 0, xnT[s][:, :], 0, TOK),
                        "norm_t2": lambda s, n: copy_out("norm_t2", s, n, 0, xnT[s][:, :], 0, TOK),
                        "heads_t": lambda s, n: copy_out("heads_t", s, n, 0, xhT[s], 0, TOK),
                        "choose": choose, "dispatch": dispatch, "context1_t": context1_t, "slots": slots, "qkv": qkv, "stack_t": stack_t,
                        "gate_up": gate_up, "qkv1": qkv1, "unit": unit, "split1": split1, "stack1_t": stack1_t,
                        "router1": lambda s, n: router("router1", s, n, h1[s], "rb1"),
                        "router2": lambda s, n: router("router2", s, n, h2[s], "rb2"),
                        "window": lambda s, n: attend("window", s, n, ACT.Exp, HD ** -0.5, 0.0),
                        "resonance": lambda s, n: attend("resonance", s, n, ACT.Tanh, SHARP, tanh_bias[:, 0:1]),
                    }
                    act.wait_ge(weights_in, 16 * len(w))
                    act.wait_ge(consts_done, CONSTS)
                    for step, s, n in STEPS:
                        if step in todo:
                            todo[step](s, n)

                @block.gpsimd
                def _(pool):
                    def power(s, k):
                        pool.wait_ge(var_ready[s], k)
                        pool.tensor_tensor(rstd[s][:, :], var_eps[s][:, :], minus_half[:, 0:NT], ALU.pow) \
                            .then_inc(rstd_ready[s], 1)

                    def dispatch(s, n):
                        pool.wait_ge(place_ready[s], n + 1)
                        pool.tensor_tensor(share[s].rearrange("p t (e c) -> p (t e) c", e=E),
                                           place[s].rearrange("p t (e c) -> p (t e) c", e=E),
                                           small[s][:, 6, :, :].rearrange("p t e -> p (t e)")[:, :, None]
                                           .to_broadcast([P, NT * E, CAP]), ALU.mult).then_inc(share_ready[s], 1)

                    def experts(s, n):
                        for e in range(E):
                            wait_read(pool, "experts", s, n, E // EG + e)
                            pool.tensor_scalar(hh[:, e, :, :], hraw[:, e % 2, :, :], 0.0, None, ALU.max) \
                                .then_inc(hh_ready, 1)

                    def qkv(s, n):
                        pool.wait_ge(xn_ready[s], 2)
                        pool.memset(ks[s][:, :, 0:KV, USED:USED + 1], 1.0).then_inc(k_ones[s], 1)

                    todo = {
                        "norm": lambda s, n: power(s, [1, 2, 3, 4, 5, 7][n]), "renorm": lambda s, n: power(s, 6),
                        "dispatch": dispatch, "experts": experts, "qkv": qkv,
                    }
                    for step, s, n in STEPS:
                        if step in todo:
                            todo[step](s, n)

                @block.vector
                def _(dve):
                    linked = [0]

                    def link(ins):
                        linked[0] += 1
                        ins.then_inc(dve_link, 1)

                    def settle():
                        dve.wait_ge(dve_link, linked[0])

                    def variances(s, src):
                        for t in range(NT):
                            link(dve.bn_stats(stats[s][:, t, :], src[s][:, t, :]))
                        settle()
                        for t in range(NT):
                            link(dve.bn_aggr(mean_var[s][:, t, :], stats[s][:, t, :]))
                        settle()
                        dve.tensor_scalar(var_eps[s][:, :], mean_var[s][:, :, 1], LN_EPS, None, ALU.add) \
                            .then_inc(var_ready[s], 1)

                    def stats_of_x(s, n):
                        if n == 0:
                            dve.wait_ge(x_in_done[s], 16)
                        else:
                            step, k = [None, ("combine", 0), ("project", 0), ("combine", 1), ("down", 0),
                                       ("project1", 0)][n]
                            wait_read(dve, step, s, k, 0)
                        variances(s, x)

                    def normalise(s, src, dst, k):
                        dve.wait_ge(rstd_ready[s], k)
                        for t in range(NT):
                            last = dve.tensor_scalar(dst[s][:, t, :], src[s][:, t, :], mean_var[s][:, t, 0:1],
                                                     rstd[s][:, t:t + 1], ALU.subtract, ALU.mult)
                        last.then_inc(xn_ready[s], 1)

                    def norm(s, n):
                        normalise(s, x, xn, [1, 2, 3, 4, 5, 7][n])

                    def restats(s, n):
                        dve.wait_ge(xn_ready[s], 5)
                        variances(s, xn)

                    def renorm(s, n):
                        normalise(s, xn, xh, 6)
                        dve.tensor_tensor(x[s][:, :, :], x[s][:, :, :],
                                          W["bo1"][:, None, :].to_broadcast([P, NT, C]), ALU.add)

                    def router(step, s, n, dst, bias):
                        for c in range(1, HC, 2):
                            wait_full(dve, step, s, n, c)
                            dve.tensor_scalar(dst[:, c, :], cols(step, s, n, c, 0, TOK), W[bias][:, c:c + 1], 0.0,
                                              ALU.add, ALU.max).then_inc(read(step, s, n, c), 1)

                    def row(s, i):
                        return small[s][:, i, :, :]

                    def over_experts(ap):
                        return ap.to_broadcast([P, NT, E])

                    def logits(s, n):
                        wait_full(dve, "logits", s, n, 0)
                        ps = cols("logits", s, n, 0, 0, NT * E).rearrange("p (t e) -> p t e", e=E)
                        dve.tensor_tensor(row(s, 7), ps, W["rb3"][:, None, :].to_broadcast([P, NT, E]), ALU.add) \
                            .then_inc(read("logits", s, n, 0), 1)
                        wait_read(dve, "logits", s, n, 0)
                        link(dve.tensor_reduce(row(s, 3)[:, :, 0:1], row(s, 7), AX.X, ALU.max))
                        settle()
                        dve.tensor_tensor(row(s, 0), row(s, 7), over_experts(row(s, 3)[:, :, 0:1]), ALU.subtract) \
                            .then_inc(logit_shifted[s], 1)

                    def choose(s, n):
                        dve.wait_ge(logit_exp[s], n + 1)
                        link(dve.tensor_reduce(row(s, 3)[:, :, 1:2], row(s, 1), AX.X, ALU.add))
                        settle()
                        link(dve.reciprocal(row(s, 3)[:, :, 2:3], row(s, 3)[:, :, 1:2]))
                        settle()
                        link(dve.tensor_tensor(row(s, 2), row(s, 1), over_experts(row(s, 3)[:, :, 2:3]), ALU.mult))
                        settle()
                        for t in range(NT):
                            link(dve.max(top[s][:, t, :], small[s][:, 2, t, :]))
                        settle()
                        for t in range(NT):
                            link(dve.max_index(top_at[s][:, t, :], top[s][:, t, :], small[s][:, 2, t, :]))
                        settle()
                        numbers = expert_no[:, None, :].to_broadcast([P, NT, E])
                        for k in range(2):
                            link(dve.tensor_tensor(row(s, 4 + k), numbers, over_experts(top_at[s][:, :, k:k + 1]),
                                                   ALU.is_equal))
                        settle()
                        dve.tensor_tensor(chosen[s][:, :, :], row(s, 4), row(s, 5), ALU.add) \
                            .then_inc(chosen_ready[s], 1)
                        dve.wait_ge(chosen_ready[s], n + 1)
                        link(dve.tensor_tensor(row(s, 6), row(s, 2), chosen[s][:, :, :], ALU.mult))

                    def prefix(s, n):
                        wait_full(dve, "prefix", s, n, 0)
                        ps = cols("prefix", s, n, 0, 0, NT * E).rearrange("p (t e) -> p t e", e=E)
                        dve.scalar_tensor_tensor(out=row(s, 5), in0=ps, scalar=1.0, in1=chosen[s][:, :, :],
                                                 op0=ALU.add, op1=ALU.mult).then_inc(read("prefix", s, n, 0), 1)
                        wait_read(dve, "prefix", s, n, 0)
                        dve.tensor_tensor(place[s].rearrange("p t (e c) -> p (t e) c", e=E),
                                          slot_no[:, None, :].to_broadcast([P, NT * E, CAP]),
                                          row(s, 5).rearrange("p t e -> p (t e)")[:, :, None]
                                          .to_broadcast([P, NT * E, CAP]), ALU.is_equal).then_inc(place_ready[s], 1)

                    def dispatch(s, n):
                        for i, (c, m) in enumerate(CHUNKS):
                            wait_full(dve, "dispatch", s, n, NB + i)
                            dve.tensor_copy(shareT[s][0:m, i, :], cols("dispatch", s, n, NB + i, 0, TOK)[0:m, :]) \
                                .then_inc(read("dispatch", s, n, NB + i), 1)

                    def experts(s, n):
                        for i in range(E + SKEW + 1):
                            if i < E:
                                u = E // EG + i
                                wait_full(dve, "experts", s, n, u)
                                if E * n + i >= 2:
                                    dve.wait_ge(hh_ready, E * n + i - 1)
                                ps = cols("experts", s, n, u, 0, 2 * PSF).rearrange("p (a n) -> p a n", a=2)
                                dve.tensor_tensor(hraw[:, i % 2, :, :].rearrange("p (a c) n -> p a c n", a=2),
                                                  ps[:, :, 0:2 * SLOT4].rearrange("p a (c n) -> p a c n", c=2),
                                                  W["eb1"][:, i, :].rearrange("p (a c) -> p a c", a=2)[:, :, :, None]
                                                  .to_broadcast([P, 2, 2, SLOT4]), ALU.add) \
                                    .then_inc(read("experts", s, n, u), 1)
                            e = i - SKEW - 1
                            if e < 0 or e % EG != EG - 1:
                                continue
                            g = e // EG
                            wait_full(dve, "experts", s, n, g)
                            dve.tensor_tensor(eoT[:, :, g * EG:(g + 1) * EG, :].rearrange("p b e c -> p e b c"),
                                              cols("experts", s, n, g, 0, EG * SLOT4)
                                              .rearrange("p (e b c) -> p e b c", e=EG, b=NSB),
                                              W["eb2"][:, g * EG:(g + 1) * EG, None, None]
                                              .to_broadcast([P, EG, NSB, CAP]), ALU.add) \
                                .then_inc(read("experts", s, n, g), 1)

                    def add_to_x(step, s, n, factor):
                        wait_full(dve, step, s, n, 0)
                        dve.scalar_tensor_tensor(out=x[s][:, :, :].rearrange("p t c -> p (t c)"),
                                                 in0=cols(step, s, n, 0, 0, NT * C), scalar=factor,
                                                 in1=x[s][:, :, :].rearrange("p t c -> p (t c)"),
                                                 op0=ALU.mult, op1=ALU.add).then_inc(read(step, s, n, 0), 1)

                    def qkv(s, n):
                        for i in range(NT // 2):
                            wait_full(dve, "qkv", s, n, i)
                            dve.wait_ge(q_high[s], 2 * i + 2)
                            for j in range(2):
                                t = 2 * i + j
                                heads = cols("qkv", s, n, i, j * 192, (j + 1) * 192) \
                                    .rearrange("p (h d) -> p h d", d=HD)
                                dve.tensor_tensor(qs[s][:, t, :, 2 * HD:3 * HD], heads[:, 0:HEADS, :],
                                                  qs[s][:, t, :, 0:HD], ALU.subtract)
                                last = dve.tensor_tensor(ks[s][:, t, 0:KV, HD:2 * HD], heads[:, HEADS:HEADS + KV, :],
                                                         ks[s][:, t, 0:KV, 0:HD], ALU.subtract)
                            last.then_inc(read("qkv", s, n, i), 1)

                    def copy_out(step, s, n, i, dst):
                        wait_full(dve, step, s, n, i)
                        dve.tensor_copy(dst, cols(step, s, n, i, 0, TOK)).then_inc(read(step, s, n, i), 1)

                    def stack_t(s, n):
                        for j in range(1, 4, 2):
                            copy_out("stack_t", s, n, j, qT[s][:, j, :])
                        if n == 0:
                            copy_out("stack_t", s, n, 4, kT[s][:, 0, :])

                    def stack1_t(s, n):
                        for i in range(1, 8, 2):
                            copy_out("stack1_t", s, n, i, (qT if i < 4 else kT)[s][:, i % 4, :])

                    def row_max(s, n):
                        for t in range(NT):
                            for m in range(4):
                                u = 4 * t + m
                                g, j = 2 * (m // 2), 2 * (m % 2)
                                wait_full(dve, "row_max", s, n, u)
                                into = qs[s][:, t, :, USED:USED + 1].rearrange("p (j g) o -> p g j o", g=KV)
                                dve.tensor_reduce(into[:, g:g + 2, j:j + 2, :],
                                                  cols("row_max", s, n, u, 0, 2 * PSF)
                                                  .rearrange("p (g j k) -> p g j k", g=2, j=2),
                                                  AX.X, ALU.max, negate=True).then_inc(read("row_max", s, n, u), 1)

                    def context_t(s, n):
                        for i in range(CTX):
                            b, jp = i // 2, i % 2
                            wait_full(dve, "context_t", s, n, i)
                            ps = cols("context_t", s, n, i, 0, PSF).rearrange("p (a g r) -> p a g r", a=4, g=KV)
                            den = rden[s][:, i, :, :]
                            link(dve.reciprocal(den[:, :, :, None], ps[:, :, :, HD:HD + 1]))
                            settle()
                            for q in range(TS):
                                o = xh[s][:, b * TS + q, :].rearrange("p (g j d) -> p j g d", g=KV, j=GQ)
                                last = dve.tensor_tensor(o[:, 2 * jp:2 * jp + 2, :, :],
                                                         ps[:, q::TS, :, 0:HD],
                                                         den[:, q::TS, :, None].to_broadcast([P, 2, KV, HD]), ALU.mult)
                            last.then_inc(read("context_t", s, n, i), 1)

                    def context1_t(s, n):
                        wait_read(dve, "context1_t", s, n, CTX)
                        for i in range(CTX):
                            b, m = i // 2, i % 2
                            wait_full(dve, "context1_t", s, n, i)
                            ps = cols("context1_t", s, n, i, 0, PSF)
                            for q in range(TS):
                                t = b * TS + q
                                for jj in range(2):
                                    blk = 2 * m + jj
                                    at = (jj * TS + q) * P
                                    src = ps[:, at:at + P].rearrange("p (r n) -> p r n", r=4)
                                    o = xh[s][:, t, blk * PART:(blk + 1) * PART].rearrange("p (r d) -> p r d", d=HD)
                                    vs = vsum[s][:, b, blk * PART:(blk + 1) * PART].rearrange("p (r d) -> p r d", d=HD)
                                    diag = bass.AP(src.tensor, src.offset, [list(src.ap[0]), [PART + HD, 4], [1, HD]])
                                    last = dve.tensor_tensor(o, diag, vs, ALU.add)
                            last.then_inc(read("context1_t", s, n, i), 1)
                        wait_read(dve, "context1_t", s, n, CTX - 1)
                        heads = xh[s][:, :, :].rearrange("p t (h d) -> p t h d", d=HD)
                        dve.tensor_tensor(heads, heads, gates[s][:, :, 0:HEADS, None]
                                          .to_broadcast([P, NT, HEADS, HD]), ALU.mult).then_inc(gated_heads[s], 1)

                    def gate_up(s, n):
                        for c in range(FC):
                            wait_full(dve, "gate_up", s, n, 2 * c)
                            dve.wait_ge(tanh_gate[s], FC * n + c + 1)
                            dve.scalar_tensor_tensor(out=gg[s][:, c, :], in0=gt[s], scalar=1.0,
                                                     in1=cols("gate_up", s, n, 2 * c, 0, TOK),
                                                     op0=ALU.add, op1=ALU.mult) \
                                .then_inc(read("gate_up", s, n, 2 * c), 1)
                            wait_read(dve, "gate_up", s, n, 2 * c)
                            wait_full(dve, "gate_up", s, n, 2 * c + 1)
                            dve.tensor_tensor(gh[s][:, c, :], gg[s][:, c, :], cols("gate_up", s, n, 2 * c + 1, 0, TOK),
                                              ALU.mult).then_inc(read("gate_up", s, n, 2 * c + 1), 1)

                    def norm_t2(s, n):
                        wait_full(dve, "norm_t2", s, n, 1)
                        dve.tensor_scalar(xhT[s], cols("norm_t2", s, n, 1, 0, TOK), W["gamma"][:, 0:1],
                                          W["beta"][:, 0:1], ALU.mult, ALU.add).then_inc(read("norm_t2", s, n, 1), 1)

                    def heads_of(ap):
                        return ap.rearrange("p t (h d) -> p (t h) d", d=HD)

                    def per_head(ap):
                        return ap.rearrange("p t h -> p (t h)")[:, :, None]

                    def qkv1(s, n):
                        for i in range(NT // 2):
                            wait_read(dve, "qkv1", s, n, i)
                            link(dve.tensor_reduce(per_head(ss[s][:, 2 * i:2 * i + 2, :]),
                                                   heads_of(qk2[s][:, 2 * i:2 * i + 2, :]), AX.X, ALU.add))
                        settle()
                        v, y, z = (a[s][:, :, :].rearrange("p t h -> p (t h)") if len(a[s].shape) == 3 else a[s][:, :]
                                   for a in (ss, inv, newton))
                        link(dve.tensor_scalar(v, v, NORM_FLOOR, None, ALU.max))
                        settle()
                        link(dve.tensor_scalar(y.bitcast(I32), v.bitcast(I32), -0.5, GUESS, ALU.mult, ALU.add))
                        settle()
                        for _ in range(3):
                            link(dve.scalar_tensor_tensor(out=z, in0=y, scalar=-0.5, in1=y, op0=ALU.mult, op1=ALU.mult))
                            settle()
                            link(dve.tensor_tensor(z, z, v, ALU.mult))
                            settle()
                            link(dve.scalar_tensor_tensor(out=y, in0=z, scalar=1.5, in1=y, op0=ALU.add, op1=ALU.mult))
                            settle()

                    def unit(s, n):
                        for t in range(NT):
                            a = qk[s][:, t, :].rearrange("p (h d) -> p h d", d=HD)
                            dve.tensor_tensor(a, a, inv[s][:, t, :, None].to_broadcast([P, 2 * HEADS, HD]), ALU.mult) \
                                .then_inc(unit_qk[s], 1)
                        dve.wait_ge(unit_qk[s], NT)
                        link(dve.tensor_tensor(qk2[s], qk[s], W["g_qk"][:, None, :].to_broadcast([P, NT, 2 * C]),
                                               ALU.mult))
                        settle()
                        dve.tensor_reduce(per_head(ss[s][:, :, :]), heads_of(qk2[s]), AX.X, ALU.add) \
                            .then_inc(gate_arg[s], 1)

                    def split1(s, n):
                        for t in range(NT):
                            dve.wait_ge(q_high[s], NT + t + 1)
                            u = qk[s][:, t, :].rearrange("p (m h d) -> p m h d", m=2, d=HD)
                            dve.tensor_tensor(qs[s][:, t, :, 2 * HD:3 * HD], u[:, 0, :, :], qs[s][:, t, :, 0:HD],
                                              ALU.subtract)
                            dve.tensor_tensor(ks[s][:, t, :, HD:2 * HD], u[:, 1, :, :], ks[s][:, t, :, 0:HD],
                                              ALU.subtract).then_inc(q_stacked[s], 1)
                        dve.wait_ge(gate_tanh[s], 1)
                        link(dve.tensor_scalar(gates[s][:, :, 0:HEADS], gates[s][:, :, 0:HEADS], 0.1875, 0.3125,
                                               ALU.mult, ALU.add))
                        link(dve.tensor_scalar(gates[s][:, :, HEADS:], gates[s][:, :, HEADS:], 0.375, 0.625,
                                               ALU.mult, ALU.add))
                        settle()
                        wait_full(dve, "qkv1", s, n, 2)
                        for t in range(NT):
                            last = dve.tensor_tensor(
                                v1[s][:, t, :].rearrange("p (h d) -> p h d", d=HD),
                                cols("qkv1", s, n, 2, t * C, (t + 1) * C).rearrange("p (h d) -> p h d", d=HD),
                                gates[s][:, t, HEADS:, None].to_broadcast([P, HEADS, HD]), ALU.mult)
                        last.then_inc(read("qkv1", s, n, 2), 1)

                    todo = {
                        "stats": stats_of_x, "norm": norm, "restats": restats, "renorm": renorm,
                        "router1": lambda s, n: router("router1", s, n, h1[s], "rb1"),
                        "router2": lambda s, n: router("router2", s, n, h2[s], "rb2"),
                        "logits": logits, "choose": choose, "prefix": prefix, "dispatch": dispatch,
                        "experts": experts, "combine": lambda s, n: add_to_x("combine", s, n, 0.5),
                        "qkv": qkv, "stack_t": stack_t, "row_max": row_max, "context_t": context_t,
                        "project": lambda s, n: add_to_x("project", s, n, 1.0), "gate_up": gate_up,
                        "down": lambda s, n: add_to_x("down", s, n, 0.25),
                        "norm_t2": norm_t2, "qkv1": qkv1, "unit": unit, "split1": split1, "stack1_t": stack1_t,
                        "context1_t": context1_t, "project1": lambda s, n: add_to_x("project1", s, n, 1.0),
                    }
                    dve.wait_ge(weights_in, 16 * len(w))
                    dve.wait_ge(consts_done, CONSTS)
                    for step, s, n in STEPS:
                        if step in todo:
                            todo[step](s, n)

            numbers = sorted(one.num for one in round_sems)
            assert numbers == list(range(numbers[0], numbers[-1] + 1))
            nc.gpsimd.sem_clear(range(numbers[0], numbers[-1] + 1))
            nc.all_engine_barrier()


def lay_out(inputs):
    import numpy as np

    g = {k: np.asarray(v) for k, v in inputs.items()}

    def rows(a, shape):
        return np.broadcast_to(a, shape)

    def chunks(a):
        return a.reshape(-1, P, a.shape[-1]).transpose(1, 0, 2)

    wq = g["L0_attn_Wq"].reshape(KV, GQ, HD, C).transpose(1, 0, 2, 3).reshape(HEADS * HD, C)
    out = {
        "rW1": g["L0_ffn_rW1"],
        "rb1": g["L0_ffn_rb1"].reshape(HC, P).T,
        "rb2": g["L0_ffn_rb2"].reshape(HC, P).T,
        "rW2": chunks(g["L0_ffn_rW2"]),
        "rW3": chunks(g["L0_ffn_rW3"]),
        "rb3": rows(g["L0_ffn_rb3"], (P, E)),
        "eb1": g["L0_ffn_eb1"].reshape(E, HC, P).transpose(2, 0, 1),
        "eb2": g["L0_ffn_eb2"].T,
        "w_gate": g["L1_ffn_w_gate"].T,
        "w_up": g["L1_ffn_w_up"].T,
        "w_down": chunks(g["L1_ffn_w_down"].T),
        "eW1": g["L0_ffn_eW1"].transpose(1, 0, 2),
        "eW2": g["L0_ffn_eW2"].reshape(E, HC, P, C).transpose(2, 0, 1, 3),
        "qkv0": np.concatenate([wq, g["L0_attn_Wk"], g["L0_attn_Wv"]]).T,
        "wo0": g["L0_attn_Wo"].T,
        "qk1": np.concatenate([g["L1_attn_w_q"], g["L1_attn_w_k"]], 1),
        "v1": g["L1_attn_w_v"],
        "wo1": g["L1_attn_w_o"],
        "bo1": rows(g["L1_attn_b_o"], (P, C)),
        "gamma": g["L1_attn_gamma"].reshape(C, 1),
        "beta": g["L1_attn_beta"].reshape(C, 1),
        "g_qk": rows(np.concatenate([np.tile(g["L1_attn_g_q"], HEADS), np.tile(g["L1_attn_g_k"], HEADS)]),
                     (P, 2 * C)),
    }
    return {k: np.ascontiguousarray(v) for k, v in out.items()}


def kernel(**inputs):
    import numpy as np
    from concourse import bacc
    from concourse.bass_utils import run_bass_kernel_spmd

    x = np.ascontiguousarray(np.asarray(inputs["L0_attn_x"]))
    arrays = {"x": x, **{f"w_{k}": v for k, v in lay_out(inputs).items()}}
    nc = bacc.Bacc("TRN2", target_bir_lowering=False, num_devices=1)
    dram = {k: nc.dram_tensor(f"{k}_dram", v.shape, mybir.dt.from_np(v.dtype), kind="ExternalInput").ap()
            for k, v in arrays.items()}
    out = nc.dram_tensor("out_dram", x.shape, F32, kind="ExternalOutput").ap()
    macaron_kernel(nc, dram["x"], {k[2:]: ap for k, ap in dram.items() if k != "x"}, out)
    r = run_bass_kernel_spmd(nc, [{f"{k}_dram": v for k, v in arrays.items()}], core_ids=[0])
    return r.results[0]["out_dram"]
```

```python
from contextlib import ExitStack

import concourse.bass as bass
from concourse import mybir

ALU = mybir.AluOpType
ACT = mybir.ActivationFunctionType
AX = mybir.AxisListType
F32 = mybir.dt.float32
F32R = mybir.dt.float32r
BF16 = mybir.dt.bfloat16
I32 = mybir.dt.int32
U32 = mybir.dt.uint32

P = 128
C = 128
SEQ = 256
TS = SEQ // P
NB = 2
NT = NB * TS
TOK = NT * P
STREAMS = 2
PSF = 512

RH = 512
HC = RH // P
VECTOR_CHUNK = 1
E = 8
CAP = SEQ * 5 // 4 // E
SLOTS = E * CAP
CHUNKS = [(c, min(P, SLOTS - c)) for c in range(0, SLOTS, P)]
NSB = STREAMS * NB
SLOT4 = NSB * CAP
EG = 2

HEADS = 16
HD = 8
KV = 4
GQ = HEADS // KV
PART = 32
USED = 3 * HD
FH = 384
FC = FH // P

LN_EPS = 1e-5
NORM_FLOOR = 1e-24
GUESS = float(0x5F3759DF)
MASKED = -1e30
SHARP = 15.0
THRESHOLD = 0.27
DEQUANT = 1.0 / 127.0

RING = 6
P_RING = 3
UNITS = NB * 8
CTX = NB * 2
SKEW = 2
PARTS = {"router2": HC, "row_max": NT * 4, "window": UNITS + 1, "resonance": UNITS + 1}
CONSTS = 17 + 2 * STREAMS

MOE = ["stats", "norm", "norm_t", "router1", "router2", "logits", "logits_sum", "choose", "prefix", "dispatch",
       "experts", "slots", "combine"]
WINDOW = ["stats", "norm", "norm_t", "qkv", "stack_t", "row_max", "stack_t", "window", "context_t",
          "heads_t", "project"]
GATED = ["stats", "norm", "norm_t", "gate_up", "down"]
RESONANCE = ["stats", "norm", "restats", "renorm", "norm_t2", "qkv1", "unit", "split1", "stack1_t", "resonance",
             "context1_t", "heads_t", "project1"]
ROUND_STEPS = MOE + WINDOW + MOE + GATED + RESONANCE + GATED
TURNS = (
    (3, 1, 1, 1, 2, 1, 1, 1, 1, 2, 1, 1, 2, 1, 1, 4, 1, 1),
    (3, 1, 1, 1, 1, 1, 1, 1, 1, 1, 4, 1, 8, 1, 4, 1, 1, 2, 1, 1, 2, 1, 2, 1, 2, 1, 1, 2, 2, 1, 1, 1, 2, 1, 1,
     4, 2, 1, 1, 1, 1, 2, 1, 2, 1, 2, 1, 4, 1, 1, 1, 2, 1, 2, 1, 2, 1, 4, 2, 2, 1, 2, 1, 2, 1, 1, 1, 3, 1, 1),
    (1, 1, 2, 1, 1, 1, 1, 2, 1, 1, 1, 1, 1, 1, 2, 1, 1, 1, 1, 1, 1, 1, 2, 1, 3, 1, 7, 1, 6, 1, 3, 2, 1, 7, 1,
     2, 1, 1, 1, 6, 1, 1, 1, 3, 1, 3),
)

SPLIT = ("rW1", "rW2", "gate", "up")
STAGED = ("rW1", "rW2", "g_qk", "w_gate", "w_up", "w_down")
LATE = ("eW1", "eW2")


def psum_uses(step, n):
    attention = ([2, "a"] if n % 4 == 0 else [2]) if n < UNITS else []
    return {
        "norm_t": [1], "router1": [1] * HC, "router2": [1], "logits": [1], "logits_sum": [1], "prefix": [1],
        "dispatch": [1] * (NB + len(CHUNKS)), "experts": ["a"] * (E // EG) + [2] * E, "slots": [1] * NB,
        "combine": [1], "qkv": [1] * (NT // 2), "stack_t": [1] * (5 - n), "row_max": [2],
        "window": attention, "context_t": [1] * CTX, "heads_t": [1], "project": [1],
        "gate_up": [1] * (2 * FC), "down": [1],
        "norm_t2": [1, 1], "qkv1": [1] * (NT // 2 + 1), "split1": [1], "stack1_t": [1] * 8,
        "resonance": attention, "context1_t": [1] * (CTX + 1), "project1": [1],
    }.get(step, [])


def schedule():
    seen, out, stretches = {}, [], [[]]
    for step in ROUND_STEPS:
        if step == "experts":
            stretches.append([])
        else:
            stretches[-1] += [step] * PARTS.get(step, 1)
    for k, (steps, turns) in enumerate(zip(stretches, TURNS)):
        if k:
            out.append(("experts", 0, k - 1))
        rest = [iter(steps) for _ in range(STREAMS)]
        for i, count in enumerate(turns):
            s = i % STREAMS
            for _ in range(count):
                step = next(rest[s])
                n = seen.get((step, s), 0)
                seen[(step, s)] = n + 1
                out.append((step, s, n))
        assert not any(list(left) for left in rest)
    return out


def bank_plan(steps):
    plan, count, last = {}, [0] * 8, [None] * 8
    at = held = 0
    for step, s, n in steps:
        for i, size in enumerate(psum_uses(step, n)):
            if size == "a":
                b, width = RING + held, 1
                held = (held + 1) % 2
            else:
                width = size
                at += at % width
                b = at % RING
                at += width
            before = {last[k] for k in range(b, b + width)} - {None}
            count[b] += 1
            for k in range(b, b + width):
                last[k] = (b, count[b])
            plan[(step, s, n, i)] = (b, count[b], sorted(before))
    return plan


def macaron_kernel(nc, x_in, w, out):
    B = x_in.shape[0]
    ROUNDS = B // (NB * STREAMS)
    STEPS = schedule()
    PLAN = bank_plan(STEPS)
    unit_no = {}
    for step, s, n in STEPS:
        if step in ("window", "resonance") and n < UNITS:
            unit_no[(step, s, n)] = len(unit_no)

    ctx = ExitStack()
    with ctx:
        def sb(name, shape, dt=F32):
            return ctx.enter_context(nc.sbuf_tensor(name, shape, dt))

        round_sems = []

        def sem(name):
            one = ctx.enter_context(nc.semaphore(name))
            round_sems.append(one)
            return one

        def per_stream(name):
            return [sem(f"{name}{s}") for s in range(STREAMS)]

        W = {name: sb(f"w_{name}", list(ap.shape), ap.dtype) for name, ap in w.items() if name not in STAGED}
        parts_of = {"rW1": [RH], "rW2": [HC, RH], "gate": [FH], "up": [FH]}
        halves = {name: sb(f"{name}_halves", [P, 2] + parts_of[name], F32R) for name in SPLIT}
        down_f = sb("down_f", [P, FC, C])
        rw3 = sb("rw3", [P, HC, PART])
        w_gates = sb("w_gates", [P, 2 * HEADS])
        pick = sb("pick", [P, E])
        ident = sb("ident", [P, P])
        ident_b = sb("ident_b", [P, P], BF16)
        ones = sb("ones", [P, P])
        ones_b = sb("ones_b", [P, P], BF16)
        earlier = sb("earlier", [P, P], BF16)
        slot_no = sb("slot_no", [P, CAP])
        expert_no = sb("expert_no", [P, E])
        far_low = sb("far_low", [P, P], BF16)
        far_high = sb("far_high", [P, P], BF16)
        minus_half = sb("minus_half", [P, NT])
        tanh_bias = sb("tanh_bias", [P, 1])
        warm_up = sb("warm_up", [P, 1])

        def both(name, shape, dt=F32):
            return [sb(f"{name}{s}", shape, dt) for s in range(STREAMS)]

        def overlaid(name, shape):
            plain, rounded = [], []
            for s in range(STREAMS):
                with nc.sbuf_tensor(f"{name}{s}", shape, F32) as one:
                    plain.append(one)
                rounded.append(sb(f"{name}_r{s}", shape, F32R))
            return plain, rounded

        x = both("x", [P, NT, C])
        stats = both("stats", [P, NT, 6])
        mean_var = both("mean_var", [P, NT, 2])
        var_eps = both("var_eps", [P, NT])
        rstd = both("rstd", [P, NT])
        xn = both("xn", [P, NT, C])
        xnT, xnT_r = overlaid("xnT", [P, TOK])
        big, big_r = overlaid("big", [P, 2 * HC * TOK])
        hid_all = sb("hid", [P, STREAMS, HC * E * NB * CAP])
        hid = [hid_all[:, s, :] for s in range(STREAMS)]
        small = both("small", [P, 8, NT, E])
        top = both("top", [P, NT, 8])
        top_at = both("top_at", [P, NT, 8], U32)
        chosen = both("chosen", [P, NT, E], BF16)
        shareT, shareT_r = overlaid("shareT", [P, len(CHUNKS), TOK])
        eoT = sb("eoT", [P, NSB, E, CAP])
        eo_flat = eoT[:, :, :, :].rearrange("p b e c -> p (b e c)")
        xh = [eo_flat[:, s * TOK:(s + 1) * TOK].rearrange("p (t c) -> p t c", t=NT) for s in range(STREAMS)]
        eo = both("eo", [P, NB, len(CHUNKS), C])
        v0 = both("v0", [P, NT, KV + 1, 2 * HD])
        ss = both("ss", [P, NT, 2 * HEADS])
        gates = both("gates", [P, NT, 2 * HEADS])
        rden = both("rden", [P, CTX, 4, KV])
        probs = sb("probs", [P, P_RING, 2 * PSF])

        h1 = [big_r[s][:, :].rearrange("p (a c t) -> p a c t", a=2, c=HC) for s in range(STREAMS)]
        h1_full = [big[s][:, HC * TOK:2 * HC * TOK].rearrange("p (c t) -> p c t", c=HC) for s in range(STREAMS)]
        logit_parts = [big[s][:, 0:TOK] for s in range(STREAMS)]
        h2 = [hid[s][:, 0:HC * TOK].rearrange("p (c t) -> p c t", c=HC) for s in range(STREAMS)]
        xnT_high = [xnT_r[s][:, :] for s in range(STREAMS)]
        xnT_low = [shareT_r[s][:, 1, :] for s in range(STREAMS)]
        q_place, qT = overlaid("qT", [P, 4, TOK])
        k_place, kT = overlaid("kT", [P, 4, TOK])
        x_start = [q_place[s][:, 3, :].rearrange("p (t c) -> p t c", t=NT) for s in range(STREAMS)]
        slotT = k_place[0][:, :, :].rearrange("p c t -> p (c t)")[:, 0:E * NSB * CAP] \
            .rearrange("p (e b c) -> p e b c", e=E, b=NSB)
        hraw = k_place[1][:, :, :].rearrange("p c t -> p (c t)")[:, 0:2 * HC * SLOT4] \
            .rearrange("p (i c n) -> p i c n", i=2, c=HC)
        place = [hid[s][:, 0:NT * SLOTS].rearrange("p (t c) -> p t c", t=NT) for s in range(STREAMS)]
        share = [hid[s][:, NT * SLOTS:2 * NT * SLOTS].rearrange("p (t c) -> p t c", t=NT) for s in range(STREAMS)]
        xhT = [shareT[s][:, 0, :] for s in range(STREAMS)]
        v1 = [eo[s][:, :, :, :].rearrange("p b i c -> p (b i c)")[:, 0:NT * C].rearrange("p (t c) -> p t c", t=NT)
              for s in range(STREAMS)]
        hh = hid_all[:, :, :].rearrange("p s n -> p (s n)").rearrange("p (e c n) -> p e c n", e=E, c=HC)
        ctxT = [big[s][:, 0:CTX * PSF].rearrange("p (u n) -> p u n", u=CTX) for s in range(STREAMS)]
        LENGTHS = NT * 2 * HEADS
        inv, newton = ([small[s][:, :, :, :].rearrange("p a t e -> p (a t e)")[:, i * LENGTHS:(i + 1) * LENGTHS]
                        .rearrange("p (t h) -> p t h", t=NT) for s in range(STREAMS)] for i in range(2))
        vsum = [hid[s][:, 0:NB * C].rearrange("p (b c) -> p b c", b=NB) for s in range(STREAMS)]
        qs = [big[s][:, 0:NT * HEADS * PART].rearrange("p (t h r) -> p t h r", t=NT, h=HEADS) for s in range(STREAMS)]
        ks = [big[s][:, NT * HEADS * PART:2 * NT * HEADS * PART].rearrange("p (t h r) -> p t h r", t=NT, h=HEADS)
              for s in range(STREAMS)]
        qk = [hid[s][:, 0:NT * 2 * C].rearrange("p (t n) -> p t n", t=NT) for s in range(STREAMS)]
        qk2 = [hid[s][:, NT * 2 * C:2 * NT * 2 * C].rearrange("p (t n) -> p t n", t=NT) for s in range(STREAMS)]
        gt = [hid[s][:, 0:TOK] for s in range(STREAMS)]
        gg = [hid[s][:, TOK:(1 + FC) * TOK].rearrange("p (c t) -> p c t", c=FC) for s in range(STREAMS)]
        gh = [big[s][:, 0:FC * TOK].rearrange("p (c t) -> p c t", c=FC) for s in range(STREAMS)]

        at = {0: 0, 1: 0}
        for name in STAGED:
            ap = w[name]
            n = ap.shape[1] if len(ap.shape) == 2 else ap.shape[1] * ap.shape[2]
            s = 0 if ap.dtype == I32 else 1
            W[name] = big[s][:, at[s]:at[s] + n]
            if ap.dtype == I32:
                W[name] = W[name].bitcast(I32)
            if len(ap.shape) == 3:
                W[name] = W[name].rearrange("p (c n) -> p c n", c=ap.shape[1])
            at[s] += n
        W["gate"] = big[0][:, at[0]:at[0] + FH]
        W["up"] = big[0][:, at[0] + FH:at[0] + 2 * FH]

        psum = ctx.enter_context(nc.psum_tensor("psum", [P, 8, PSF], F32))

        x_out_done = [ctx.enter_context(nc.semaphore(f"x_out_done{s}")) for s in range(STREAMS)]
        first_x_in = ctx.enter_context(nc.semaphore("first_x_in"))
        weights_in = ctx.enter_context(nc.semaphore("weights_in"))
        expert_weights_in = ctx.enter_context(nc.semaphore("expert_weights_in"))
        consts_done = ctx.enter_context(nc.semaphore("consts_done"))
        dequant_done = ctx.enter_context(nc.semaphore("dequant_done"))
        high_done = ctx.enter_context(nc.semaphore("high_done"))
        bank_full = [sem(f"bank_full{b}") for b in range(8)]
        bank_read = [sem(f"bank_read{b}") for b in range(8)]
        probs_used = sem("probs_used")
        x_in_done = per_stream("x_in_done")
        dve_link = sem("dve_link")
        var_ready = per_stream("var_ready")
        rstd_ready = per_stream("rstd_ready")
        xn_ready = per_stream("xn_ready")
        logit_shifted = per_stream("logit_shifted")
        logit_exp = per_stream("logit_exp")
        chosen_ready = per_stream("chosen_ready")
        place_ready = per_stream("place_ready")
        share_ready = per_stream("share_ready")
        hh_ready = sem("hh_ready")
        h1_high = per_stream("h1_high")
        xnT_rounded = per_stream("xnT_rounded")
        k_zero = per_stream("k_zero")
        pads_set = per_stream("pads_set")
        q_high = per_stream("q_high")
        q_stacked = per_stream("q_stacked")
        tanh_gate = per_stream("tanh_gate")
        unit_qk = per_stream("unit_qk")
        gated_heads = per_stream("gated_heads")
        gate_tanh = per_stream("gate_tanh")

        def bank(step, s, n, i):
            return PLAN[(step, s, n, i)][0]

        def units_of_part(n, skew):
            return [n] if n < UNITS else range(UNITS, UNITS + skew)

        def sums_by_vector(step, s):
            return step == "resonance" or s == 1

        def cols(step, s, n, i, lo, hi):
            b = bank(step, s, n, i)
            if hi <= PSF:
                return psum[:, b, lo:hi]
            return psum[:, b:b + 2, :].rearrange("p a n -> p (a n)")[:, lo:hi]

        def wait_full(eng, step, s, n, i):
            b, k, _ = PLAN[(step, s, n, i)]
            eng.wait_ge(bank_full[b], k)

        def wait_free(eng, step, s, n, i):
            for b, k in PLAN[(step, s, n, i)][2]:
                eng.wait_ge(bank_read[b], k)

        def full(step, s, n, i):
            return bank_full[bank(step, s, n, i)]

        def read(step, s, n, i):
            return bank_read[bank(step, s, n, i)]

        def wait_read(eng, step, s, n, i):
            b, k, _ = PLAN[(step, s, n, i)]
            eng.wait_ge(bank_read[b], k)

        def wait_probs_used(eng, unit):
            step, s, n = next(key for key, number in unit_no.items() if number == unit)
            if unit % 4 == 3:
                wait_full(eng, step, s, n - 3, 1)
            else:
                eng.wait_ge(probs_used, unit + 1 - (unit + 1) // 4)

        def load_x(sp, rnd, s, done):
            src = x_in[bass.ds(rnd * NSB + s * NB, NB)].rearrange("b (k p) c -> p (b k) c", p=P)
            sp.dma_start(x_start[s], src).then_inc(done, 16)

        with nc.Block() as block:
            @block.sync
            def _(sp):
                for s in range(STREAMS):
                    load_x(sp, 0, s, first_x_in)
                for name, ap in w.items():
                    sp.dma_start(W[name][...], ap).then_inc(expert_weights_in if name in LATE else weights_in, 16)
                sp.wait_ge(first_x_in, 16 * STREAMS)

            @block.gpsimd
            def _(pool):
                done = [0]

                def const(ins):
                    done[0] += 1
                    ins.then_inc(consts_done, 1)

                def chained(ins):
                    const(ins)
                    pool.wait_ge(consts_done, done[0])

                for s in range(STREAMS):
                    pool.memset(x[s][:, 0, 0:1], 0.0).then_inc(x_out_done[s], 16)
                const(pool.memset(ones[:, :], 1.0))
                const(pool.memset(ones_b[:, :], 1.0))
                const(pool.memset(minus_half[:, :], -0.5))
                const(pool.memset(tanh_bias[:, :], -SHARP * THRESHOLD))
                const(pool.memset(rw3[:, :, :], 0.0))
                for m in (ident, ident_b, far_low, far_high):
                    const(pool.memset(m[:, :], 0.0))
                chained(pool.memset(earlier[:, :], 1.0))
                for m in (ident, ident_b):
                    const(pool.affine_select(out=m[:, :], in_=m[:, :], compare_op=ALU.not_equal, fill=1.0,
                                             base=0, pattern=[[-1, P]], channel_multiplier=1))
                const(pool.affine_select(out=earlier[:, :], in_=earlier[:, :], compare_op=ALU.is_gt, fill=0.0,
                                         base=0, pattern=[[1, P]], channel_multiplier=-1))
                const(pool.affine_select(out=far_low[:, :], in_=far_low[:, :], compare_op=ALU.is_ge, fill=MASKED,
                                         base=0, pattern=[[-1, P]], channel_multiplier=1))
                const(pool.affine_select(out=far_high[:, :], in_=far_high[:, :], compare_op=ALU.is_ge, fill=MASKED,
                                         base=0, pattern=[[1, P]], channel_multiplier=-1))
                const(pool.iota(slot_no[:, :], pattern=[[1, CAP]], base=1, channel_multiplier=0,
                                allow_small_or_imprecise_dtypes=True))
                const(pool.iota(expert_no[:, :], pattern=[[1, E]], base=0, channel_multiplier=0,
                                allow_small_or_imprecise_dtypes=True))
                for s in range(STREAMS):
                    chained(pool.memset(v0[s][:, :, :, :], 0.0))
                    const(pool.memset(v0[s][:, :, :, HD:HD + 1], 1.0))

            @block.vector
            def _(dve):
                dve.wait_ge(weights_in, 16 * (len(w) - len(LATE)))
                for a, b in ((W["gate"], "w_gate"), (W["up"], "w_up"), (down_f, "w_down")):
                    dve.tensor_scalar(a[...], W[b][...], DEQUANT, None, ALU.mult).then_inc(dequant_done, 1)
                dve.wait_ge(dequant_done, 3)
                for name in SPLIT:
                    dve.tensor_copy(halves[name][:, 0], W[name][...]).then_inc(high_done, 1)
                dve.wait_ge(high_done, len(SPLIT))
                for name in SPLIT:
                    dve.tensor_tensor(halves[name][:, 1], W[name][...], halves[name][:, 0].bitcast(F32), ALU.subtract) \
                        .then_inc(dequant_done, 1)
                dve.wait_ge(consts_done, CONSTS)
                dve.tensor_copy(rw3[:, :, 0:E], W["rW3"][:, :, :]).then_inc(dequant_done, 1)
                product = xn[0][:, 0:2, :].rearrange("p t c -> p (t c)")
                dve.tensor_tensor(product, W["qk1"][:, :], W["g_qk"], ALU.mult).then_inc(high_done, 1)
                dve.wait_ge(high_done, len(SPLIT) + 1)
                dve.tensor_reduce(w_gates[:, :], product.rearrange("p (h d) -> p h d", d=HD), AX.X, ALU.add) \
                    .then_inc(dequant_done, 1)
                dve.tensor_reduce(pick[:, :], ident[:, :].rearrange("p (c e) -> p e c", c=HC)[:, 0:E, :],
                                  AX.X, ALU.add).then_inc(dequant_done, 1)

        with nc.Fori(0, ROUNDS, hint_back_edge=True) as rnd:
            with nc.Block() as block:
                @block.sync
                def _(sp):
                    for s in range(STREAMS):
                        wait_full(sp, "resonance", s, UNITS - 1, 0)
                        load_x(sp, (rnd + 1) % ROUNDS, s, x_in_done[s])
                    for s in range(STREAMS):
                        wait_read(sp, "down", s, 1, 0)
                        dst = out[bass.ds(rnd * NSB + s * NB, NB)].rearrange("b (k p) c -> p (b k) c", p=P)
                        sp.dma_start(dst, x[s][:, :, :]).then_inc(x_out_done[s], 16)
                    for s in range(STREAMS):
                        sp.wait_ge(x_in_done[s], 16)

                @block.tensor
                def _(pe):
                    def transposes(step, s, n, i, src, tiles, wait=lambda t: None):
                        wait_free(pe, step, s, n, i)
                        for t in range(tiles):
                            wait(t)
                            last = pe.transpose(cols(step, s, n, i, t * P, (t + 1) * P), src(t), ident[:, :])
                        last.then_inc(full(step, s, n, i), 1)

                    def norm_t(s, n):
                        k = [1, 2, 3, 4, 7][n]
                        transposes("norm_t", s, n, 0, lambda t: xn[s][:, t, :], NT, lambda t: wait_tile(s, k, t))

                    def wait_tile(s, k, t):
                        pe.wait_ge(xn_ready[s], NT * (k - 1) + t + 1)

                    def three_passes(o, weights, high, low, start=True, stop=True, wait_low=lambda: None):
                        pe.matmul(o, weights[0], high, start=start, stop=False)
                        pe.matmul(o, weights[1], high, start=False, stop=False)
                        wait_low()
                        return pe.matmul(o, weights[0], low, start=False, stop=stop)

                    def router1(s, n):
                        pe.wait_ge(xnT_rounded[s], n + 1)
                        for c in range(HC):
                            wait_free(pe, "router1", s, n, c)
                            three_passes(cols("router1", s, n, c, 0, TOK),
                                         [halves["rW1"][:, i, c * P:(c + 1) * P] for i in range(2)],
                                         xnT_high[s], xnT_low[s],
                                         wait_low=lambda: wait_read(pe, "norm_t", s, 2 * n, 0)) \
                                .then_inc(full("router1", s, n, c), 1)

                    def router2(s, n):
                        c = n % HC
                        wait_free(pe, "router2", s, n, 0)
                        for k in range(HC):
                            if c == 0:
                                wait_read(pe, "router1", s, n // HC, k)
                            last = three_passes(cols("router2", s, n, 0, 0, TOK),
                                                [halves["rW2"][:, i, k, c * P:(c + 1) * P] for i in range(2)],
                                                h1[s][:, 0, k, :], h1[s][:, 1, k, :], k == 0, k == HC - 1)
                        last.then_inc(full("router2", s, n, 0), 1)

                    def logits(s, n):
                        wait_free(pe, "logits", s, n, 0)
                        for c in range(HC):
                            wait_read(pe, "router2", s, HC * n + c, 0)
                            last = pe.matmul(cols("logits", s, n, 0, 0, TOK)[c * PART:(c + 1) * PART, :], rw3[:, c, :],
                                             h2[s][:, c, :], start=True, stop=True)
                        last.then_inc(full("logits", s, n, 0), 1)

                    def logits_sum(s, n):
                        wait_read(pe, "logits", s, n, 0)
                        wait_free(pe, "logits_sum", s, n, 0)
                        for t in range(NT):
                            last = pe.matmul(cols("logits_sum", s, n, 0, t * E, (t + 1) * E),
                                             logit_parts[s][:, t * P:(t + 1) * P], pick[:, :], start=True, stop=True)
                        last.then_inc(full("logits_sum", s, n, 0), 1)

                    def prefix(s, n):
                        pe.wait_ge(chosen_ready[s], n + 1)
                        wait_free(pe, "prefix", s, n, 0)
                        for t in range(NT):
                            o = cols("prefix", s, n, 0, t * E, (t + 1) * E)
                            first_tile = t % TS == 0
                            last = pe.matmul(o, earlier[:, :], chosen[s][:, t, :], start=True, stop=first_tile)
                            if not first_tile:
                                last = pe.matmul(o, ones_b[:, :], chosen[s][:, t - 1, :], start=False, stop=True)
                        last.then_inc(full("prefix", s, n, 0), 1)

                    def dispatch(s, n):
                        pe.wait_ge(place_ready[s], n + 1)
                        for b in range(NB):
                            wait_free(pe, "dispatch", s, n, b)
                            for k in range(TS):
                                t = b * TS + k
                                last = pe.matmul(cols("dispatch", s, n, b, 0, SLOTS), xn[s][:, t, :],
                                                 place[s][:, t, :], start=(k == 0), stop=(k == TS - 1))
                            last.then_inc(full("dispatch", s, n, b), 1)
                        pe.wait_ge(share_ready[s], n + 1)
                        for i, (c, m) in enumerate(CHUNKS):
                            u = NB + i
                            wait_free(pe, "dispatch", s, n, u)
                            for t in range(NT):
                                last = pe.transpose(cols("dispatch", s, n, u, t * P, (t + 1) * P)[0:m, :],
                                                    share[s][:, t, c:c + m], ident[:, :])
                            last.then_inc(full("dispatch", s, n, u), 1)

                    def experts(s, n):
                        if n == 0:
                            pe.wait_ge(expert_weights_in, 16 * len(LATE))
                        for one in range(STREAMS):
                            for b in range(NB):
                                wait_read(pe, "dispatch", one, n, b)
                        for i in range(E + SKEW):
                            if i < E:
                                wait_free(pe, "experts", s, n, E // EG + i)
                                for c in range(HC):
                                    at = c // 2 * PSF + c % 2 * SLOT4
                                    last = pe.matmul(cols("experts", s, n, E // EG + i, at, at + SLOT4),
                                                     W["eW1"][:, i, c * P:(c + 1) * P],
                                                     slotT[:, i, :, :].rearrange("p b c -> p (b c)"),
                                                     start=True, stop=True)
                                last.then_inc(full("experts", s, n, E // EG + i), 1)
                            e = i - SKEW
                            if e < 0:
                                continue
                            if e % EG == 0:
                                wait_free(pe, "experts", s, n, e // EG)
                            pe.wait_ge(hh_ready, E * n + e + 1)
                            for c in range(HC):
                                last = pe.matmul(cols("experts", s, n, e // EG, e % EG * SLOT4, (e % EG + 1) * SLOT4),
                                                 W["eW2"][:, e, c, :], hh[:, e, c, :],
                                                 start=(c == 0), stop=(c == HC - 1))
                            if e % EG == EG - 1:
                                last.then_inc(full("experts", s, n, e // EG), 1)

                    def slots(s, n):
                        for i in range(E // EG):
                            wait_read(pe, "experts", 0, n, i)
                        for b in range(NB):
                            wait_free(pe, "slots", s, n, b)
                            flat = eoT[:, s * NB + b, :, :].rearrange("p e c -> p (e c)")
                            for i, (c, m) in enumerate(CHUNKS):
                                last = pe.transpose(cols("slots", s, n, b, i * P, (i + 1) * P)[0:m, :],
                                                    flat[:, c:c + m], ident[:, :])
                            last.then_inc(full("slots", s, n, b), 1)

                    def combine(s, n):
                        for i in range(len(CHUNKS)):
                            wait_read(pe, "dispatch", s, n, NB + i)
                        wait_free(pe, "combine", s, n, 0)
                        for t in range(NT):
                            wait_read(pe, "slots", s, n, t // TS)
                            for i, (c, m) in enumerate(CHUNKS):
                                last = pe.matmul(cols("combine", s, n, 0, t * C, (t + 1) * C),
                                                 shareT[s][0:m, i, t * P:(t + 1) * P], eo[s][0:m, t // TS, i, :],
                                                 start=(i == 0), stop=(i == len(CHUNKS) - 1))
                        last.then_inc(full("combine", s, n, 0), 1)

                    def qkv(s, n):
                        wait_read(pe, "norm_t", s, 1, 0)
                        for i in range(NT // 2):
                            wait_free(pe, "qkv", s, n, i)
                            for j in range(2):
                                t = 2 * i + j
                                last = pe.matmul(cols("qkv", s, n, i, j * 192, (j + 1) * 192),
                                                 xnT[s][:, t * P:(t + 1) * P], W["qkv0"][:, :], start=True, stop=True)
                            last.then_inc(full("qkv", s, n, i), 1)

                    def stack_t(s, n):
                        if n == 0:
                            pe.wait_ge(pads_set[s], 3)
                        else:
                            for u in range(NT * 4):
                                wait_read(pe, "row_max", s, u, 0)
                        for j in range(4):
                            transposes("stack_t", s, n, j, lambda t: qs[s][:, t, 4 * j:4 * j + 4, :]
                                       .rearrange("p h r -> p (h r)"), NT,
                                       lambda t: wait_read(pe, "qkv", s, 0, t // 2) if n == 0 and j == 0 else None)
                        if n == 0:
                            transposes("stack_t", s, n, 4, lambda t: ks[s][:, t, 0:4, :]
                                       .rearrange("p h r -> p (h r)"), NT)

                    def row_max(s, n):
                        if n == 0:
                            for j in range(5):
                                wait_read(pe, "stack_t", s, 0, j)
                            pe.wait_ge(k_zero[s], 1)
                        t, m = n // 4, n % 4
                        b, k = t // TS, t % TS
                        wait_free(pe, "row_max", s, n, 0)
                        for g in range(0, KV, 2):
                            pe.matmul(cols("row_max", s, n, 0, g // 2 * PSF, (g // 2 + 1) * PSF),
                                      qT[s][:, m, t * P:(t + 1) * P], kT[s][:, g:g + 2, b * SEQ:(b + 1) * SEQ],
                                      start=True, stop=False, skip_group_check=True)
                        for half in range(2):
                            o = cols("row_max", s, n, 0, half * PSF, (half + 1) * PSF) \
                                .rearrange("p (g k) -> p g k", g=2)[:, :, (1 - k) * P:(2 - k) * P]
                            far = (far_low if k == 0 else far_high)[:, None, :].to_broadcast([P, 2, P])
                            last = pe.matmul(o, ident_b[:, :], far, start=False, stop=True,
                                             skip_group_check=True)
                        last.then_inc(full("row_max", s, n, 0), 1)

                    def window(s, n):
                        if n == 0:
                            for j in range(4):
                                wait_read(pe, "stack_t", s, 1, j)
                        for i in units_of_part(n, SKEW):
                            if i < UNITS:
                                b, jp, g = i // 8, i // 4 % 2, i % 4
                                wait_free(pe, "window", s, n, 0)
                                for k in range(TS):
                                    o = cols("window", s, n, 0, k * PSF, (k + 1) * PSF)
                                    pe.matmul(o, kT[s][:, g, b * SEQ + k * P:b * SEQ + (k + 1) * P],
                                              qT[s][:, 2 * jp:2 * jp + 2, b * SEQ:(b + 1) * SEQ],
                                              start=True, stop=False, skip_group_check=True)
                                for k in range(TS):
                                    o = cols("window", s, n, 0, k * PSF, (k + 1) * PSF) \
                                        .rearrange("p (j q) -> p j q", j=2)[:, :, (1 - k) * P:(2 - k) * P]
                                    far = (far_low if k == 0 else far_high)[:, None, :].to_broadcast([P, 2, P])
                                    last = pe.matmul(o, ident_b[:, :], far, start=False, stop=True,
                                                     skip_group_check=True)
                                last.then_inc(full("window", s, n, 0), 1)
                            u = i - SKEW
                            if u < 0:
                                continue
                            b, g = u // 8, u % 4
                            sums = ("window", s, u - g, 1)
                            if g == 0:
                                wait_free(pe, *sums)
                            wait_read(pe, "window", s, u, 0)
                            pr = probs[:, unit_no[("window", s, u)] % P_RING, :].rearrange("p (k n) -> p k n", k=TS)
                            for k in range(TS):
                                vv = v0[s][:, b * TS + k, g:g + 2, :].rearrange("p g d -> p (g d)")
                                last = pe.matmul(cols(*sums, 0, PSF)[g * PART:(g + 1) * PART, :],
                                                 vv, pr[:, k, :], start=(k == 0), stop=(k == TS - 1))
                            last.then_inc(full(*sums) if g == 3 else probs_used, 1)

                    def context_t(s, n, step="context_t", source="window"):
                        for i in range(CTX):
                            wait_read(pe, source, s, 4 * i, 1)
                            transposes(step, s, n, i, lambda t: ctxT[s][:, i, t * P:(t + 1) * P], 4)

                    def context1_t(s, n):
                        wait_free(pe, "context1_t", s, n, CTX)
                        for b in range(NB):
                            for k in range(TS):
                                last = pe.matmul(cols("context1_t", s, n, CTX, b * C, (b + 1) * C), ones[:, :],
                                                 v1[s][:, b * TS + k, :], start=(k == 0), stop=(k == TS - 1))
                        last.then_inc(full("context1_t", s, n, CTX), 1)
                        context_t(s, n, "context1_t", "resonance")

                    def heads_t(s, n):
                        if n == 0:
                            for i in range(CTX):
                                wait_read(pe, "context_t", s, 0, i)
                        else:
                            pe.wait_ge(gated_heads[s], 1)
                        transposes("heads_t", s, n, 0, lambda t: xh[s][:, t, :], NT)

                    def project(s, n, step="project", wname="wo0", k=0):
                        wait_read(pe, "heads_t", s, k, 0)
                        wait_free(pe, step, s, n, 0)
                        for t in range(NT):
                            last = pe.matmul(cols(step, s, n, 0, t * C, (t + 1) * C), xhT[s][:, t * P:(t + 1) * P],
                                             W[wname][:, :], start=True, stop=True)
                        last.then_inc(full(step, s, n, 0), 1)

                    def gate_up(s, n):
                        pe.wait_ge(xnT_rounded[s], 3 + n)
                        for c in range(FC):
                            for i, name in enumerate(("gate", "up")):
                                wait_free(pe, "gate_up", s, n, 2 * c + i)
                                three_passes(cols("gate_up", s, n, 2 * c + i, 0, TOK),
                                             [halves[name][:, h, c * P:(c + 1) * P] for h in range(2)],
                                             xnT_high[s], xnT_low[s],
                                             wait_low=lambda: wait_read(pe, "norm_t", s, 3 + n, 0)) \
                                    .then_inc(full("gate_up", s, n, 2 * c + i), 1)

                    def down(s, n):
                        wait_free(pe, "down", s, n, 0)
                        for c in range(FC):
                            wait_read(pe, "gate_up", s, n, 2 * c + 1)
                            for t in range(NT):
                                last = pe.matmul(cols("down", s, n, 0, t * C, (t + 1) * C),
                                                 gh[s][:, c, t * P:(t + 1) * P], down_f[:, c, :],
                                                 start=(c == t == 0), stop=(c == FC - 1), skip_group_check=True)
                        last.then_inc(full("down", s, n, 0), 1)

                    def norm_t2(s, n):
                        transposes("norm_t2", s, n, 0, lambda t: xn[s][:, t, :], NT, lambda t: wait_tile(s, 5, t))
                        transposes("norm_t2", s, n, 1, lambda t: xh[s][:, t, :], NT, lambda t: wait_tile(s, 6, t))

                    def qkv1(s, n):
                        wait_read(pe, "norm_t2", s, 0, 1)
                        for i in range(NT // 2):
                            wait_free(pe, "qkv1", s, n, i)
                            for j in range(2):
                                t = 2 * i + j
                                last = pe.matmul(cols("qkv1", s, n, i, j * 2 * C, (j + 1) * 2 * C),
                                                 xhT[s][:, t * P:(t + 1) * P], W["qk1"][:, :], start=True, stop=True)
                            last.then_inc(full("qkv1", s, n, i), 1)
                        i = NT // 2
                        wait_free(pe, "qkv1", s, n, i)
                        for t in range(NT):
                            last = pe.matmul(cols("qkv1", s, n, i, t * 2 * HEADS, (t + 1) * 2 * HEADS),
                                             xhT[s][:, t * P:(t + 1) * P], w_gates[:, :], start=True, stop=True)
                        last.then_inc(full("qkv1", s, n, i), 1)

                    def split1(s, n):
                        wait_read(pe, "norm_t2", s, 0, 0)
                        wait_free(pe, "split1", s, n, 0)
                        for t in range(NT):
                            last = pe.matmul(cols("split1", s, n, 0, t * C, (t + 1) * C), xnT[s][:, t * P:(t + 1) * P],
                                             W["v1"][:, :], start=True, stop=True)
                        last.then_inc(full("split1", s, n, 0), 1)

                    def stack1_t(s, n):
                        for m, src in enumerate((qs, ks)):
                            for j in range(4):
                                transposes("stack1_t", s, n, 4 * m + j, lambda t: src[s][:, t, 4 * j:4 * j + 4, :]
                                           .rearrange("p h r -> p (h r)"), NT,
                                           lambda t: pe.wait_ge(q_stacked[s], t // 2 + 1) if m == j == 0 else None)

                    def resonance(s, n):
                        if n == 0:
                            for i in range(8):
                                wait_read(pe, "stack1_t", s, 0, i)
                            wait_read(pe, "split1", s, 0, 0)
                        for i in units_of_part(n, SKEW):
                            if i < UNITS:
                                b, m, r = i // 8, i // 4 % 2, i % 4
                                wait_free(pe, "resonance", s, n, 0)
                                rows = slice(r * PART, r * PART + USED)
                                for k in range(TS):
                                    for jj in range(2):
                                        o = cols("resonance", s, n, 0, k * PSF + jj * SEQ, k * PSF + (jj + 1) * SEQ)
                                        blk = 2 * m + jj
                                        last = pe.matmul(o, kT[s][rows, blk, b * SEQ + k * P:b * SEQ + (k + 1) * P],
                                                         qT[s][rows, blk, b * SEQ:(b + 1) * SEQ],
                                                         start=True, stop=True)
                                last.then_inc(full("resonance", s, n, 0), 1)
                            u = i - SKEW
                            if u < 0:
                                continue
                            b, m, r = u // 8, u // 4 % 2, u % 4
                            sums = ("resonance", s, u - r, 1)
                            if r == 0:
                                wait_free(pe, *sums)
                            wait_read(pe, "resonance", s, u, 0)
                            pr = probs[:, unit_no[("resonance", s, u)] % P_RING, :] \
                                .rearrange("p (k j q) -> p k j q", k=TS, j=2)
                            for jj in range(2):
                                o = cols(*sums, jj * SEQ, (jj + 1) * SEQ)
                                for k in range(TS):
                                    vv = v1[s][:, b * TS + k, (2 * m + jj) * PART:(2 * m + jj + 1) * PART]
                                    last = pe.matmul(o[r * PART:(r + 1) * PART, :], vv, pr[:, k, jj, :],
                                                     start=(k == 0), stop=(k == TS - 1))
                            last.then_inc(full(*sums) if r == 3 else probs_used, 1)

                    pe.wait_ge(weights_in, 16 * (len(w) - len(LATE)))
                    pe.wait_ge(consts_done, CONSTS)
                    pe.wait_ge(dequant_done, 6 + len(SPLIT))
                    todo = {"norm_t": norm_t, "router1": router1, "router2": router2, "logits": logits,
                            "logits_sum": logits_sum, "prefix": prefix, "dispatch": dispatch, "experts": experts,
                            "slots": slots,
                            "combine": combine, "qkv": qkv, "stack_t": stack_t, "row_max": row_max,
                            "window": window, "heads_t": heads_t, "project": project, "gate_up": gate_up,
                            "down": down, "norm_t2": norm_t2, "qkv1": qkv1, "split1": split1, "stack1_t": stack1_t,
                            "resonance": resonance, "context_t": context_t, "context1_t": context1_t,
                            "project1": lambda s, n: project(s, n, "project1", "wo1", 1)}
                    for step, s, n in STEPS:
                        if step in todo:
                            todo[step](s, n)

                @block.scalar
                def _(act):
                    def copy_out(step, s, n, i, dst, lo, hi):
                        wait_full(act, step, s, n, i)
                        act.activation(dst, cols(step, s, n, i, lo, hi), ACT.Copy).then_inc(read(step, s, n, i), 1)

                    def norm_t(s, n):
                        if n == 1:
                            copy_out("norm_t", s, n, 0, xnT[s][:, :], 0, TOK)
                        else:
                            wait_full(act, "norm_t", s, n, 0)
                            act.activation(xnT_high[s], cols("norm_t", s, n, 0, 0, TOK), ACT.Copy) \
                                .then_inc(xnT_rounded[s], 1)

                    def router1(s, n):
                        for c in [c for c in range(HC) if c != VECTOR_CHUNK]:
                            ps = cols("router1", s, n, c, 0, TOK)
                            wait_full(act, "router1", s, n, c)
                            act.activation(h1_full[s][:, c, :], ps, ACT.Relu, bias=W["rb1"][:, c:c + 1])
                            act.activation(h1[s][:, 0, c, :], ps, ACT.Relu, bias=W["rb1"][:, c:c + 1]) \
                                .then_inc(h1_high[s], 1)

                    def router2(s, n):
                        c = n % HC
                        if c % 2 == 0:
                            wait_full(act, "router2", s, n, 0)
                            act.activation(h2[s][:, c, :], cols("router2", s, n, 0, 0, TOK), ACT.Relu,
                                           bias=W["rb2"][:, c:c + 1]).then_inc(read("router2", s, n, 0), 1)

                    def choose(s, n):
                        act.wait_ge(logit_shifted[s], n + 1)
                        act.activation(small[s][:, 1, :, :], small[s][:, 0, :, :], ACT.Exp).then_inc(logit_exp[s], 1)

                    def dispatch(s, n):
                        for b in range(NB):
                            wait_full(act, "dispatch", s, n, b)
                            act.activation(slotT[:, :, s * NB + b, :],
                                           cols("dispatch", s, n, b, 0, SLOTS).rearrange("p (e c) -> p e c", e=E),
                                           ACT.Copy).then_inc(read("dispatch", s, n, b), 1)

                    def slots(s, n):
                        whole = SLOTS // P
                        m = CHUNKS[-1][1]
                        for b in range(NB):
                            wait_full(act, "slots", s, n, b)
                            act.activation(eo[s][:, b, 0:whole, :], cols("slots", s, n, b, 0, whole * P)
                                           .rearrange("p (i c) -> p i c", c=C), ACT.Copy)
                            act.activation(eo[s][0:m, b, whole, :],
                                           cols("slots", s, n, b, whole * P, (whole + 1) * P)[0:m, :],
                                           ACT.Copy).then_inc(read("slots", s, n, b), 1)

                    def high_parts(s, t, heads_q, heads_k):
                        nk = heads_k.shape[1]
                        act.activation(qs[s][:, t, :, 0:2 * HD].bitcast(F32R).rearrange("p h (c d) -> p h c d", c=2),
                                       heads_q[:, :, None, :].to_broadcast([P, HEADS, 2, HD]), ACT.Copy)
                        for c in (0, 2):
                            last = act.activation(ks[s][:, t, 0:nk, c * HD:(c + 1) * HD].bitcast(F32R), heads_k,
                                                  ACT.Copy)
                        last.then_inc(q_high[s], 1)

                    def qkv(s, n):
                        for i in range(NT // 2):
                            wait_full(act, "qkv", s, n, i)
                            for j in range(2):
                                ps = cols("qkv", s, n, i, j * 192, (j + 1) * 192)
                                heads = ps.rearrange("p (h d) -> p h d", d=HD)
                                act.activation(v0[s][:, 2 * i + j, 0:KV, 0:HD], heads[:, HEADS + KV:, :], ACT.Copy)
                                high_parts(s, 2 * i + j, heads[:, 0:HEADS, :], heads[:, HEADS:HEADS + KV, :])

                    def attend(step, s, n, func, scale, bias):
                        for i in units_of_part(n, SKEW + 1):
                            if i < UNITS:
                                unit = unit_no[(step, s, n)]
                                wait_full(act, step, s, n, 0)
                                if unit >= P_RING:
                                    wait_probs_used(act, unit - P_RING)
                                act.activation(probs[:, unit % P_RING, :], cols(step, s, n, 0, 0, 2 * PSF), func,
                                               scale=scale, bias=bias).then_inc(read(step, s, n, 0), 1)
                            u = i - SKEW - 1
                            if u % 4 == 3 and u > 0 and not sums_by_vector(step, s):
                                copy_out(step, s, u - 3, 1, ctxT[s][:, u // 4, :], 0, PSF)

                    def context1_t(s, n):
                        copy_out("context1_t", s, n, CTX, vsum[s][:, :, :].rearrange("p b c -> p (b c)"), 0, NB * C)

                    def gate_up(s, n):
                        for c in range(FC):
                            wait_full(act, "gate_up", s, n, 2 * c)
                            if c:
                                wait_read(act, "gate_up", s, n, 2 * c - 2)
                            act.activation(gt[s], cols("gate_up", s, n, 2 * c, 0, TOK), ACT.Tanh, scale=0.5) \
                                .then_inc(tanh_gate[s], 1)

                    def qkv1(s, n):
                        for i in range(NT // 2):
                            wait_full(act, "qkv1", s, n, i)
                            src = cols("qkv1", s, n, i, 0, PSF).rearrange("p (t n) -> p t n", t=2)
                            act.activation(qk2[s][:, 2 * i:2 * i + 2, :], src, ACT.Square)
                            act.activation(qk[s][:, 2 * i:2 * i + 2, :], src, ACT.Copy) \
                                .then_inc(read("qkv1", s, n, i), 1)

                    def unit(s, n):
                        for t in range(NT):
                            act.wait_ge(unit_qk[s], t // 2 + 1)
                            u = qk[s][:, t, :].rearrange("p (m h d) -> p m h d", m=2, d=HD)
                            high_parts(s, t, u[:, 0, :, :], u[:, 1, :, :])

                    def split1(s, n):
                        wait_read(act, "qkv1", s, n, NT // 2)
                        act.activation(gates[s][:, :, :], ss[s][:, :, :], ACT.Tanh, scale=0.5).then_inc(gate_tanh[s], 1)

                    def stack_t(s, n):
                        for j in range(0, 4, 2):
                            copy_out("stack_t", s, n, j, qT[s][:, j, :], 0, TOK)

                    def stack1_t(s, n):
                        for i in range(0, 8, 2):
                            copy_out("stack1_t", s, n, i, (qT if i < 4 else kT)[s][:, i % 4, :], 0, TOK)

                    todo = {
                        "norm_t": norm_t,
                        "norm_t2": lambda s, n: copy_out("norm_t2", s, n, 0, xnT[s][:, :], 0, TOK),
                        "heads_t": lambda s, n: copy_out("heads_t", s, n, 0, xhT[s], 0, TOK),
                        "logits": lambda s, n: copy_out("logits", s, n, 0, logit_parts[s], 0, TOK),
                        "choose": choose, "dispatch": dispatch, "context1_t": context1_t, "slots": slots,
                        "qkv": qkv, "stack_t": stack_t,
                        "gate_up": gate_up, "qkv1": qkv1, "unit": unit, "split1": split1, "stack1_t": stack1_t,
                        "router1": router1,
                        "router2": router2,
                        "window": lambda s, n: attend("window", s, n, ACT.Exp, HD ** -0.5, 0.0),
                        "resonance": lambda s, n: attend("resonance", s, n, ACT.Tanh, SHARP, tanh_bias[:, 0:1]),
                    }
                    act.wait_ge(weights_in, 16 * (len(w) - len(LATE)))
                    act.wait_ge(consts_done, CONSTS)
                    act.activation(warm_up[:, :], tanh_bias[:, :], ACT.Tanh)
                    for step, s, n in STEPS:
                        if step in todo:
                            todo[step](s, n)

                @block.gpsimd
                def _(pool):
                    def power(s, k):
                        pool.wait_ge(var_ready[s], k)
                        pool.tensor_tensor(rstd[s][:, :], var_eps[s][:, :], minus_half[:, 0:NT], ALU.pow) \
                            .then_inc(rstd_ready[s], 1)

                    def dispatch(s, n):
                        if s == n == 0:
                            for one in range(STREAMS):
                                pool.wait_ge(x_out_done[one], 16)
                            pool.sem_clear(range(x_out_done[0].num, x_out_done[-1].num + 1))
                        pool.wait_ge(place_ready[s], n + 1)
                        pool.tensor_tensor(share[s].rearrange("p t (e c) -> p (t e) c", e=E),
                                           place[s].rearrange("p t (e c) -> p (t e) c", e=E),
                                           small[s][:, 6, :, :].rearrange("p t e -> p (t e)")[:, :, None]
                                           .to_broadcast([P, NT * E, CAP]), ALU.mult).then_inc(share_ready[s], 1)

                    def experts(s, n):
                        for e in range(E):
                            wait_read(pool, "experts", s, n, E // EG + e)
                            pool.tensor_scalar(hh[:, e, :, :], hraw[:, e % 2, :, :], 0.0, None, ALU.max) \
                                .then_inc(hh_ready, 1)

                    def qkv(s, n):
                        pool.wait_ge(xn_ready[s], 2 * NT)
                        pool.memset(qs[s][:, :, :, USED:PART], 0.0).then_inc(pads_set[s], 1)
                        pool.memset(ks[s][:, :, 0:KV, USED:USED + 1], 1.0).then_inc(pads_set[s], 1)
                        pool.memset(ks[s][:, :, 0:KV, USED + 1:PART], 0.0).then_inc(pads_set[s], 1)
                        pool.memset(kT[s][:, :, :].bitcast(F32), 0.0).then_inc(k_zero[s], 1)

                    todo = {
                        "norm": lambda s, n: power(s, [1, 2, 3, 4, 5, 7][n]), "renorm": lambda s, n: power(s, 6),
                        "dispatch": dispatch, "experts": experts, "qkv": qkv,
                    }
                    for step, s, n in STEPS:
                        if step in todo:
                            todo[step](s, n)

                @block.vector
                def _(dve):
                    linked = [0]

                    def link(ins):
                        linked[0] += 1
                        ins.then_inc(dve_link, 1)

                    def settle():
                        dve.wait_ge(dve_link, linked[0])

                    def variances(s, src):
                        for t in range(NT):
                            link(dve.bn_stats(stats[s][:, t, :], src[s][:, t, :]))
                        settle()
                        for t in range(NT):
                            link(dve.bn_aggr(mean_var[s][:, t, :], stats[s][:, t, :]))
                        settle()
                        dve.tensor_scalar(var_eps[s][:, :], mean_var[s][:, :, 1], LN_EPS, None, ALU.add) \
                            .then_inc(var_ready[s], 1)

                    def stats_of_x(s, n):
                        if n:
                            step, k = [None, ("combine", 0), ("project", 0), ("combine", 1), ("down", 0),
                                       ("project1", 0)][n]
                            wait_read(dve, step, s, k, 0)
                        variances(s, x if n else x_start)

                    def normalise(s, src, dst, k):
                        dve.wait_ge(rstd_ready[s], k)
                        for t in range(NT):
                            dve.tensor_scalar(dst[s][:, t, :], src[s][:, t, :], mean_var[s][:, t, 0:1],
                                              rstd[s][:, t:t + 1], ALU.subtract, ALU.mult).then_inc(xn_ready[s], 1)

                    def norm(s, n):
                        normalise(s, x if n else x_start, xn, [1, 2, 3, 4, 5, 7][n])

                    def restats(s, n):
                        dve.wait_ge(xn_ready[s], 5 * NT)
                        variances(s, xn)

                    def renorm(s, n):
                        normalise(s, xn, xh, 6)
                        dve.tensor_tensor(x[s][:, :, :], x[s][:, :, :],
                                          W["bo1"][:, None, :].to_broadcast([P, NT, C]), ALU.add)

                    def norm_t(s, n):
                        if n != 1:
                            dve.wait_ge(xnT_rounded[s], n if n > 1 else 1)
                            dve.tensor_tensor(xnT_low[s], cols("norm_t", s, n, 0, 0, TOK), xnT_high[s].bitcast(F32),
                                              ALU.subtract).then_inc(read("norm_t", s, n, 0), 1)

                    def router1(s, n):
                        for c in range(HC):
                            high, low = (h1[s][:, i, c, :] for i in range(2))
                            if c == VECTOR_CHUNK:
                                wait_full(dve, "router1", s, n, c)
                                for dst in (h1_full[s][:, c, :], high):
                                    link(dve.tensor_scalar(dst, cols("router1", s, n, c, 0, TOK),
                                                           W["rb1"][:, c:c + 1], 0.0, ALU.add, ALU.max))
                                settle()
                            else:
                                dve.wait_ge(h1_high[s], (HC - 1) * n + c + (c < VECTOR_CHUNK))
                            dve.tensor_tensor(low, h1_full[s][:, c, :], high.bitcast(F32), ALU.subtract) \
                                .then_inc(read("router1", s, n, c), 1)

                    def router2(s, n):
                        c = n % HC
                        if c % 2 == 1:
                            wait_full(dve, "router2", s, n, 0)
                            dve.tensor_scalar(h2[s][:, c, :], cols("router2", s, n, 0, 0, TOK), W["rb2"][:, c:c + 1],
                                              0.0, ALU.add, ALU.max).then_inc(read("router2", s, n, 0), 1)

                    def row(s, i):
                        return small[s][:, i, :, :]

                    def over_experts(ap):
                        return ap.to_broadcast([P, NT, E])

                    def logits_sum(s, n):
                        wait_full(dve, "logits_sum", s, n, 0)
                        ps = cols("logits_sum", s, n, 0, 0, NT * E).rearrange("p (t e) -> p t e", e=E)
                        dve.tensor_tensor(row(s, 7), ps, W["rb3"][:, None, :].to_broadcast([P, NT, E]), ALU.add) \
                            .then_inc(read("logits_sum", s, n, 0), 1)
                        wait_read(dve, "logits_sum", s, n, 0)
                        link(dve.tensor_reduce(row(s, 3)[:, :, 0:1], row(s, 7), AX.X, ALU.max))
                        settle()
                        dve.tensor_tensor(row(s, 0), row(s, 7), over_experts(row(s, 3)[:, :, 0:1]), ALU.subtract) \
                            .then_inc(logit_shifted[s], 1)

                    def choose(s, n):
                        dve.wait_ge(logit_exp[s], n + 1)
                        for t in range(NT):
                            link(dve.max(top[s][:, t, :], small[s][:, 1, t, :]))
                        settle()
                        for t in range(NT):
                            link(dve.max_index(top_at[s][:, t, :], top[s][:, t, :], small[s][:, 1, t, :]))
                        settle()
                        numbers = expert_no[:, None, :].to_broadcast([P, NT, E])
                        for k in range(2):
                            link(dve.tensor_tensor(row(s, 4 + k), numbers, over_experts(top_at[s][:, :, k:k + 1]),
                                                   ALU.is_equal))
                        settle()
                        dve.tensor_tensor(chosen[s][:, :, :], row(s, 4), row(s, 5), ALU.add) \
                            .then_inc(chosen_ready[s], 1)
                        link(dve.tensor_reduce(row(s, 3)[:, :, 1:2], row(s, 1), AX.X, ALU.add))
                        settle()
                        link(dve.reciprocal(row(s, 3)[:, :, 2:3], row(s, 3)[:, :, 1:2]))
                        settle()
                        link(dve.tensor_tensor(row(s, 2), row(s, 1), over_experts(row(s, 3)[:, :, 2:3]), ALU.mult))
                        settle()
                        dve.wait_ge(chosen_ready[s], n + 1)
                        link(dve.tensor_tensor(row(s, 6), row(s, 2), chosen[s][:, :, :], ALU.mult))

                    def prefix(s, n):
                        wait_full(dve, "prefix", s, n, 0)
                        ps = cols("prefix", s, n, 0, 0, NT * E).rearrange("p (t e) -> p t e", e=E)
                        dve.scalar_tensor_tensor(out=row(s, 5), in0=ps, scalar=1.0, in1=chosen[s][:, :, :],
                                                 op0=ALU.add, op1=ALU.mult).then_inc(read("prefix", s, n, 0), 1)
                        wait_read(dve, "prefix", s, n, 0)
                        dve.tensor_tensor(place[s].rearrange("p t (e c) -> p (t e) c", e=E),
                                          slot_no[:, None, :].to_broadcast([P, NT * E, CAP]),
                                          row(s, 5).rearrange("p t e -> p (t e)")[:, :, None]
                                          .to_broadcast([P, NT * E, CAP]), ALU.is_equal).then_inc(place_ready[s], 1)

                    def dispatch(s, n):
                        for i, (c, m) in enumerate(CHUNKS):
                            wait_full(dve, "dispatch", s, n, NB + i)
                            dve.tensor_copy(shareT[s][0:m, i, :], cols("dispatch", s, n, NB + i, 0, TOK)[0:m, :]) \
                                .then_inc(read("dispatch", s, n, NB + i), 1)

                    def experts(s, n):
                        for i in range(E + SKEW + 1):
                            if i < E:
                                u = E // EG + i
                                wait_full(dve, "experts", s, n, u)
                                if E * n + i >= 2:
                                    dve.wait_ge(hh_ready, E * n + i - 1)
                                ps = cols("experts", s, n, u, 0, 2 * PSF).rearrange("p (a n) -> p a n", a=2)
                                dve.tensor_tensor(hraw[:, i % 2, :, :].rearrange("p (a c) n -> p a c n", a=2),
                                                  ps[:, :, 0:2 * SLOT4].rearrange("p a (c n) -> p a c n", c=2),
                                                  W["eb1"][:, i, :].rearrange("p (a c) -> p a c", a=2)[:, :, :, None]
                                                  .to_broadcast([P, 2, 2, SLOT4]), ALU.add) \
                                    .then_inc(read("experts", s, n, u), 1)
                            e = i - SKEW - 1
                            if e < 0 or e % EG != EG - 1:
                                continue
                            g = e // EG
                            wait_full(dve, "experts", s, n, g)
                            dve.tensor_tensor(eoT[:, :, g * EG:(g + 1) * EG, :].rearrange("p b e c -> p e b c"),
                                              cols("experts", s, n, g, 0, EG * SLOT4)
                                              .rearrange("p (e b c) -> p e b c", e=EG, b=NSB),
                                              W["eb2"][:, g * EG:(g + 1) * EG, None, None]
                                              .to_broadcast([P, EG, NSB, CAP]), ALU.add) \
                                .then_inc(read("experts", s, n, g), 1)

                    def add_to_x(step, s, n, factor):
                        wait_full(dve, step, s, n, 0)
                        before = x_start[s] if (step, n) == ("combine", 0) else x[s]
                        dve.scalar_tensor_tensor(out=x[s][:, :, :].rearrange("p t c -> p (t c)"),
                                                 in0=cols(step, s, n, 0, 0, NT * C), scalar=factor,
                                                 in1=before[:, :, :].rearrange("p t c -> p (t c)"),
                                                 op0=ALU.mult, op1=ALU.add).then_inc(read(step, s, n, 0), 1)

                    def qkv(s, n):
                        for i in range(NT // 2):
                            wait_full(dve, "qkv", s, n, i)
                            dve.wait_ge(q_high[s], 2 * i + 2)
                            for j in range(2):
                                t = 2 * i + j
                                heads = cols("qkv", s, n, i, j * 192, (j + 1) * 192) \
                                    .rearrange("p (h d) -> p h d", d=HD)
                                dve.tensor_tensor(qs[s][:, t, :, 2 * HD:3 * HD], heads[:, 0:HEADS, :],
                                                  qs[s][:, t, :, 0:HD], ALU.subtract)
                                last = dve.tensor_tensor(ks[s][:, t, 0:KV, HD:2 * HD], heads[:, HEADS:HEADS + KV, :],
                                                         ks[s][:, t, 0:KV, 0:HD], ALU.subtract)
                            last.then_inc(read("qkv", s, n, i), 1)

                    def copy_out(step, s, n, i, dst):
                        wait_full(dve, step, s, n, i)
                        dve.tensor_copy(dst, cols(step, s, n, i, 0, PSF)).then_inc(read(step, s, n, i), 1)

                    def stack_t(s, n):
                        for j in range(1, 4, 2):
                            copy_out("stack_t", s, n, j, qT[s][:, j, :])
                        if n == 0:
                            dve.wait_ge(k_zero[s], 1)
                            wait_full(dve, "stack_t", s, n, 4)
                            for g in range(KV):
                                rows = slice(g * PART, (g + 1) * PART)
                                last = dve.tensor_copy(kT[s][rows, g, :], cols("stack_t", s, n, 4, 0, TOK)[rows, :])
                            last.then_inc(read("stack_t", s, n, 4), 1)

                    def stack1_t(s, n):
                        for i in range(1, 8, 2):
                            copy_out("stack1_t", s, n, i, (qT if i < 4 else kT)[s][:, i % 4, :])

                    def row_max(s, n):
                        t, m = n // 4, n % 4
                        wait_full(dve, "row_max", s, n, 0)
                        dve.tensor_reduce(qs[s][:, t, 4 * m:4 * m + 4, USED:USED + 1],
                                          cols("row_max", s, n, 0, 0, 2 * PSF).rearrange("p (g k) -> p g k", g=KV),
                                          AX.X, ALU.max, negate=True).then_inc(read("row_max", s, n, 0), 1)

                    def sums(step, s, n):
                        for i in units_of_part(n, SKEW + 1):
                            u = i - SKEW - 1
                            if u % 4 == 3 and u > 0 and sums_by_vector(step, s):
                                copy_out(step, s, u - 3, 1, ctxT[s][:, u // 4, :])

                    def context_t(s, n):
                        for i in range(CTX):
                            b, jp = i // 2, i % 2
                            wait_full(dve, "context_t", s, n, i)
                            ps = cols("context_t", s, n, i, 0, PSF).rearrange("p (a g r) -> p a g r", a=4, g=KV)
                            den = rden[s][:, i, :, :]
                            link(dve.reciprocal(den[:, :, :, None], ps[:, :, :, HD:HD + 1]))
                            settle()
                            for q in range(TS):
                                o = xh[s][:, b * TS + q, :].rearrange("p (g j d) -> p j g d", g=KV, j=GQ)
                                last = dve.tensor_tensor(o[:, 2 * jp:2 * jp + 2, :, :],
                                                         ps[:, q::TS, :, 0:HD],
                                                         den[:, q::TS, :, None].to_broadcast([P, 2, KV, HD]), ALU.mult)
                            last.then_inc(read("context_t", s, n, i), 1)

                    def context1_t(s, n):
                        wait_read(dve, "context1_t", s, n, CTX)
                        for i in range(CTX):
                            b, m = i // 2, i % 2
                            wait_full(dve, "context1_t", s, n, i)
                            ps = cols("context1_t", s, n, i, 0, PSF)
                            for q in range(TS):
                                t = b * TS + q
                                for jj in range(2):
                                    blk = 2 * m + jj
                                    at = (jj * TS + q) * P
                                    src = ps[:, at:at + P].rearrange("p (r n) -> p r n", r=4)
                                    o = xh[s][:, t, blk * PART:(blk + 1) * PART].rearrange("p (r d) -> p r d", d=HD)
                                    vs = vsum[s][:, b, blk * PART:(blk + 1) * PART].rearrange("p (r d) -> p r d", d=HD)
                                    diag = bass.AP(src.tensor, src.offset, [list(src.ap[0]), [PART + HD, 4], [1, HD]])
                                    last = dve.tensor_tensor(o, diag, vs, ALU.add)
                            last.then_inc(read("context1_t", s, n, i), 1)
                        wait_read(dve, "context1_t", s, n, CTX - 1)
                        heads = xh[s][:, :, :].rearrange("p t (h d) -> p t h d", d=HD)
                        dve.tensor_tensor(heads, heads, gates[s][:, :, 0:HEADS, None]
                                          .to_broadcast([P, NT, HEADS, HD]), ALU.mult).then_inc(gated_heads[s], 1)

                    def gate_up(s, n):
                        for c in range(FC):
                            wait_full(dve, "gate_up", s, n, 2 * c)
                            dve.wait_ge(tanh_gate[s], FC * n + c + 1)
                            dve.scalar_tensor_tensor(out=gg[s][:, c, :], in0=gt[s], scalar=1.0,
                                                     in1=cols("gate_up", s, n, 2 * c, 0, TOK),
                                                     op0=ALU.add, op1=ALU.mult) \
                                .then_inc(read("gate_up", s, n, 2 * c), 1)
                            wait_read(dve, "gate_up", s, n, 2 * c)
                            wait_full(dve, "gate_up", s, n, 2 * c + 1)
                            dve.tensor_tensor(gh[s][:, c, :], gg[s][:, c, :], cols("gate_up", s, n, 2 * c + 1, 0, TOK),
                                              ALU.mult).then_inc(read("gate_up", s, n, 2 * c + 1), 1)

                    def norm_t2(s, n):
                        wait_full(dve, "norm_t2", s, n, 1)
                        dve.tensor_scalar(xhT[s], cols("norm_t2", s, n, 1, 0, TOK), W["gamma"][:, 0:1],
                                          W["beta"][:, 0:1], ALU.mult, ALU.add).then_inc(read("norm_t2", s, n, 1), 1)

                    def heads_of(ap):
                        return ap.rearrange("p t (h d) -> p (t h) d", d=HD)

                    def per_head(ap):
                        return ap.rearrange("p t h -> p (t h)")[:, :, None]

                    def qkv1(s, n):
                        for i in range(NT // 2):
                            wait_read(dve, "qkv1", s, n, i)
                            link(dve.tensor_reduce(per_head(ss[s][:, 2 * i:2 * i + 2, :]),
                                                   heads_of(qk2[s][:, 2 * i:2 * i + 2, :]), AX.X, ALU.add))
                        settle()
                        v, y, z = (a[s][:, :, :].rearrange("p t h -> p (t h)") for a in (ss, inv, newton))
                        link(dve.tensor_scalar(v, v, NORM_FLOOR, None, ALU.max))
                        settle()
                        link(dve.tensor_scalar(y.bitcast(I32), v.bitcast(I32), -0.5, GUESS, ALU.mult, ALU.add))
                        settle()
                        for _ in range(3):
                            link(dve.scalar_tensor_tensor(out=z, in0=y, scalar=-0.5, in1=y, op0=ALU.mult, op1=ALU.mult))
                            settle()
                            link(dve.tensor_tensor(z, z, v, ALU.mult))
                            settle()
                            link(dve.scalar_tensor_tensor(out=y, in0=z, scalar=1.5, in1=y, op0=ALU.add, op1=ALU.mult))
                            settle()
                        wait_full(dve, "qkv1", s, n, NT // 2)
                        dve.tensor_tensor(ss[s][:, :, :], cols("qkv1", s, n, NT // 2, 0, NT * 2 * HEADS)
                                          .rearrange("p (t h) -> p t h", t=NT), inv[s][:, :, :], ALU.mult) \
                            .then_inc(read("qkv1", s, n, NT // 2), 1)

                    def unit(s, n):
                        for i in range(NT // 2):
                            a = qk[s][:, 2 * i:2 * i + 2, :].rearrange("p t (h d) -> p (t h) d", d=HD)
                            length = inv[s][:, 2 * i:2 * i + 2, :].rearrange("p t h -> p (t h)")
                            dve.tensor_tensor(a, a, length[:, :, None].to_broadcast([P, 2 * 2 * HEADS, HD]), ALU.mult) \
                                .then_inc(unit_qk[s], 1)

                    def split1(s, n):
                        for i in range(NT // 2):
                            dve.wait_ge(q_high[s], NT + 2 * i + 2)
                            tiles = slice(2 * i, 2 * i + 2)
                            u = qk[s][:, tiles, :].rearrange("p t (m h d) -> p t m h d", m=2, d=HD)
                            dve.tensor_tensor(qs[s][:, tiles, :, 2 * HD:3 * HD], u[:, :, 0, :, :],
                                              qs[s][:, tiles, :, 0:HD], ALU.subtract)
                            dve.tensor_tensor(ks[s][:, tiles, :, HD:2 * HD], u[:, :, 1, :, :],
                                              ks[s][:, tiles, :, 0:HD], ALU.subtract).then_inc(q_stacked[s], 1)
                        dve.wait_ge(gate_tanh[s], 1)
                        link(dve.tensor_scalar(gates[s][:, :, 0:HEADS], gates[s][:, :, 0:HEADS], 0.1875, 0.3125,
                                               ALU.mult, ALU.add))
                        link(dve.tensor_scalar(gates[s][:, :, HEADS:], gates[s][:, :, HEADS:], 0.375, 0.625,
                                               ALU.mult, ALU.add))
                        settle()
                        wait_full(dve, "split1", s, n, 0)
                        dve.tensor_tensor(v1[s].rearrange("p t (h d) -> p t h d", d=HD),
                                          cols("split1", s, n, 0, 0, NT * C)
                                          .rearrange("p (t h d) -> p t h d", t=NT, d=HD),
                                          gates[s][:, :, HEADS:, None].to_broadcast([P, NT, HEADS, HD]), ALU.mult) \
                            .then_inc(read("split1", s, n, 0), 1)

                    todo = {
                        "stats": stats_of_x, "norm": norm, "norm_t": norm_t, "restats": restats, "renorm": renorm,
                        "router1": router1,
                        "router2": router2,
                        "logits_sum": logits_sum, "choose": choose, "prefix": prefix, "dispatch": dispatch,
                        "experts": experts, "combine": lambda s, n: add_to_x("combine", s, n, 0.5),
                        "qkv": qkv, "stack_t": stack_t, "row_max": row_max, "context_t": context_t,
                        "window": lambda s, n: sums("window", s, n),
                        "resonance": lambda s, n: sums("resonance", s, n),
                        "project": lambda s, n: add_to_x("project", s, n, 1.0), "gate_up": gate_up,
                        "down": lambda s, n: add_to_x("down", s, n, 0.25),
                        "norm_t2": norm_t2, "qkv1": qkv1, "unit": unit, "split1": split1, "stack1_t": stack1_t,
                        "context1_t": context1_t, "project1": lambda s, n: add_to_x("project1", s, n, 1.0),
                    }
                    dve.wait_ge(weights_in, 16 * (len(w) - len(LATE)))
                    dve.wait_ge(consts_done, CONSTS)
                    for step, s, n in STEPS:
                        if step in todo:
                            todo[step](s, n)

            numbers = sorted(one.num for one in round_sems)
            assert numbers == list(range(numbers[0], numbers[-1] + 1))
            nc.gpsimd.sem_clear(range(numbers[0], numbers[-1] + 1))
            nc.all_engine_barrier()

        with nc.Block() as block:
            @block.sync
            def _(sp):
                for s in range(STREAMS):
                    sp.wait_ge(x_out_done[s], 16)


def lay_out(inputs):
    import numpy as np

    g = {k: np.asarray(v) for k, v in inputs.items()}

    def rows(a, shape):
        return np.broadcast_to(a, shape)

    def chunks(a):
        return a.reshape(-1, P, a.shape[-1]).transpose(1, 0, 2)

    wq = g["L0_attn_Wq"].reshape(KV, GQ, HD, C).transpose(1, 0, 2, 3).reshape(HEADS * HD, C)
    out = {
        "rW1": g["L0_ffn_rW1"],
        "rb1": g["L0_ffn_rb1"].reshape(HC, P).T,
        "rb2": g["L0_ffn_rb2"].reshape(HC, P).T,
        "rW2": chunks(g["L0_ffn_rW2"]),
        "rW3": chunks(g["L0_ffn_rW3"]),
        "rb3": rows(g["L0_ffn_rb3"], (P, E)),
        "eb1": g["L0_ffn_eb1"].reshape(E, HC, P).transpose(2, 0, 1),
        "eb2": g["L0_ffn_eb2"].T,
        "w_gate": g["L1_ffn_w_gate"].T,
        "w_up": g["L1_ffn_w_up"].T,
        "w_down": chunks(g["L1_ffn_w_down"].T),
        "qkv0": np.concatenate([wq, g["L0_attn_Wk"], g["L0_attn_Wv"]]).T,
        "wo0": g["L0_attn_Wo"].T,
        "qk1": np.concatenate([g["L1_attn_w_q"], g["L1_attn_w_k"]], 1),
        "v1": g["L1_attn_w_v"],
        "wo1": g["L1_attn_w_o"],
        "bo1": rows(g["L1_attn_b_o"], (P, C)),
        "gamma": g["L1_attn_gamma"].reshape(C, 1),
        "beta": g["L1_attn_beta"].reshape(C, 1),
        "g_qk": rows(np.concatenate([np.tile(g["L1_attn_g_q"], HEADS), np.tile(g["L1_attn_g_k"], HEADS)]),
                     (P, 2 * C)),
        "eW1": g["L0_ffn_eW1"].transpose(1, 0, 2),
        "eW2": g["L0_ffn_eW2"].reshape(E, HC, P, C).transpose(2, 0, 1, 3),
    }
    return {k: np.ascontiguousarray(v) for k, v in out.items()}


def kernel(**inputs):
    import numpy as np
    from concourse import bacc
    from concourse.bass_utils import run_bass_kernel_spmd

    x = np.ascontiguousarray(np.asarray(inputs["L0_attn_x"]))
    arrays = {"x": x, **{f"w_{k}": v for k, v in lay_out(inputs).items()}}
    nc = bacc.Bacc("TRN2", target_bir_lowering=False, num_devices=1)
    dram = {k: nc.dram_tensor(f"{k}_dram", v.shape, mybir.dt.from_np(v.dtype), kind="ExternalInput").ap()
            for k, v in arrays.items()}
    out = nc.dram_tensor("out_dram", x.shape, F32, kind="ExternalOutput").ap()
    macaron_kernel(nc, dram["x"], {k[2:]: ap for k, ap in dram.items() if k != "x"}, out)
    r = run_bass_kernel_spmd(nc, [{f"{k}_dram": v for k, v in arrays.items()}], core_ids=[0])
    return r.results[0]["out_dram"]
```
